# Optimizing a Trainium2 kernel written in Bass

```python
import numpy as np
import jax
import jax.numpy as jnp

def _softmax(x, axis=-1):
    return jax.nn.softmax(x, axis=axis)

def _gelu(x):
    return jax.nn.gelu(x, approximate=True)

def _silu(x):
    return jax.nn.silu(x)

def _sigmoid(x):
    return jax.nn.sigmoid(x)

def _layernorm(x, axis=-1, eps=1e-05):
    m = jnp.mean(x, axis=axis, keepdims=True)
    v = jnp.var(x, axis=axis, keepdims=True)
    return (x - m) / jnp.sqrt(v + eps)

def _scatter_add(tgt, idx, src, axis=0):
    return tgt.at[idx].add(src)

def _segment_sum(src, seg, n):
    return jax.ops.segment_sum(src, seg, n)
kernel_name = 'mk_decoder_preln_d1_seqx_r2_046ddf'

def setup_inputs(seed: int=0):
    np.random.seed(seed)
    _w = jnp.asarray

    def _rec_inputs():
        import jax
        import jax.numpy as jnp
        _rk = jax.random.key(seed)
        x = 7.22e-05 + 1 * jax.random.normal(jax.random.fold_in(_rk, 1), (2, 2048, 512), jnp.float32)
        _lenS = 2048 - jax.random.randint(jax.random.fold_in(_rk, 7), (2,), 0, max(1, 2048 // 4) + 1, jnp.int32)
        _lenS2 = 77 - jax.random.randint(jax.random.fold_in(_rk, 8), (2,), 0, max(1, 77 // 4) + 1, jnp.int32)
        _ctx_1024P = jax.random.normal(jax.random.fold_in(_rk, 11), (2, 16, 512), jnp.float32)
        _ctx_1024c = jax.random.dirichlet(jax.random.fold_in(_rk, 511), 0.3 * jnp.ones((16,), jnp.float32), (2, 77))
        _ctx_1024t = jnp.einsum('bsk,bkd->bsd', _ctx_1024c, _ctx_1024P)
        _ctx_1024t = _ctx_1024t * jax.lax.rsqrt(jnp.mean(jnp.square(_ctx_1024t)) + 1e-12) * 0.953939
        ctx_1024 = 4.13588e-05 + 0.999923 * (_ctx_1024t + 0.3 * jax.random.normal(jax.random.fold_in(_rk, 611), (2, 77, 512), jnp.float32))
        return (x, ctx_1024)
    x, ctx_1024 = _rec_inputs()

    def _L0_attn_setup():
        import jax, jax.numpy as jnp
        import numpy as np
        B, S, D = (4, 4096, 512)
        N = 4
        K = D // N
        Z_BIAS_MIN, Z_BIAS_MAX = (-2.0, 2.0)

        def _binop(q_i, q_j):
            a_i, b_i = q_i
            a_j, b_j = q_j
            return (a_i * a_j, a_j * b_i + b_j)
        key = jax.random.key(seed)
        k0, k1, k2, k3 = jax.random.split(key, 4)
        scale = 1.0 / np.sqrt(D)
        x = jax.random.normal(k0, (B, S, D), jnp.float32)
        Wz = jax.random.normal(k1, (N, D, K), jnp.float32) * scale
        z_biases = jnp.asarray(np.linspace(Z_BIAS_MIN, Z_BIAS_MAX, N).astype(np.float32))
        bz = jnp.broadcast_to(z_biases[:, None], (N, K))
        Wh = jax.random.normal(k2, (N, D, K), jnp.float32) * scale
        bh = jnp.zeros((N, K), jnp.float32)
        Wg = jax.random.normal(k3, (D, D), jnp.float32) * scale
        bg = jnp.zeros((D,), jnp.float32)
        return {'x': x, 'Wz': Wz, 'bz': bz, 'Wh': Wh, 'bh': bh, 'Wg': Wg, 'bg': bg}
    _L0_attn_all = _L0_attn_setup()
    _L0_attn_in = {k: v for k, v in _L0_attn_all.items() if k in ('Wz', 'bz', 'Wh', 'bh', 'Wg', 'bg')}
    del _L0_attn_all

    def _L0_xattn_setup():
        import jax, jax.numpy as jnp
        import numpy as np
        D_MODEL = 512
        HEADS = 16
        D_HEAD = D_MODEL // HEADS
        CAUSAL = True

        def _split(x):
            B, L, _ = x.shape
            return x.reshape(B, L, HEADS, D_HEAD).transpose(0, 2, 1, 3)
        key = jax.random.key(seed)
        ks = jax.random.split(key, 11)
        B, L = (4, 1024)
        s = 1.0 / np.sqrt(D_MODEL)
        inp = {'q': jax.random.normal(ks[0], (B, L, D_MODEL), jnp.float32), 'k': jax.random.normal(ks[1], (B, L, D_MODEL), jnp.float32), 'v': jax.random.normal(ks[2], (B, L, D_MODEL), jnp.float32), 'Wq': jax.random.normal(ks[3], (D_MODEL, D_MODEL), jnp.float32) * s, 'bq': jnp.zeros((D_MODEL,), jnp.float32), 'Wk': jax.random.normal(ks[4], (D_MODEL, D_MODEL), jnp.float32) * s, 'bk': jnp.zeros((D_MODEL,), jnp.float32), 'Wv': jax.random.normal(ks[5], (D_MODEL, D_MODEL), jnp.float32) * s, 'bv': jnp.zeros((D_MODEL,), jnp.float32), 'Wo': jax.random.normal(ks[6], (D_MODEL, D_MODEL), jnp.float32) * s, 'bo': jnp.zeros((D_MODEL,), jnp.float32)}
        return inp
    _L0_xattn_all = _L0_xattn_setup()
    _L0_xattn_in = {k: v for k, v in _L0_xattn_all.items() if k in ('Wq', 'bq', 'Wk', 'bk', 'Wv', 'bv', 'Wo', 'bo')}
    del _L0_xattn_all

    def _L0_ffn_setup():
        import jax, jax.numpy as jnp
        import numpy as np
        LN_EPS = 1e-05

        def _layernorm(x, g, b):
            m = jnp.mean(x, axis=-1, keepdims=True)
            v = jnp.mean(jnp.square(x - m), axis=-1, keepdims=True)
            return (x - m) * jax.lax.rsqrt(v + LN_EPS) * g + b
        K_TOP = 2
        key = jax.random.key(seed)
        ks = jax.random.split(key, 4)
        B, N, D, E = (8, 1024, 512, 4)
        s = 0.02
        return {'x': jax.random.normal(ks[0], (B, N, D), dtype=jnp.float32), 'gate_W': jax.random.normal(ks[1], (D, E), dtype=jnp.float32) * s, 'gate_b': jnp.zeros((E,), jnp.float32), 'W1': jax.random.normal(ks[2], (E, D, D), dtype=jnp.float32) * s, 'b1': jnp.zeros((E, D), jnp.float32), 'g1': jnp.ones((E, D), jnp.float32), 'be1': jnp.zeros((E, D), jnp.float32), 'W2': jax.random.normal(ks[3], (E, D, D), dtype=jnp.float32) * s, 'b2': jnp.zeros((E, D), jnp.float32), 'g2': jnp.ones((E, D), jnp.float32), 'be2': jnp.zeros((E, D), jnp.float32)}
    _L0_ffn_all = _L0_ffn_setup()
    _L0_ffn_in = {k: v for k, v in _L0_ffn_all.items() if k in ('gate_W', 'gate_b', 'W1', 'b1', 'g1', 'be1', 'W2', 'b2', 'g2', 'be2')}
    del _L0_ffn_all
    return {'x': x, 'ctx_1024': ctx_1024, 'L0_attn_Wz': _L0_attn_in['Wz'], 'L0_attn_bz': _L0_attn_in['bz'], 'L0_attn_Wh': _L0_attn_in['Wh'], 'L0_attn_bh': _L0_attn_in['bh'], 'L0_attn_Wg': _L0_attn_in['Wg'], 'L0_attn_bg': _L0_attn_in['bg'], 'L0_xattn_Wq': _L0_xattn_in['Wq'], 'L0_xattn_bq': _L0_xattn_in['bq'], 'L0_xattn_Wk': _L0_xattn_in['Wk'], 'L0_xattn_bk': _L0_xattn_in['bk'], 'L0_xattn_Wv': _L0_xattn_in['Wv'], 'L0_xattn_bv': _L0_xattn_in['bv'], 'L0_xattn_Wo': _L0_xattn_in['Wo'], 'L0_xattn_bo': _L0_xattn_in['bo'], 'L0_ffn_gate_W': _L0_ffn_in['gate_W'], 'L0_ffn_gate_b': _L0_ffn_in['gate_b'], 'L0_ffn_W1': _L0_ffn_in['W1'], 'L0_ffn_b1': _L0_ffn_in['b1'], 'L0_ffn_g1': _L0_ffn_in['g1'], 'L0_ffn_be1': _L0_ffn_in['be1'], 'L0_ffn_W2': _L0_ffn_in['W2'], 'L0_ffn_b2': _L0_ffn_in['b2'], 'L0_ffn_g2': _L0_ffn_in['g2'], 'L0_ffn_be2': _L0_ffn_in['be2']}

def reference(x, ctx_1024, L0_attn_Wz, L0_attn_bz, L0_attn_Wh, L0_attn_bh, L0_attn_Wg, L0_attn_bg, L0_xattn_Wq, L0_xattn_bq, L0_xattn_Wk, L0_xattn_bk, L0_xattn_Wv, L0_xattn_bv, L0_xattn_Wo, L0_xattn_bo, L0_ffn_gate_W, L0_ffn_gate_b, L0_ffn_W1, L0_ffn_b1, L0_ffn_g1, L0_ffn_be1, L0_ffn_W2, L0_ffn_b2, L0_ffn_g2, L0_ffn_be2):
    import jax
    import jax.numpy as jnp

    def _L0_attn_ref(x, Wz, bz, Wh, bh, Wg, bg):
        import jax, jax.numpy as jnp
        import numpy as np
        B, S, D = (4, 4096, 512)
        N = 4
        K = D // N
        Z_BIAS_MIN, Z_BIAS_MAX = (-2.0, 2.0)

        def _binop(q_i, q_j):
            a_i, b_i = q_i
            a_j, b_j = q_j
            return (a_i * a_j, a_j * b_i + b_j)
        b_, s_, d_ = x.shape
        z = jax.nn.sigmoid(jnp.einsum('bsd,ndk->bsnk', x, Wz) + bz)
        h_tilde = jnp.einsum('bsd,ndk->bsnk', x, Wh) + bh
        a = (1.0 - z).reshape(b_, s_, d_)
        bb = (z * h_tilde).reshape(b_, s_, d_)
        _, h = jax.lax.associative_scan(_binop, (a, bb), axis=1)
        gate = jax.nn.sigmoid(jnp.einsum('bsd,de->bse', h, Wg) + bg)
        return gate * h

    def _L0_xattn_ref(q, k, v, Wq, bq, Wk, bk, Wv, bv, Wo, bo):
        import jax, jax.numpy as jnp
        import numpy as np
        D_MODEL = 512
        HEADS = 16
        D_HEAD = D_MODEL // HEADS
        CAUSAL = True

        def _split(x):
            B, L, _ = x.shape
            return x.reshape(B, L, HEADS, D_HEAD).transpose(0, 2, 1, 3)
        qh = _split(q @ Wq + bq)
        kh = _split(k @ Wk + bk)
        vh = _split(v @ Wv + bv)
        scores = jnp.einsum('bhqd,bhkd->bhqk', qh, kh) / jnp.sqrt(jnp.float32(D_HEAD))
        if CAUSAL:
            Lq, Lk = (q.shape[1], k.shape[1])
            mask = jnp.triu(jnp.ones((Lq, Lk), bool), k=1)
            scores = jnp.where(mask[None, None], -jnp.inf, scores)
        attn = jax.nn.softmax(scores, axis=-1)
        out = jnp.einsum('bhqk,bhkd->bhqd', attn, vh)
        B, H, L, Dh = out.shape
        out = out.transpose(0, 2, 1, 3).reshape(B, L, H * Dh)
        return out @ Wo + bo

    def _L0_ffn_ref(x, gate_W, gate_b, W1, b1, g1, be1, W2, b2, g2, be2):
        import jax, jax.numpy as jnp
        import numpy as np
        LN_EPS = 1e-05

        def _layernorm(x, g, b):
            m = jnp.mean(x, axis=-1, keepdims=True)
            v = jnp.mean(jnp.square(x - m), axis=-1, keepdims=True)
            return (x - m) * jax.lax.rsqrt(v + LN_EPS) * g + b
        K_TOP = 2
        B, N, D = x.shape
        BN = B * N
        xf = x.reshape(BN, D)
        gate_scores = xf @ gate_W + gate_b
        topk_scores, topk_idx = jax.lax.top_k(gate_scores, K_TOP)
        weights = jax.nn.softmax(topk_scores, axis=-1)

        def expert(w1, bb1, gg1, bbe1, w2, bb2, gg2, bbe2):
            h = jax.nn.relu(_layernorm(xf @ w1 + bb1, gg1, bbe1))
            return _layernorm(h @ w2 + bb2, gg2, bbe2)
        all_out = jax.vmap(expert)(W1, b1, g1, be1, W2, b2, g2, be2)
        exp_out = all_out[topk_idx, jnp.arange(BN)[:, None]]
        out = jnp.sum(weights[..., None] * exp_out, axis=1)
        return (out + xf).reshape(B, N, D)
    x = x + _L0_attn_ref(_layernorm(x, axis=-1), L0_attn_Wz, L0_attn_bz, L0_attn_Wh, L0_attn_bh, L0_attn_Wg, L0_attn_bg)
    x = x + _L0_xattn_ref(_layernorm(x, axis=-1), ctx_1024, ctx_1024, L0_xattn_Wq, L0_xattn_bq, L0_xattn_Wk, L0_xattn_bk, L0_xattn_Wv, L0_xattn_bv, L0_xattn_Wo, L0_xattn_bo)
    x = x + _L0_ffn_ref(_layernorm(x, axis=-1), L0_ffn_gate_W, L0_ffn_gate_b, L0_ffn_W1, L0_ffn_b1, L0_ffn_g1, L0_ffn_be1, L0_ffn_W2, L0_ffn_b2, L0_ffn_g2, L0_ffn_be2)
    return x

_drawn_inputs = setup_inputs


def setup_inputs(seed=0):
    import zlib

    import numpy as np

    out = dict(_drawn_inputs(seed))
    spreads = {'L0_attn_bh': (0.0, 0.1),
     'L0_attn_bg': (0.0, 0.1),
     'L0_xattn_bq': (0.0, 0.1),
     'L0_xattn_bk': (0.0, 0.8),
     'L0_xattn_bv': (0.0, 0.1),
     'L0_xattn_bo': (0.0, 0.1),
     'L0_ffn_gate_b': (0.0, 0.1),
     'L0_ffn_b1': (0.0, 0.1),
     'L0_ffn_g1': (1.0, 0.2),
     'L0_ffn_be1': (0.0, 0.269),
     'L0_ffn_b2': (0.0, 0.1),
     'L0_ffn_g2': (1.0, 0.2),
     'L0_ffn_be2': (0.0, 0.269)}
    factors = {}
    for name, (base, spread) in spreads.items():
        noise = np.random.default_rng([zlib.crc32(name.encode()), seed]).standard_normal(out[name].shape)
        drawn = base * np.exp(spread * noise) if base else spread * noise
        out[name] = jnp.asarray(drawn.astype(out[name].dtype))
    for name, factor in factors.items():
        out[name] = (out[name] * factor).astype(out[name].dtype)
    return out
```

```python
from contextlib import ExitStack

import numpy as np
import concourse.bass as bass
from concourse import mybir

F32, F32R, I32 = mybir.dt.float32, mybir.dt.float32r, mybir.dt.int32
ACT = mybir.ActivationFunctionType
ALU = mybir.AluOpType
AX = mybir.AxisListType

P = 128
B, S, D = 2, 2048, 512
T = B * S
KC = D // P
CH = 512
TPC = CH // P
NCH = T // CH
NT = T // P
CPB = S // CH
NH, DH = 16, 32
HPG = P // DH
SK = 77
GK = HPG * SK
U = 3
UK = -(-GK // U)
NE = 4
EPS = 1e-5
NEG = -(2.0 ** 99)
NSLOT = 2 * T // P + NE - 1
REG = (T // P + NE + 2) * P
EARLY_CH = NCH - 2
EARLY = 2 * EARLY_CH * TPC - (NE - 1)
HI, LO = 0, 1
ROUTE_CHOSEN, ROUTE_COUNTED, ROUTE_SHIFTED, ROUTE_WEIGHED, NROUTE = 6, 10, 12, 21, 31
TERMS = ((HI, HI), (HI, LO), (LO, HI))
ROW_BZ, ROW_BH, ROW_BG, ROW_BQ, ROW_BK, ROW_G1, ROW_BE1 = 0, 4, 8, 12, 16, 20, 36
NROWS = 52


TABW = NE * REG // P


def need(engine, semaphore, value):
    if isinstance(value, int) and value <= 0:
        return
    engine.wait_ge(semaphore, value)


def need_alone(engine, semaphore, value, passed):
    need(engine, semaphore, value)
    engine.sem_inc(passed, 1)


def decoder_layer(nc, io, out, scratch_kind="Internal"):
    ctx = ExitStack()
    with ctx:
        def sb(name, shape, dt):
            return ctx.enter_context(nc.sbuf_tensor(name, shape, dt))

        def sem(name):
            return ctx.enter_context(nc.semaphore(name))

        def sems(names):
            return [sem(n) for n in names.split()]

        def dram(name, shape, dt):
            return nc.dram_tensor(name, shape, dt, kind=scratch_kind).ap()

        x1_d = dram("x1_rows", [T, D], F32)
        xf_d = dram("xf_rows", [T + P, D], F32)
        slots_d = dram("slot_table", [NE * REG, 2], I32)
        vb_d = dram("v_blocks", [B, 2 * KC * U, UK, P], F32)
        ws_d = dram("expert_parts", [2 * NE, P, 2, KC, D], F32)
        x_v = io["x"].rearrange("b (c j p) f -> (b c) p j f", j=TPC, p=P)
        x1_v = x1_d.rearrange("(c j p) f -> c p j f", j=TPC, p=P)
        xf_v = xf_d[0:T, :].rearrange("(n p) f -> n p f", p=P)
        out_v = out[0:T, :].rearrange("(n p) f -> n p f", p=P)

        KB_ = 256
        R = sb("operands", [P, 136 * KB_], F32R)
        F = sb("rows", [P, 64 * KB_], F32)

        def r_at(kb, n):
            return R[:, int(kb * KB_):int(kb * KB_) + n]

        def f_at(kb, n):
            return F[:, int(kb * KB_):int(kb * KB_) + n]

        def w_at(kb):
            return r_at(kb, 2 * KC * D).rearrange("p (a k f) -> p a k f", a=2, k=KC)

        wz, wh, wg, wk, wv = (w_at(16 * i) for i in range(5))
        wq, wo = wk, wv
        kblk = r_at(80, 2 * B * KC * GK).rearrange("p (a b m g) -> p a b m g", a=2, b=B, m=KC)
        xnT = w_at(100)
        hTr = w_at(116)
        w_stage = r_at(132, 2 * D).rearrange("p (a f) -> p a f", a=2)
        zeros_r = r_at(132, 4 * KB_)
        ctxT = r_at(100, 2 * KC * B * SK).rearrange("p (a k n) -> p a k n", a=2, k=KC)
        v_r = r_at(116, B * 2 * D).rearrange("p (b a f) -> p b a f", b=B, a=2)
        ring = f_at(0, 3 * TPC * D).rearrange("p (r j f) -> p r j f", r=3, j=TPC)
        xn = f_at(24, TPC * D).rearrange("p (j f) -> p j f", j=TPC)
        za = f_at(32, 2 * CH).rearrange("p (i t) -> p i t", i=2)
        zb = f_at(36, 2 * CH).rearrange("p (i t) -> p i t", i=2)
        hT = f_at(40, KC * CH).rearrange("p (m t) -> p m t", m=KC)
        gate = f_at(48, 2 * CH).rearrange("p (i t) -> p i t", i=2)
        ghT = f_at(52, KC * CH).rearrange("p (m t) -> p m t", m=KC)
        w_raw = f_at(60, 2 * D).rearrange("p (i f) -> p i f", i=2)
        raw = [f_at(24 + 8 * i, KC * D).rearrange("p (k f) -> p k f", k=KC) for i in range(5)]
        ctx_rows = f_at(8, B * D).rearrange("p (b f) -> p b f", b=B)
        v_rows = f_at(12, B * D).rearrange("p (b f) -> p b f", b=B)
        bv_rows = f_at(16, D)

        prow = f_at(20, P)[0:NROWS]
        tab0 = f_at(18, TABW * 2).bitcast(I32).rearrange("p (n w) -> p n w", w=2)

        x1T, qT, outT = (w_at(16 * i) for i in range(3))
        pT = r_at(100, 2 * U * CH).rearrange("p (a u t) -> p a u t", a=2, u=U)
        vblk = r_at(112, 2 * KC * U * P).rearrange("p (a m u f) -> p a m u f", a=2, m=KC, u=U)
        mask_r = r_at(124, CPB * GK).rearrange("p (s g) -> p s g", s=CPB)
        ident_r = r_at(130, P)
        x1n = xn
        pb = [f_at(32 + 5 * i, TPC * GK).rearrange("p (j g) -> p j g", j=TPC) for i in range(2)]
        xf = f_at(50, TPC * D).rearrange("p (j f) -> p j f", j=TPC)
        base = f_at(58, 2 * D).rearrange("p (i f) -> p i f", i=2)
        xfT = f_at(42, TPC * KC * P).rearrange("p (j k t) -> p j k t", j=TPC, k=KC)
        bo_rows = f_at(62, D)

        weights = r_at(0, 4 * NE * KC * D).rearrange("p (e w a k f) -> p e w a k f", e=NE, w=2, a=2, k=KC)
        xT = r_at(128, 2 * KC * P).rearrange("p (a k t) -> p a k t", a=2, k=KC)
        hTc = r_at(132, 2 * KC * P).rearrange("p (a k t) -> p a k t", a=2, k=KC)
        b1_rows, b2_rows, g2_rows, be2_rows = (f_at(kb, NE * D).rearrange("p (e f) -> p e f", e=NE)
                                               for kb in (8, 16, 24, 32))
        tile_slots = f_at(0, 2 * NSLOT).bitcast(I32).rearrange("p (i w) -> p i w", w=2)
        xg = [f_at(kb, D) for kb in (62, 40)]
        u1, n1, hf, v2, z2 = (f_at(kb, D) for kb in (42, 44, 46, 50, 52))
        u2 = [f_at(kb, D) for kb in (48, 58)]
        y2 = [f_at(kb, D) for kb in (54, 56)]

        ident = sb("ident", [P, P], F32)
        before = sb("before", [P, P], F32)
        ones = sb("ones", [P, P], F32)
        causal = sb("causal", [P, SK], F32)
        tie = sb("tie", [P, NE, NE], F32)
        region0 = sb("region0", [P, NE], F32)
        tok_i = sb("token_ints", [P, TPC], I32)
        tok = sb("tokens", [P, TPC], F32)
        half = sb("minus_half", [P, TPC], F32)
        gate_w = sb("gate_w", [P, KC, NE], F32)
        gate_b = sb("gate_b", [P, NE], F32)
        smax = sb("score_max", [P, TPC * HPG], F32)
        nmax = sb("score_shift", [P, 2, TPC * HPG], F32)
        ssum = sb("score_sum", [P, 2, TPC * HPG], F32)
        srec = sb("score_rec", [P, 2, TPC * HPG], F32)
        st3 = sb("ln3_stats", [P, TPC, 6], F32)
        mv3 = sb("ln3_mean_var", [P, TPC, 2], F32)
        ve3 = sb("ln3_var_eps", [P, TPC], F32)
        rs3 = sb("ln3_rstd", [P, TPC], F32)
        gs = sb("gate_scores", [P, TPC, NE], F32)
        gcmp = sb("gate_compare", [P, 2, TPC, NE, NE], F32)
        rank = sb("gate_rank", [P, TPC, NE], F32)
        sel = sb("gate_sel", [P, TPC, NE], F32)
        gmax = sb("gate_max", [P, TPC], F32)
        gexp = sb("gate_exp", [P, 2, TPC, NE], F32)
        grec = sb("gate_rec", [P, 2, TPC], F32)
        is_k = sb("is_kth", [P, 2, TPC, NE], F32)
        kth = sb("kth_of", [P, 2, TPC, NE], F32)
        counts = sb("counts", [P, TPC + 1, NE], F32)
        pos = sb("positions", [P, TPC, NE], F32)
        kval = sb("kth_value", [P, 2, 2, TPC], F32)
        slot_ix = sb("slot_rows", [P, 2, TPC], I32)
        payload = sb("slot_payload", [P, TPC, 2, 2], I32)
        plan_e = sb("plan_experts", [P, NSLOT], I32)
        plan_row = sb("plan_rows", [P, NSLOT], I32)
        plan_pair = sb("plan_pairs", [P, NSLOT // 2], I32)
        tile_no = sb("tile_numbers", [P, EARLY], F32)
        tile_ge = sb("tile_behind", [P, NE - 1, EARLY], F32)
        tile_e = sb("tile_experts", [P, EARLY], F32)
        tile_row = sb("tile_rows", [P, EARLY], F32)
        tile_int = sb("tile_ints", [P, EARLY], I32)
        total = sb("expert_totals", [P, NE], F32)
        total_i = sb("expert_total_ints", [P, NE], I32)
        tiles = sb("expert_tiles", [P, NE], F32)
        taken = sb("expert_tiles_taken", [P, NE], F32)
        first = sb("expert_first_tile", [P, NE], F32)
        jump = sb("expert_row_jump", [P, NE], F32)
        gix = [sb(f"gather_rows{i}", [P, 1], I32) for i in range(2)]
        six = [sb(f"scatter_rows{i}", [P, 1], I32) for i in range(2)]
        c_st = sb("moe_stats", [P, 2, 6], F32)
        c_mv = sb("moe_mean_var", [P, 2, 2], F32)
        c_ve = sb("moe_var_eps", [P, 2], F32)
        c_rs = sb("moe_rstd", [P, 2], F32)
        pcol = sb("param_cols", [P, NROWS], F32)
        carry = sb("carry", [P, KC, NCH + B + 1], F32)
        st1 = sb("ln1_stats", [P, TPC, 6], F32)
        mv1 = sb("ln1_mean_var", [P, TPC, 2], F32)
        ve1 = sb("ln1_var_eps", [P, TPC], F32)
        rs1 = sb("ln1_rstd", [P, TPC], F32)
        st2 = sb("ln2_stats", [P, TPC, 6], F32)
        mv2 = sb("ln2_mean_var", [P, TPC, 2], F32)
        mean2 = sb("ln2_mean", [P, NT], F32)
        ve2 = sb("ln2_var_eps", [P, NT], F32)
        rs2 = sb("ln2_rstd", [P, NT], F32)

        ps = ctx.enter_context(nc.psum_tensor("banks", [P, 8, CH], F32))
        mm_bank = [ps[:, i, :] for i in (2, 3)]
        s_banks = ps[:, 4:8, 0:GK]
        t_bank = [ps[:, i, :] for i in (0, 1)]
        z_bank = [ps[:, i, :] for i in (2, 3)]
        h_bank = [ps[:, i, :] for i in (4, 5)]
        g_bank = [ps[:, i, :] for i in (6, 7)]

        cx_bank, ch_bank, m1_bank, m2_bank = (ps[:, i, :] for i in range(4, 8))

        (const_ready, prow_in, ptr_done, pcol_ready, ctx_in, wk_in, wv_in, wz_in, wh_in, wg_in, bv_in,
         w_hi, w_lo, ctxT_done, ctxT_hi, ctxT_lo, k_done, k_hi, k_lo, v_done, v_ready, v_hi, v_lo,
         zero_out, vb_out, kzero, pool_step, dve_passed, pool_passed) = sems(
            "const_ready prow_in ptr_done pcol_ready ctx_in wk_in wv_in wz_in wh_in wg_in bv_in "
            "w_hi w_lo ctxT_done ctxT_hi ctxT_lo k_done k_hi k_lo v_done v_ready v_hi v_lo "
            "zero_out vb_out kzero pool_step dve_passed pool_passed")
        (x_in, ln1_stat, ln1_aggr, ln1_eps, ln1_rstd, xn_ready, a_t_done, xnT_hi, a_t_read, z_done,
         h_done, z_ready, b_ready, a_ready, h_ready, carry_ready, hT_hi, hT_lo, g_done, gate_ready, gh_ready,
         x1_out, ln2_stat, ln2_aggr, ln2_eps, ln2_rstd, split_hi, split_lo, split_out) = sems(
            "x_in ln1_stat ln1_aggr ln1_eps ln1_rstd xn_ready a_t_done xnT_hi a_t_read z_done "
            "h_done z_ready b_ready a_ready h_ready carry_ready hT_hi hT_lo g_done gate_ready gh_ready "
            "x1_out ln2_stat ln2_aggr ln2_eps ln2_rstd split_hi split_lo split_out")
        (consts_done, tok_ready, gw_in, bo_in, x1_in, vb_in, mask_ready, x1n_ready, x1b_ready, b_t_done, x1T_hi, b_t_read,
         mm_done, mm_read, qT_hi, s_done, s_read, smax_ready, shift_ready, p_rec, p_ready, pT_hi, outT_hi,
         ln3_stat, ln3_aggr, ln3_eps, ln3_rstd, xf_ready, base_ready, gs_ready, route, route_exp,
         scattered, prefill_ready, prefill_out) = sems(
            "consts_done tok_ready gw_in bo_in x1_in vb_in mask_ready x1n_ready x1b_ready b_t_done x1T_hi b_t_read "
            "mm_done mm_read qT_hi s_done s_read smax_ready shift_ready p_rec p_ready pT_hi outT_hi "
            "ln3_stat ln3_aggr ln3_eps ln3_rstd xf_ready base_ready gs_ready route route_exp "
            "scattered prefill_ready prefill_out")
        (p1_in, plan, plan_ready, experts_ready, cx_done, cx_hi, cx_lo, m1_done, u1_ready, ch_done, relu_done,
         hh_ready, hl_ready, m2_done, u2_ready, c1_stat, c1_aggr, c1_eps, c1_rstd, n1_ready, c2_stat, c2_aggr, c2_eps,
         c2_rstd, v2_ready, z2_ready, y2_ready) = sems(
            "p1_in plan plan_ready experts_ready cx_done cx_hi cx_lo m1_done u1_ready ch_done relu_done "
            "hh_ready hl_ready m2_done u2_ready c1_stat c1_aggr c1_eps c1_rstd n1_ready c2_stat c2_aggr c2_eps "
            "c2_rstd v2_ready z2_ready y2_ready")
        w_in = [sem(f"w_in{i}") for i in range(2 * NE)]
        slots_in = [sem(f"slots_in{i}") for i in range(2)]
        gix_ready, six_ready = sems("gix_ready six_ready")
        gathered = [sem(f"gathered{i}") for i in range(2)]
        added = [sem(f"added{i}") for i in range(2)]
        split_in = [sem(f"split_in{i}") for i in range(2)]
        xf_out = [sem(f"xf_out{i}") for i in range(TPC)]
        base_out = [sem(f"base_out{i}") for i in range(2)]

        def t_group(c):
            return 0 if isinstance(c, int) and c == 0 else 8 * c - 4

        def tg_group(c):
            return 8 * (NCH - 1) + 4 if isinstance(c, int) and c == NCH - 1 else 8 * c + 8

        A_T_GROUPS = 8 * NCH

        T_ORDER = "p00 p01 p02 x0 x1 x2 x3 p10 p11 p12 xf0 xf1 p20 p21 p22 xf2 xf3 p30 p31 p32".split()
        MM_ORDER = "o0 o1 r o2 v0 o3 q0 v1 q1 q2 v2 q3 g v3".split()

        LEAD = {id(T_ORDER): "x0 x1 x2 x3".split(), id(MM_ORDER): "q0 q1 q2 q3".split()}
        TAIL = {id(T_ORDER): "xf0 xf1 xf2 xf3".split(), id(MM_ORDER): "o0 o1 r o2 o3 g t".split()}

        def groups_of(order, c):
            if isinstance(c, int) and not 0 <= c < NCH:
                return [(g, i % 2) for i, g in enumerate((LEAD if c < 0 else TAIL)[id(order)])]
            n = c if isinstance(c, int) else 2
            return [(g, i % 2) for i, g in enumerate(order) if not (
                n == 0 and (g[0] in "go" or g[:2] == "xf") or n < 2 and g == "r"
                or n == NCH - 1 and (g[0] == "q" or g in ("x0", "x1", "x2", "x3")))]

        def in_front(order, c):
            if isinstance(c, int):
                return sum(len(groups_of(order, i)) for i in range(-1, c))
            return in_front(order, 2) + (c - 2) * len(order)

        def index_in(order, c, name):
            return [g for g, _ in groups_of(order, c)].index(name)

        def t_num(c, name):
            return in_front(T_ORDER, c) + index_in(T_ORDER, c, name)

        def mm_num(c, name):
            return in_front(MM_ORDER, c) + index_in(MM_ORDER, c, name)

        def bank_of(order, c, name):
            return dict(groups_of(order, c))[name]

        def last_in_bank(order, c, name):
            before_c = c - 1 if isinstance(c, int) else 1 if len(groups_of(order, 1)) == len(order) else 2
            own = groups_of(order, c)
            at = index_in(order, c, name)
            older = [] if isinstance(c, int) and c < 0 else groups_of(order, before_c)
            row = older + own[:at]
            same = [i for i, (_, bank) in enumerate(row) if bank == own[at][1]]
            return in_front(order, c) - len(older) + same[-1] + 1 if same else 0

        def tb(c, name):
            return t_bank[bank_of(T_ORDER, c, name)]

        def mb(c, name):
            return mm_bank[bank_of(MM_ORDER, c, name)]

        def slot3(c):
            return ring[:, (c + NCH) % 3] if isinstance(c, int) else ring[:, bass.ds((c + NCH) % 3, 1)].rearrange(
                "p r j f -> p (r j) f")

        def expert_at(engine, i):
            return engine.value_load(plan_e[0:1, bass.ds(i, 1)], min_val=0, max_val=NE - 1)

        def experts_around(engine, n):
            packed = engine.value_load(plan_pair[0:1, bass.ds(n, 1)], min_val=0, max_val=NE ** 5 - 1)
            return [packed % NE] + [packed // NE ** k % NE for k in range(1, 4)] + [packed // NE ** 4]

        def tiles_of(engine, tile):
            def alone(i):
                around = [expert_at(engine, t) if 0 <= t < NSLOT else None for t in range(i - 1, i + 3)]
                tile(i // 2, i % 2, around, NSLOT - 1 - i)
            for i in range(4):
                alone(i)
            with engine.Fori(2, (NSLOT - 5) // 2) as n:
                around = experts_around(engine, n)
                for u in range(2):
                    tile(n, u, around[u:u + 4], NSLOT)
            for i in range(NSLOT - 5, NSLOT):
                alone(i)

        block = ctx.enter_context(nc.Block())

        def split_source(n):
            return ("L0_ffn_W1", "L0_ffn_W2")[n // 2], n % 2

        @block.sync
        def _(sp):
            for name, row, n in (("L0_attn_bz", ROW_BZ, 4), ("L0_attn_bh", ROW_BH, 4)):
                sp.dma_start(prow[row:row + n, :], io[name]).then_inc(prow_in, 16)
            for name, row in (("L0_attn_bg", ROW_BG), ("L0_xattn_bq", ROW_BQ), ("L0_xattn_bk", ROW_BK)):
                sp.dma_start(prow[row:row + KC, :], io[name].rearrange("(k p) -> k p", p=P)).then_inc(prow_in, 16)
            for name, row in (("L0_ffn_g1", ROW_G1), ("L0_ffn_be1", ROW_BE1)):
                sp.dma_start(prow[row:row + NE * KC, :],
                             io[name].rearrange("e (k p) -> (e k) p", p=P)).then_inc(prow_in, 16)
            sp.dma_start(ctx_rows[0:SK], io["ctx_1024"].rearrange("b s f -> s b f")).then_inc(ctx_in, 16)
            sp.dma_start(raw[3], io["L0_xattn_Wk"].rearrange("(k p) f -> p k f", p=P)).then_inc(wk_in, 16)
            sp.dma_start(raw[4], io["L0_xattn_Wv"].rearrange("(k p) f -> p k f", p=P)).then_inc(wv_in, 16)
            sp.dma_start(bv_rows[0:SK], io["L0_xattn_bv"].partition_broadcast(SK)).then_inc(bv_in, 16)
            sp.dma_start(ring[:, 0], x_v[0]).then_inc(x_in, 16)
            for slot, name, loaded in ((0, "L0_attn_Wz", wz_in), (1, "L0_attn_Wh", wh_in)):
                for n in range(KC):
                    sp.dma_start(raw[slot][:, :, n * P:(n + 1) * P],
                                 io[name][n].rearrange("(k p) f -> p k f", p=P)).then_inc(loaded, 16)
            sp.dma_start(raw[2], io["L0_attn_Wg"].rearrange("(k p) f -> p k f", p=P)).then_inc(wg_in, 16)
            need(sp, kzero, 1)
            flat = vb_d.rearrange("b g r f -> (b g r f)").rearrange("(p n) -> p n", p=P)
            n_zero = flat.shape[1] // 8
            for i in range(8):
                sp.dma_start(flat[:, i * n_zero:(i + 1) * n_zero], zeros_r[:, 0:n_zero].bitcast(F32)).then_inc(zero_out, 16)
            sp.dma_start(xf_d[T:T + P, :], zeros_r[:, 0:D].bitcast(F32)).then_inc(zero_out, 16)
            sp.dma_start(out[T:T + P, :], zeros_r[:, 0:D].bitcast(F32)).then_inc(zero_out, 16)
            sp.wait_ge(zero_out, 16 * 10)
            sp.wait_ge(v_hi, B)
            sp.wait_ge(v_lo, B)
            for b in range(B):
                for part in (HI, LO):
                    rows = vb_d[b, part * KC * U:(part + 1) * KC * U].rearrange("(m u) r f -> m (u r) f", m=KC)
                    for hl in range(HPG):
                        sp.dma_start(
                            rows[:, hl * SK:(hl + 1) * SK, hl * DH:(hl + 1) * DH].rearrange("m s f -> s m f"),
                            v_r[0:SK, b, part, :].rearrange("p (m f) -> p m f", m=KC)[:, :, hl * DH:(hl + 1) * DH].bitcast(F32),
                        ).then_inc(vb_out, 16)
            sp.dma_start(gate_w[:, :, :], io["L0_ffn_gate_W"].rearrange("(k p) e -> p k e", p=P)).then_inc(gw_in, 16)
            sp.dma_start(gate_b[:, :], io["L0_ffn_gate_b"].partition_broadcast(P)).then_inc(gw_in, 16)
            sp.wait_ge(prefill_ready, 1)
            sp.dma_start(slots_d.rearrange("(p n) w -> p n w", p=P), tab0[:, :, :]).then_inc(prefill_out, 16)
            sp.wait_ge(w_lo, 2)
            sp.dma_start(raw[3], io["L0_xattn_Wq"].rearrange("(k p) f -> p k f", p=P)).then_inc(wk_in, 16)
            sp.dma_start(raw[4], io["L0_xattn_Wo"].rearrange("(k p) f -> p k f", p=P)).then_inc(wv_in, 16)
            sp.wait_ge(prefill_out, 16)
            sp.wait_ge(pcol_ready, 1)
            sp.wait_ge(ctxT_done, 2)
            sp.wait_ge(x_in, 16)
            sp.wait_ge(v_lo, B)
            sp.dma_start(ring[:, 1], x_v[1]).then_inc(x_in, 16)
            sp.wait_ge(x_in, 32)
            sp.dma_start(ring[:, 2], x_v[2]).then_inc(x_in, 16)

            def a_chunk(c, last=False):
                for n in range(4):
                    need(sp, split_lo, 4 * c + n - 1)
                    if n < 2 and isinstance(c, int) and c == 0:
                        sp.wait_ge(w_lo, 7)
                    name, k = split_source(n)
                    src = io[name].rearrange("e (k p) f -> e k p f", p=P)
                    e, kc = c // 2, (c % 2) * 2 + k
                    src = src[e, kc] if isinstance(c, int) else src[bass.ds(e, 1), bass.ds(kc, 1)].rearrange(
                        "a b p f -> p (a b f)")
                    sp.dma_start(w_raw[:, n % 2], src).then_inc(split_in[n % 2], 16)
                    if not (isinstance(c, int) and c == 0 and n == 0):
                        store_piece(c if n else c - 1, (n - 1) % 4, 4 * c + n)

            def store_piece(c, n, count):
                need(sp, split_lo, count)
                e2 = (c // 2) * 2 + n // 2
                kc = (c % 2) * 2 + n % 2
                dst = ws_d[e2, :, :, kc, :] if isinstance(c, int) else ws_d[
                    bass.ds(e2, 1), :, :, bass.ds(kc, 1), :].rearrange("m p a k f -> p (m a k) f")
                sp.dma_start(dst, w_stage[:, :, :].bitcast(F32)).then_inc(split_out, 16)

            def a_store(c, prefetch=True):
                need(sp, ln2_stat, 4 * (c + 1))
                x1 = ring[:, c % 3] if isinstance(c, int) else ring[:, bass.ds(c % 3, 1)].rearrange(
                    "p r j f -> p (r j) f")
                dst = x1_v[c] if isinstance(c, int) else x1_v[bass.ds(c, 1)].rearrange("c p j f -> p (c j) f")
                sp.dma_start(dst, x1).then_inc(x1_out, 16)
                sp.wait_ge(x1_out, 16 * (c + 1))
                if isinstance(c, int) and c >= NCH - 3:
                    sp.dma_start(x1, x1_v[c - (NCH - 3)]).then_inc(x1_in, 16)
                if prefetch:
                    sp.wait_ge(x_in, 16 * (c + 3))
                    src = x_v[c + 3] if isinstance(c, int) else x_v[bass.ds(c + 3, 1)].rearrange(
                        "c p j f -> p (c j) f")
                    sp.dma_start(x1, src).then_inc(x_in, 16)

            a_chunk(0)
            with sp.Fori(1, NCH - 2) as c:
                a_chunk(c)
                a_store(c - 1)
            a_chunk(NCH - 2)
            a_store(NCH - 3, prefetch=False)
            a_chunk(NCH - 1)
            a_store(NCH - 2, prefetch=False)
            store_piece(NCH - 1, 3, 4 * NCH)
            a_store(NCH - 1, prefetch=False)

            def load_v(c):
                need(sp, mm_done, mm_num(c - 1, "v3") + 1 if not (isinstance(c, int) and c == 0) else 0)
                b = c // CPB
                src = vb_d[b] if isinstance(b, int) else vb_d[bass.ds(b, 1)].rearrange("b g r f -> (b g) r f")
                sp.dma_start(vblk[0:UK].rearrange("p a m u f -> p (a m u) f").bitcast(F32),
                             src.rearrange("g r f -> r g f")).then_inc(vb_in, 16)

            def store_rows(c):
                for j in range(TPC):
                    t = 4 * c + j
                    need(sp, xf_ready, t + 1)
                    sp.dma_start(xf_v[t] if isinstance(t, int) else xf_v[bass.ds(t, 1)].rearrange("n p f -> p (n f)"),
                                 xf[:, j]).then_inc(xf_out[j], 16)
                    need(sp, base_ready, t + 1)
                    sp.dma_start(out_v[t] if isinstance(t, int) else out_v[bass.ds(t, 1)].rearrange("n p f -> p (n f)"),
                                 base[:, j % 2]).then_inc(base_out[j % 2], 16)

            def b_chunk(c, first=False, load=True):
                load_v(c)
                if not first:
                    store_rows(c - 1)
                    if load:
                        sp.wait_ge(x1_in, 16 * (c + 2))
                        src = x1_v[c + 2] if isinstance(c, int) else x1_v[bass.ds(c + 2, 1)].rearrange(
                            "c p j f -> p (c j) f")
                        sp.dma_start(slot3(c + 2), src).then_inc(x1_in, 16)

            sp.wait_ge(w_lo, 7)
            sp.wait_ge(g_done, KC * NCH)
            sp.dma_start(bo_rows, io["L0_xattn_bo"].partition_broadcast(P)).then_inc(bo_in, 16)
            b_chunk(0, first=True)
            b_chunk(1)
            with sp.Fori(2, NCH - 2) as c:
                b_chunk(c)
            b_chunk(NCH - 2, load=False)
            load_v(NCH - 1)

            def load_expert(s):
                e, w = s // 2, s % 2
                sp.dma_start(weights[:, e, w].rearrange("p a k f -> p (a k f)").bitcast(F32),
                             ws_d[s].rearrange("p a k f -> p (a k f)")).then_inc(w_in[s], 16)

            def load_rows(dst, name):
                sp.dma_start(dst, io[name].rearrange("e f -> (e f)").partition_broadcast(P).rearrange(
                    "p (e f) -> p e f", e=NE)).then_inc(p1_in, 16)

            sp.wait_ge(split_out, 16 * 4 * NCH)
            sp.wait_ge(mm_done, mm_num(NCH - 2, "q3") + 1)
            load_expert(0)
            load_expert(3)
            load_rows(b1_rows, "L0_ffn_b1")
            load_rows(g2_rows, "L0_ffn_g2")
            store_rows(NCH - 2)
            load_rows(b2_rows, "L0_ffn_b2")
            sp.wait_ge(s_done, 2 * KC * NCH)
            load_expert(1)
            load_expert(5)
            sp.wait_ge(b_t_done, t_num(NCH - 1, f"p3{U - 1}") + 1)
            load_rows(be2_rows, "L0_ffn_be2")
            sp.wait_ge(mm_done, mm_num(NCH - 1, "v3") + 1)
            load_expert(6)
            load_expert(7)
            sp.wait_ge(mm_done, mm_num(NCH, "o3") + 1)
            load_expert(2)
            load_expert(4)
            store_rows(NCH - 1)
            for e in range(NE):
                sp.wait_ge(w_in[2 * e], 16)
                sp.wait_ge(w_in[2 * e + 1], 16)
                sp.sem_inc(experts_ready, 1)

            def load_slots(n, u):
                i = 2 * n + u
                row = sp.value_load(plan_row[0:1, bass.ds(i, 1)], min_val=0, max_val=NE * REG - P)
                need(sp, slots_in[u], 16 * n)
                sp.dma_start(tile_slots[:, bass.ds(i, 1), :].rearrange("p i w -> p (i w)"),
                             slots_d[bass.ds(row, P), :]).then_inc(slots_in[u], 16)

            sp.wait_ge(plan_ready, 2)
            sp.wait_ge(scattered, 16 * 2 * NT)
            for u in range(2):
                load_slots(0, u)
            with sp.Fori(1, NSLOT // 2) as n:
                for u in range(2):
                    load_slots(n, u)
            load_slots(NSLOT // 2, 0)

        @block.tensor
        def _(pe):
            def product(dst, terms, n_k, stationary, moving):
                last = None
                for t, (a, b) in enumerate(terms):
                    for k in range(n_k):
                        last = nc.tensor.matmul(dst, stationary(a, k), moving(b, k), start=(t == 0 and k == 0),
                                                stop=(t == len(terms) - 1 and k == n_k - 1))
                return last

            pe.wait_ge(const_ready, 1)
            pe.wait_ge(prow_in, 16 * 7)
            nc.tensor.transpose(g_bank[0][:, 0:NROWS], prow[:, :], ident[0:NROWS, 0:NROWS]).then_inc(ptr_done, 1)
            pe.wait_ge(ctx_in, 16)
            for half_k in range(2):
                for b in range(B):
                    for i in range(2):
                        k = 2 * half_k + i
                        last = nc.tensor.transpose(
                            t_bank[half_k][:, i * B * SK + b * SK:i * B * SK + (b + 1) * SK],
                            ctx_rows[0:SK, b, k * P:(k + 1) * P], ident[0:SK, 0:SK])
                last.then_inc(ctxT_done, 1)
            pe.wait_ge(w_lo, 1)
            pe.wait_ge(ctxT_lo, 2)
            for m in range(KC):
                if m >= 2:
                    pe.wait_ge(k_lo, HPG * (m - 1))
                product(z_bank[m % 2][:, 0:B * SK], TERMS, KC,
                        lambda a, k: wk[:, a, k, m * P:(m + 1) * P],
                        lambda a, k: ctxT[:, a, k, :]).then_inc(k_done, 1)
            pe.wait_ge(w_lo, 2)
            for b in range(B):
                product(h_bank[b][0:SK, :], TERMS, KC,
                        lambda a, k: ctxT[:, a, k, b * SK:(b + 1) * SK],
                        lambda a, k: wv[:, a, k, :]).then_inc(v_done, 1)

            def transpose_x(c):
                for k in range(KC):
                    g = t_group(c) + k
                    need(pe, a_t_read, g - 1)
                    for j in range(TPC):
                        if k == 0:
                            pe.wait_ge(xn_ready, 4 * c + j + 1)
                        last = nc.tensor.transpose(t_bank[k % 2][:, j * P:(j + 1) * P],
                                                   xn[:, j, k * P:(k + 1) * P], ident[:, :])
                    last.then_inc(a_t_done, 1)

            def z_and_h(c, back=True):
                pe.wait_ge(a_t_read, t_group(c) + 4)
                for m in range(KC):
                    n = 4 * c + m
                    need(pe, z_ready, n - 1)
                    product(z_bank[m % 2], TERMS, KC, lambda a, k: wz[:, a, k, m * P:(m + 1) * P],
                            lambda a, k: xnT[:, a, k, :]).then_inc(z_done, 1)
                    need(pe, b_ready, n - 1)
                    product(h_bank[m % 2], TERMS, KC, lambda a, k: wh[:, a, k, m * P:(m + 1) * P],
                            lambda a, k: xnT[:, a, k, :]).then_inc(h_done, 1)
                    if back:
                        gated_back(c - 1, m)

            def gates(c):
                for m in range(KC):
                    n = 4 * c + m
                    need(pe, gate_ready, n - 1)
                    if m == 0:
                        pe.wait_ge(hT_lo, 4 * c + 4)
                    product(g_bank[m % 2], TERMS, KC, lambda a, k: wg[:, a, k, m * P:(m + 1) * P],
                            lambda a, k: hTr[:, a, k, :]).then_inc(g_done, 1)

            def gated_back(c, j):
                g = tg_group(c) + j
                pe.wait_ge(a_t_read, g - 1)
                for m in range(KC):
                    if j == 0:
                        pe.wait_ge(gh_ready, 4 * c + m + 1)
                    last = nc.tensor.transpose(t_bank[j % 2][:, m * P:(m + 1) * P],
                                               ghT[:, m, j * P:(j + 1) * P], ident[:, :])
                last.then_inc(a_t_done, 1)

            pe.wait_ge(ctxT_lo, 2)
            transpose_x(0)
            pe.wait_ge(k_lo, HPG * KC)
            pe.wait_ge(v_ready, B)
            pe.wait_ge(w_lo, 4)
            z_and_h(0, back=False)
            transpose_x(1)
            pe.wait_ge(pcol_ready, 1)
            pe.wait_ge(w_lo, 5)
            gates(0)
            with pe.Fori(1, NCH - 1) as c:
                z_and_h(c)
                transpose_x(c + 1)
                gates(c)
            z_and_h(NCH - 1)
            gates(NCH - 1)
            for j in range(TPC):
                gated_back(NCH - 1, j)

            def t_free(c, name):
                need(pe, b_t_read, last_in_bank(T_ORDER, c, name))

            def mm_free(c, name):
                need(pe, mm_read, last_in_bank(MM_ORDER, c, name))

            def x1_to_features(c, at, ks):
                for k in ks:
                    t_free(at, f"x{k}")
                    for j in range(TPC):
                        if k == 0:
                            pe.wait_ge(x1n_ready, 4 * c + j + 1)
                        last = nc.tensor.transpose(tb(at, f"x{k}")[:, j * P:(j + 1) * P],
                                                   x1n[:, j, k * P:(k + 1) * P], ident[:, :])
                    last.then_inc(b_t_done, 1)

            def queries(c, at, m):
                mm_free(at, f"q{m}")
                pe.wait_ge(b_t_read, t_num(c - 1, "x3") + 1)
                product(mb(at, f"q{m}"), TERMS, KC, lambda a, k: wq[:, a, k, m * P:(m + 1) * P],
                        lambda a, k: x1T[:, a, k, :]).then_inc(mm_done, 1)

            def scores(c, m, tiles):
                need(pe, s_read, TPC * HPG * (4 * c + m - 1) + HPG * (tiles[-1] + 1))
                if tiles[0] == 0:
                    need(pe, mm_read, mm_num(c - 1, f"q{m}") + 1)
                b = c // CPB
                for j in tiles:
                    for t, (a, a2) in enumerate(TERMS):
                        keys = kblk[:, a2, b, m, :] if isinstance(b, int) else kblk[:, a2, bass.ds(b, 1), m, :].rearrange(
                            "p b g -> p (b g)")
                        last = nc.tensor.matmul(s_banks[:, j, :], qT[:, a, m, j * P:(j + 1) * P], keys,
                                                start=(t == 0), stop=(t == len(TERMS) - 1 and j > 0))
                    if j == 0:
                        s = c % CPB
                        last = nc.tensor.matmul(
                            s_banks[:, j, :], ident_r, mask_r[:, s, :] if isinstance(s, int) else
                            mask_r[:, bass.ds(s, 1), :].rearrange("p s g -> p (s g)"), start=False, stop=True)
                last.then_inc(s_done, 1)

            def probs_to_keys(c, m, parts):
                for u in parts:
                    if u == 0:
                        pe.wait_ge(p_ready, 4 * c + m + 1)
                    n = min(UK, GK - u * UK)
                    t_free(c, f"p{m}{u}")
                    for j in range(TPC):
                        last = nc.tensor.transpose(tb(c, f"p{m}{u}")[0:n, j * P:(j + 1) * P],
                                                   pb[m % 2][:, j, u * UK:u * UK + n], ident[:, :])
                    last.then_inc(b_t_done, 1)

            def attend(c, m):
                mm_free(c, f"v{m}")
                pe.wait_ge(vb_in, 16 * (c + 1))
                pe.wait_ge(pT_hi, 12 * c + U * (m + 1))
                for t, (a, a2) in enumerate(((HI, HI), (LO, HI), (HI, LO))):
                    if a2 == LO:
                        pe.wait_ge(b_t_read, t_num(c, f"p{m}{U - 1}") + 1)
                    for u in range(U):
                        n = min(UK, GK - u * UK)
                        last = nc.tensor.matmul(mb(c, f"v{m}"), vblk[0:n, a, m, u, :], pT[0:n, a2, u, :],
                                                start=(t == 0 and u == 0), stop=(t == len(TERMS) - 1 and u == U - 1))
                last.then_inc(mm_done, 1)

            def project(c, at, j):
                mm_free(at, f"o{j}")
                for m in range(KC):
                    pe.wait_ge(mm_read, mm_num(c, f"v{m}") + 1)
                    for t, (a, a2) in enumerate(TERMS):
                        last = nc.tensor.matmul(mb(at, f"o{j}"), outT[:, a, m, j * P:(j + 1) * P], wo[:, a2, m, :],
                                                start=(m == 0 and t == 0), stop=(m == KC - 1 and t == len(TERMS) - 1))
                last.then_inc(mm_done, 1)

            def xf_to_features(c, at, j):
                t_free(at, f"xf{j}")
                pe.wait_ge(xf_ready, 4 * c + j + 1)
                for k in range(KC):
                    last = nc.tensor.transpose(tb(at, f"xf{j}")[:, k * P:(k + 1) * P], xf[:, j, k * P:(k + 1) * P],
                                               ident[:, :])
                last.then_inc(b_t_done, 1)

            def gate_scores(c, at):
                mm_free(at, "g")
                for j in range(TPC):
                    pe.wait_ge(b_t_read, t_num(at, f"xf{j}") + 1)
                    for k in range(KC):
                        last = nc.tensor.matmul(mb(at, "g")[:, j * NE:(j + 1) * NE], xfT[:, j, k, :], gate_w[:, k, :],
                                                start=(k == 0), stop=(k == KC - 1))
                last.then_inc(mm_done, 1)

            def positions(c, at, name, totals=False):
                mm_free(at, name)
                pe.wait_ge(route, NROUTE * c + ROUTE_COUNTED)
                dst = mb(at, name)[:, 0:TPC * NE]
                nc.tensor.matmul(dst, before[:, :], sel[:, :, :].rearrange("p j e -> p (j e)"), start=True, stop=False)
                last = nc.tensor.matmul(dst, ones[:, :], counts[:, 0:TPC, :].rearrange("p j e -> p (j e)"),
                                        start=False, stop=True)
                if totals:
                    last = nc.tensor.matmul(mb(at, name)[:, TPC * NE:(TPC + 1) * NE], ones[:, :], counts[:, TPC, :],
                                            start=True, stop=True)
                last.then_inc(mm_done, 1)

            def b_turn(c, back=True, back2=True, ahead=True):
                scores(c, 1, (2, 3))
                probs_to_keys(c, 0, (0, 1))
                if back:
                    project(c - 1, c, 0)
                probs_to_keys(c, 0, (2,))
                if ahead:
                    x1_to_features(c + 1, c, (0,))
                if back:
                    project(c - 1, c, 1)
                if ahead:
                    x1_to_features(c + 1, c, (1, 2))
                if back2:
                    positions(c - 2, c, "r", totals=not ahead)
                if back:
                    project(c - 1, c, 2)
                if ahead:
                    x1_to_features(c + 1, c, (3,))
                scores(c, 2, (0, 1))
                attend(c, 0)
                scores(c, 2, (2, 3))
                probs_to_keys(c, 1, (0, 1))
                if back:
                    project(c - 1, c, 3)
                probs_to_keys(c, 1, (2,))
                if back:
                    xf_to_features(c - 1, c, 0)
                if ahead:
                    queries(c + 1, c, 0)
                if back:
                    xf_to_features(c - 1, c, 1)
                scores(c, 3, (0, 1))
                attend(c, 1)
                scores(c, 3, (2, 3))
                probs_to_keys(c, 2, (0, 1))
                if ahead:
                    queries(c + 1, c, 1)
                probs_to_keys(c, 2, (2,))
                if back:
                    xf_to_features(c - 1, c, 2)
                if ahead:
                    queries(c + 1, c, 2)
                if back:
                    xf_to_features(c - 1, c, 3)
                if ahead:
                    scores(c + 1, 0, (0, 1))
                attend(c, 2)
                if ahead:
                    scores(c + 1, 0, (2, 3))
                probs_to_keys(c, 3, (0, 1))
                if ahead:
                    queries(c + 1, c, 3)
                probs_to_keys(c, 3, (2,))
                if back:
                    gate_scores(c - 1, c)
                if ahead:
                    scores(c + 1, 1, (0, 1))
                attend(c, 3)

            pe.wait_ge(consts_done, 1)
            pe.wait_ge(gw_in, 32)
            pe.wait_ge(w_lo, 7)
            pe.wait_ge(a_t_read, A_T_GROUPS)
            pe.wait_ge(z_ready, KC * NCH)
            x1_to_features(0, -1, range(KC))
            for m in range(KC):
                queries(0, -1, m)
            pe.wait_ge(b_ready, KC * NCH)
            pe.wait_ge(gate_ready, KC * NCH)
            pe.wait_ge(mask_ready, 2)
            scores(0, 0, (0, 1))
            scores(0, 0, (2, 3))
            scores(0, 1, (0, 1))
            b_turn(0, back=False, back2=False)
            b_turn(1, back2=False)
            with pe.Fori(2, NCH - 1) as c:
                b_turn(c)
            b_turn(NCH - 1, ahead=False)
            for j in range(TPC):
                project(NCH - 1, NCH, j)
                if j == 1:
                    positions(NCH - 2, NCH, "r")
            for j in range(TPC):
                xf_to_features(NCH - 1, NCH, j)
            gate_scores(NCH - 1, NCH)
            positions(NCH - 1, NCH, "t", totals=True)

            def expert_product(dst, e, w, stationary, ready=None):
                for t, (a, a2) in enumerate(TERMS):
                    if a == LO and ready is not None:
                        pe.wait_ge(*ready)
                    for k in range(KC):
                        last = nc.tensor.matmul(
                            dst, stationary[:, a, k, :],
                            weights[:, bass.ds(e, 1), w, a2, k, :].rearrange("p e f -> p (e f)"),
                            start=(t == 0 and k == 0), stop=(t == len(TERMS) - 1 and k == KC - 1))
                return last

            def rows_in(n, u):
                i = 2 * n + u
                pe.wait_ge(gathered[u], 16 * (n + 1))
                need(pe, cx_lo, i)
                for k in range(KC):
                    last = nc.tensor.transpose(cx_bank[:, k * P:(k + 1) * P], xg[u][:, k * P:(k + 1) * P], ident[:, :])
                last.then_inc(cx_done, 1)

            def first_product(i, e):
                pe.wait_ge(experts_ready, e + 1)
                pe.wait_ge(cx_lo, i + 1)
                need(pe, u1_ready, i)
                expert_product(m1_bank, e, 0, xT).then_inc(m1_done, 1)

            def hidden_in(i):
                pe.wait_ge(n1_ready, i + 1)
                need(pe, relu_done, KC * i)
                for k in range(KC):
                    last = nc.tensor.transpose(ch_bank[:, k * P:(k + 1) * P], n1[:, k * P:(k + 1) * P], ident[:, :])
                last.then_inc(ch_done, 1)

            def second_product(i, e):
                pe.wait_ge(hh_ready, i + 1)
                need(pe, u2_ready, i)
                expert_product(m2_bank, e, 1, hTc, ready=(hl_ready, i + 1)).then_inc(m2_done, 1)

            def c_tile(n, u, experts, after):
                i = 2 * n + u
                hidden_in(i)
                if after >= 2:
                    first_product(i + 2, experts[3])
                if after >= 3:
                    rows_in(n + 1 + u, 1 - u)
                second_product(i, experts[1])

            pe.wait_ge(plan_ready, 2)
            pe.wait_ge(s_read, TPC * HPG * KC * NCH)
            rows_in(0, 0)
            first_product(0, expert_at(pe, 0))
            rows_in(0, 1)
            first_product(1, expert_at(pe, 1))
            rows_in(1, 0)
            tiles_of(pe, c_tile)

        @block.scalar
        def _(act):
            def hi_part(dst, src):
                return nc.scalar.activation(dst, src, ACT.Copy)

            for half_k in range(2):
                act.wait_ge(ctxT_done, half_k + 1)
                hi_part(ctxT[:, HI, 2 * half_k:2 * half_k + 2, :],
                        t_bank[half_k][:, 0:2 * B * SK].rearrange("p (k n) -> p k n", k=2)).then_inc(ctxT_hi, 1)
            for dst, src, loaded, count in ((wk, raw[3], wk_in, 16), (wv, raw[4], wv_in, 16)):
                act.wait_ge(loaded, count)
                hi_part(dst[:, HI], src).then_inc(w_hi, 1)
            act.wait_ge(pcol_ready, 1)
            act.wait_ge(kzero, 1)
            for m in range(KC):
                act.wait_ge(k_done, m + 1)
                for hl in range(HPG):
                    rows = slice(hl * DH, (hl + 1) * DH)
                    nc.scalar.activation(kblk[rows, HI, :, m, hl * SK:(hl + 1) * SK],
                                         z_bank[m % 2][rows, 0:B * SK].rearrange("p (b s) -> p b s", b=B),
                                         ACT.Identity, bias=pcol[rows, ROW_BK + m:ROW_BK + m + 1]).then_inc(k_hi, 1)
            for b in range(B):
                act.wait_ge(v_ready, b + 1)
                hi_part(v_r[0:SK, b, HI, :], v_rows[0:SK, b, :]).then_inc(v_hi, 1)
            for dst, src, loaded, count in ((wz, raw[0], wz_in, 64), (wh, raw[1], wh_in, 64), (wg, raw[2], wg_in, 16)):
                act.wait_ge(loaded, count)
                hi_part(dst[:, HI], src).then_inc(w_hi, 1)

            def x_hi(c):
                for k in range(KC):
                    act.wait_ge(a_t_done, t_group(c) + k + 1)
                    hi_part(xnT[:, HI, k, :], t_bank[k % 2]).then_inc(xnT_hi, 1)

            def h_hi(c, m):
                act.wait_ge(h_ready, 4 * c + m + 1)
                hi_part(hTr[:, HI, m, :], hT[:, m, :]).then_inc(hT_hi, 1)

            def a_chunk(c, last=False):
                for m in range(KC):
                    n = 4 * c + m
                    act.wait_ge(z_done, n + 1)
                    need(act, h_ready, n - 1)
                    nc.scalar.activation(za[:, m % 2, :], z_bank[m % 2], ACT.Sigmoid,
                                         bias=pcol[:, ROW_BZ + m:ROW_BZ + m + 1]).then_inc(z_ready, 1)
                    if m:
                        h_hi(c, m - 1)
                    act.wait_ge(split_in[m % 2], 16 * (2 * c + m // 2 + 1))
                    need(act, split_out, 16 * n)
                    hi_part(w_stage[:, HI], w_raw[:, m % 2]).then_inc(split_hi, 1)
                h_hi(c, KC - 1)
                if not last:
                    x_hi(c + 1)
                for m in range(KC):
                    n = 4 * c + m
                    act.wait_ge(g_done, n + 1)
                    need(act, gh_ready, n - 1)
                    nc.scalar.activation(gate[:, m % 2, :], g_bank[m % 2], ACT.Sigmoid,
                                         bias=pcol[:, ROW_BG + m:ROW_BG + m + 1]).then_inc(gate_ready, 1)

            x_hi(0)
            for dst, src, loaded, used, count in ((wq, raw[3], wk_in, k_done, KC), (wo, raw[4], wv_in, v_done, B)):
                act.wait_ge(loaded, 32)
                act.wait_ge(used, count)
                hi_part(dst[:, HI], src).then_inc(w_hi, 1)
            act.wait_ge(zero_out, 160)
            a_chunk(0)
            with act.Fori(1, NCH - 1) as c:
                a_chunk(c)
            a_chunk(NCH - 1, last=True)

            def x1_hi(c, ks):
                for k in ks:
                    act.wait_ge(b_t_done, t_num(c - 1, f"x{k}") + 1)
                    hi_part(x1T[:, HI, k, :], tb(c - 1, f"x{k}")).then_inc(x1T_hi, 1)

            def q_hi(c, m):
                act.wait_ge(mm_done, mm_num(c - 1, f"q{m}") + 1)
                nc.scalar.activation(qT[:, HI, m, :], mb(c - 1, f"q{m}"), ACT.Identity,
                                     bias=pcol[:, ROW_BQ + m:ROW_BQ + m + 1]).then_inc(qT_hi, 1)

            def exp_scores(c, m, tiles):
                for half_j in sorted({j // 2 for j in tiles if j % 2 == 0}):
                    act.wait_ge(shift_ready, 2 * (4 * c + m) + half_j + 1)
                if tiles[0] == 0:
                    need(act, p_rec, 4 * c + m - 1)
                    if m >= 2:
                        act.wait_ge(b_t_done, t_num(c, f"p{m - 2}{U - 1}") + 1)
                    elif not (isinstance(c, int) and c == 0):
                        act.wait_ge(b_t_done, t_num(c - 1, f"p{m + 2}{U - 1}") + 1)
                for j in tiles:
                    for hl in range(HPG):
                        keys, at = slice(hl * SK, (hl + 1) * SK), slice(HPG * j + hl, HPG * j + hl + 1)
                        nc.scalar.activation(pb[m % 2][:, j, keys], s_banks[:, j, keys], ACT.Exp,
                                             bias=nmax[:, m % 2, at], scale=float(DH) ** -0.5,
                                             accum_out=ssum[:, m % 2, at]).then_inc(s_read, 1)

            def pT_hi_part(c, m, parts):
                for u in parts:
                    n = min(UK, GK - u * UK)
                    act.wait_ge(b_t_done, t_num(c, f"p{m}{u}") + 1)
                    hi_part(pT[0:n, HI, u, :], tb(c, f"p{m}{u}")[0:n]).then_inc(pT_hi, 1)

            def out_hi(c, m, back=False):
                act.wait_ge(mm_done, mm_num(c, f"v{m}") + 1)
                if m == 0 and back:
                    act.wait_ge(mm_done, mm_num(c, "o3") + 1)
                hi_part(outT[:, HI, m, :], mb(c, f"v{m}")).then_inc(outT_hi, 1)

            def route_weights(c):
                act.wait_ge(route, NROUTE * c + ROUTE_SHIFTED)
                nc.scalar.activation(gexp[:, 0].rearrange("p j e -> p (j e)"), gexp[:, 0].rearrange("p j e -> p (j e)"),
                                     ACT.Exp).then_inc(route_exp, 1)

            def b_turn(c, back=True, back2=True, ahead=True):
                exp_scores(c, 1, (0,))
                pT_hi_part(c, 0, (0, 1))
                exp_scores(c, 1, (1,))
                exp_scores(c, 1, (2,))
                pT_hi_part(c, 0, (2,))
                if ahead:
                    x1_hi(c + 1, (0,))
                exp_scores(c, 1, (3,))
                if ahead:
                    x1_hi(c + 1, (1, 2))
                if back2:
                    route_weights(c - 2)
                if ahead:
                    x1_hi(c + 1, (3,))
                exp_scores(c, 2, (0,))
                pT_hi_part(c, 1, (0, 1))
                exp_scores(c, 2, (1,))
                exp_scores(c, 2, (2,))
                out_hi(c, 0, back)
                pT_hi_part(c, 1, (2,))
                exp_scores(c, 2, (3,))
                if ahead:
                    q_hi(c + 1, 0)
                out_hi(c, 1)
                exp_scores(c, 3, (0,))
                pT_hi_part(c, 2, (0, 1))
                exp_scores(c, 3, (1,))
                exp_scores(c, 3, (2,))
                if ahead:
                    q_hi(c + 1, 1)
                pT_hi_part(c, 2, (2,))
                exp_scores(c, 3, (3,))
                if ahead:
                    q_hi(c + 1, 2)
                out_hi(c, 2)
                if ahead:
                    exp_scores(c + 1, 0, (0,))
                pT_hi_part(c, 3, (0, 1))
                if ahead:
                    exp_scores(c + 1, 0, (1,))
                    exp_scores(c + 1, 0, (2,))
                    q_hi(c + 1, 3)
                pT_hi_part(c, 3, (2,))
                if ahead:
                    exp_scores(c + 1, 0, (3,))
                out_hi(c, 3)

            act.wait_ge(g_done, KC * NCH)
            hi_part(ident_r, ident[:, :]).then_inc(mask_ready, 1)
            act.wait_ge(kzero, 2)
            hi_part(mask_r[:, 0, :].rearrange("p (h s) -> p h s", h=HPG),
                    causal[:, :].unsqueeze(1).to_broadcast([P, HPG, SK])).then_inc(mask_ready, 1)
            x1_hi(0, range(KC))
            for m in range(KC):
                q_hi(0, m)
            for j in range(TPC):
                exp_scores(0, 0, (j,))
            b_turn(0, back=False, back2=False)
            b_turn(1, back2=False)
            with act.Fori(2, NCH - 1) as c:
                b_turn(c)
            b_turn(NCH - 1, ahead=False)
            route_weights(NCH - 2)
            route_weights(NCH - 1)

            def rows_hi(i):
                act.wait_ge(cx_done, i + 1)
                hi_part(xT[:, HI].rearrange("p k t -> p (k t)"), cx_bank).then_inc(cx_hi, 1)

            def hidden(i, e):
                act.wait_ge(ch_done, i + 1)
                need(act, hl_ready, i)
                for k in range(KC):
                    at = slice(k * P, (k + 1) * P)
                    nc.scalar.activation(hf[:, at], ch_bank[:, at], ACT.Relu,
                                         scale=pcol[:, bass.ds(e * KC + (ROW_G1 + k), 1)],
                                         bias=pcol[:, bass.ds(e * KC + (ROW_BE1 + k), 1)]).then_inc(relu_done, 1)
                need(act, m2_done, i)
                act.wait_ge(relu_done, KC * (i + 1))
                hi_part(hTc[:, HI].rearrange("p k t -> p (k t)"), hf).then_inc(hh_ready, 1)

            def weigh_rows(n, u):
                act.wait_ge(slots_in[u], 16 * (n + 1))
                need(act, added[u], 16 * n)
                act.wait_ge(z2_ready, 2 * n + u + 1)
                nc.scalar.activation(y2[u], z2, ACT.Copy, scale=tile_slots[:, bass.ds(2 * n + u, 1), 1].bitcast(F32)).then_inc(y2_ready, 1)

            def c_tile(n, u, experts, after):
                i = 2 * n + u
                hidden(i, experts[1])
                if not (isinstance(i, int) and i < 1):
                    weigh_rows(n if u else n - 1, 1 - u)
                if after >= 3:
                    rows_hi(i + 3)

            act.wait_ge(plan_ready, 2)
            for i in range(3):
                rows_hi(i)
            tiles_of(act, c_tile)
            weigh_rows((NSLOT - 1) // 2, (NSLOT - 1) % 2)

        @block.vector
        def _(dve):
            V = nc.vector

            def lo_part(dst, src, hi):
                return V.tensor_tensor(dst, src, hi.bitcast(F32), ALU.subtract)

            V.memset(zeros_r[:, :].bitcast(F32), 0.0)
            V.memset(carry[:, :, :], 0.0)
            V.memset(kblk[:, :, :, :, :].rearrange("p a b m g -> p (a b m g)").bitcast(F32), 0.0).then_inc(kzero, 1)
            dve.wait_ge(ptr_done, 1)
            V.tensor_copy(pcol[:, :], g_bank[0][:, 0:NROWS]).then_inc(pcol_ready, 1)
            for half_k in range(2):
                dve.wait_ge(ctxT_hi, half_k + 1)
                lo_part(ctxT[:, LO, 2 * half_k:2 * half_k + 2, :],
                        t_bank[half_k][:, 0:2 * B * SK].rearrange("p (k n) -> p k n", k=2),
                        ctxT[:, HI, 2 * half_k:2 * half_k + 2, :]).then_inc(ctxT_lo, 1)
            for i, (dst, src) in enumerate(((wk, raw[3]), (wv, raw[4]))):
                dve.wait_ge(w_hi, i + 1)
                lo_part(dst[:, LO], src, dst[:, HI]).then_inc(w_lo, 1)
            dve.wait_ge(pcol_ready, 1)
            for m in range(KC):
                for hl in range(HPG):
                    dve.wait_ge(k_hi, HPG * m + hl + 1)
                    rows = slice(hl * DH, (hl + 1) * DH)
                    keys = slice(hl * SK, (hl + 1) * SK)
                    V.scalar_tensor_tensor(kblk[rows, LO, :, m, keys],
                                           z_bank[m % 2][rows, 0:B * SK].rearrange("p (b s) -> p b s", b=B),
                                           pcol[rows, ROW_BK + m:ROW_BK + m + 1],
                                           kblk[rows, HI, :, m, keys].bitcast(F32),
                                           ALU.add, ALU.subtract).then_inc(k_lo, 1)
            dve.wait_ge(bv_in, 16)
            for b in range(B):
                dve.wait_ge(v_done, b + 1)
                V.tensor_tensor(v_rows[0:SK, b, :], h_bank[b][0:SK, :], bv_rows[0:SK], ALU.add).then_inc(v_ready, 1)
            for b in range(B):
                dve.wait_ge(v_hi, b + 1)
                lo_part(v_r[0:SK, b, LO, :], v_rows[0:SK, b, :], v_r[0:SK, b, HI, :]).then_inc(v_lo, 1)

            def xr(c, j):
                return ring[:, c % 3, j] if isinstance(c, int) else ring[:, bass.ds(c % 3, 1), j].rearrange(
                    "p r f -> p (r f)")

            def ln1_stats(c):
                need(dve, xn_ready, 4 * c)
                need_alone(dve, x_in, 16 * (c + 1), dve_passed)
                for j in range(TPC):
                    V.bn_stats(st1[:, j, :], xr(c, j)).then_inc(ln1_stat, 1)
                need_alone(dve, ln1_stat, 4 * (c + 1), dve_passed)
                for j in range(TPC):
                    V.bn_aggr(mv1[:, j, :], st1[:, j, :]).then_inc(ln1_aggr, 1)
                dve.wait_ge(ln1_aggr, 4 * (c + 1))
                need(dve, ln1_rstd, c)
                V.tensor_scalar_add(ve1[:, :], mv1[:, :, 1], EPS).then_inc(ln1_eps, 1)

            def ln1_apply(c):
                dve.wait_ge(ln1_rstd, c + 1)
                need(dve, a_t_done, t_group(c - 1) + 4 if not (isinstance(c, int) and c == 0) else 0)
                for j in range(TPC):
                    V.tensor_scalar(xn[:, j, :], xr(c, j), mv1[:, j, 0:1], rs1[:, j:j + 1],
                                    ALU.subtract, ALU.mult).then_inc(xn_ready, 1)

            def x_lo(c):
                for k in range(KC):
                    dve.wait_ge(xnT_hi, 4 * c + k + 1)
                    lo_part(xnT[:, LO, k, :], t_bank[k % 2], xnT[:, HI, k, :]).then_inc(a_t_read, 1)

            def h_lo(c, m):
                dve.wait_ge(hT_hi, 4 * c + m + 1)
                lo_part(hTr[:, LO, m, :], hT[:, m, :], hTr[:, HI, m, :]).then_inc(hT_lo, 1)

            def carry_at(c, m, n):
                at = c + c // CPB + n
                return carry[:, m, at:at + 1] if isinstance(at, int) else carry[:, m, bass.ds(at, 1)]

            def recurrence(c, m):
                n = 4 * c + m
                dve.wait_ge(z_ready, n + 1)
                dve.wait_ge(h_done, n + 1)
                need(dve, h_ready, n - 1)
                V.scalar_tensor_tensor(zb[:, m % 2, :], h_bank[m % 2], pcol[:, ROW_BH + m:ROW_BH + m + 1],
                                       za[:, m % 2, :], ALU.add, ALU.mult).then_inc(b_ready, 1)
                dve.wait_ge(b_ready, n + 1)
                V.tensor_scalar(za[:, m % 2, :], za[:, m % 2, :], -1.0, 1.0, ALU.mult, ALU.add).then_inc(a_ready, 1)
                dve.wait_ge(a_ready, n + 1)
                need(dve, carry_ready, n - 3)
                V.tensor_tensor_scan(hT[:, m, :], za[:, m % 2, :], zb[:, m % 2, :], carry_at(c, m, 0),
                                     ALU.mult, ALU.add).then_inc(h_ready, 1)
                dve.wait_ge(h_ready, n + 1)
                V.tensor_copy(carry_at(c, m, 1), hT[:, m, CH - 1:CH]).then_inc(carry_ready, 1)

            def split_piece_lo(c, m):
                dve.wait_ge(split_hi, 4 * c + m + 1)
                lo_part(w_stage[:, LO], w_raw[:, m % 2], w_stage[:, HI]).then_inc(split_lo, 1)

            def x1_rows(c, j):
                g = tg_group(c) + j
                dve.wait_ge(a_t_done, g + 1)
                V.tensor_tensor(xr(c, j), t_bank[j % 2], xr(c, j), ALU.add).then_inc(a_t_read, 1)
                need_alone(dve, a_t_read, g + 1, dve_passed)
                V.bn_stats(st2[:, j, :], xr(c, j)).then_inc(ln2_stat, 1)

            def ln2_means(c):
                need_alone(dve, ln2_stat, 4 * (c + 1), dve_passed)
                for j in range(TPC):
                    V.bn_aggr(mv2[:, j, :], st2[:, j, :]).then_inc(ln2_aggr, 1)
                dve.wait_ge(ln2_aggr, 4 * (c + 1))
                t = bass.ds(4 * c, 4)
                V.tensor_copy(mean2[:, t], mv2[:, :, 0])
                V.tensor_scalar_add(ve2[:, t], mv2[:, :, 1], EPS).then_inc(ln2_eps, 1)

            def a_chunk(c, first=False, last=False):
                for m in range(KC):
                    recurrence(c, m)
                    if m:
                        h_lo(c, m - 1)
                    split_piece_lo(c, m)
                    if m == 0 and not last:
                        ln1_stats(c + 1)
                    if m == 1 and not last:
                        ln1_apply(c + 1)
                    if not first:
                        x1_rows(c - 1, m)
                h_lo(c, KC - 1)
                if not last:
                    x_lo(c + 1)
                if not first:
                    ln2_means(c - 1)
                for m in range(KC):
                    dve.wait_ge(gate_ready, 4 * c + m + 1)
                    V.tensor_tensor(ghT[:, m, :], gate[:, m % 2, :], hT[:, m, :], ALU.mult).then_inc(gh_ready, 1)

            dve.wait_ge(consts_done, 1)
            V.memset(tab0[:, :, 1], 0)
            V.tensor_copy(tok[:, :], tok_i[:, :]).then_inc(tok_ready, 1)
            V.memset(counts[:, 0, :], 0.0)
            V.tensor_scalar(tab0[:, :, 0], tab0[:, :, 0], P - 1, T, ALU.bitwise_and,
                            ALU.bitwise_or).then_inc(prefill_ready, 1)
            ln1_stats(0)
            for i, (dst, src) in enumerate(((wz, raw[0]), (wh, raw[1]), (wg, raw[2]))):
                dve.wait_ge(w_hi, i + 3)
                lo_part(dst[:, LO], src, dst[:, HI]).then_inc(w_lo, 1)
            dve.wait_ge(w_lo, 5)
            dve.wait_ge(vb_out, 16 * 2 * B * HPG)
            ln1_apply(0)
            x_lo(0)
            for i, (dst, src) in enumerate(((wq, raw[3]), (wo, raw[4]))):
                dve.wait_ge(w_hi, i + 6)
                lo_part(dst[:, LO], src, dst[:, HI]).then_inc(w_lo, 1)
            a_chunk(0, first=True)
            with dve.Fori(1, NCH - 1) as c:
                a_chunk(c)
            a_chunk(NCH - 1, last=True)
            for j in range(TPC):
                x1_rows(NCH - 1, j)
            ln2_means(NCH - 1)

            def x1_rows_n(c):
                dve.wait_ge(x1_in, 16 * (c + 1))
                dve.wait_ge(ln2_rstd, c + 1)
                if not (isinstance(c, int) and c == 0):
                    dve.wait_ge(b_t_done, t_num(c - 2, "x3") + 1)
                for j in range(TPC):
                    t = 4 * c + j
                    V.tensor_scalar(x1n[:, j, :], slot3(c)[:, j, :], mean2[:, bass.ds(t, 1)], rs2[:, bass.ds(t, 1)],
                                    ALU.subtract, ALU.mult).then_inc(x1n_ready, 1)

            def x1_lo(c, ks):
                for k in ks:
                    dve.wait_ge(x1T_hi, 4 * c + k + 1)
                    lo_part(x1T[:, LO, k, :], tb(c - 1, f"x{k}"), x1T[:, HI, k, :]).then_inc(b_t_read, 1)

            def q_lo(c, m):
                dve.wait_ge(qT_hi, 4 * c + m + 1)
                V.scalar_tensor_tensor(qT[:, LO, m, :], mb(c - 1, f"q{m}"), pcol[:, ROW_BQ + m:ROW_BQ + m + 1],
                                       qT[:, HI, m, :].bitcast(F32), ALU.add, ALU.subtract).then_inc(mm_read, 1)

            def max_scores(c, m, i):
                n = 4 * c + m
                pair, heads = slice(2 * i, 2 * i + 2), slice(2 * HPG * i, 2 * HPG * (i + 1))
                dve.wait_ge(s_done, 2 * n + i + 1)
                V.tensor_reduce(smax[:, heads].rearrange("p (j h) -> p j h", j=2),
                                s_banks[:, pair, :].rearrange("p j (h s) -> p j h s", h=HPG), AX.X,
                                ALU.max).then_inc(smax_ready, 1)
                dve.wait_ge(smax_ready, 2 * n + i + 1)
                need(dve, s_read, TPC * HPG * (n - 1))
                V.tensor_scalar(nmax[:, m % 2, heads], smax[:, heads], -float(DH) ** -0.5, None,
                                ALU.mult).then_inc(shift_ready, 1)

            def invert_sums(c, m):
                n = 4 * c + m
                dve.wait_ge(s_read, TPC * HPG * (n + 1))
                need(dve, p_ready, n - 1)
                V.reciprocal(srec[:, m % 2, :], ssum[:, m % 2, :]).then_inc(p_rec, 1)

            def pT_lo_part(c, m, parts):
                for u in parts:
                    n = min(UK, GK - u * UK)
                    dve.wait_ge(pT_hi, 12 * c + U * m + u + 1)
                    lo_part(pT[0:n, LO, u, :], tb(c, f"p{m}{u}")[0:n], pT[0:n, HI, u, :]).then_inc(b_t_read, 1)

            def out_lo(c, m):
                dve.wait_ge(outT_hi, 4 * c + m + 1)
                lo_part(outT[:, LO, m, :], mb(c, f"v{m}"), outT[:, HI, m, :]).then_inc(mm_read, 1)

            def x2_rows(c, at, j):
                t = 4 * c + j
                dve.wait_ge(mm_done, mm_num(at, f"o{j}") + 1)
                dve.wait_ge(x1b_ready, t + 1)
                V.tensor_tensor(slot3(c)[:, j, :], mb(at, f"o{j}"), slot3(c)[:, j, :], ALU.add).then_inc(mm_read, 1)
                need_alone(dve, mm_read, mm_num(at, f"o{j}") + 1, dve_passed)
                V.bn_stats(st3[:, j, :], slot3(c)[:, j, :]).then_inc(ln3_stat, 1)

            def ln3_pair(c, i):
                need_alone(dve, ln3_stat, 4 * c + 2 * i + 2, dve_passed)
                need_alone(dve, xf_ready, 4 * (c - 1) + 2 * i + 2, dve_passed)
                for j in (2 * i, 2 * i + 1):
                    V.bn_aggr(mv3[:, j, :], st3[:, j, :]).then_inc(ln3_aggr, 1)
                dve.wait_ge(ln3_aggr, 4 * c + 2 * i + 2)
                V.tensor_scalar_add(ve3[:, 2 * i:2 * i + 2], mv3[:, 2 * i:2 * i + 2, 1], EPS).then_inc(ln3_eps, 1)

            def ln3_apply(c, at, j):
                dve.wait_ge(ln3_rstd, 2 * c + j // 2 + 1)
                need(dve, xf_out[j], 16 * c)
                need(dve, base_ready, 4 * (c - 1) + j + 1)
                if not (isinstance(at, int) and at == 1):
                    dve.wait_ge(b_t_done, t_num(at - 1, f"xf{j}") + 1)
                V.tensor_scalar(xf[:, j, :], slot3(c)[:, j, :], mv3[:, j, 0:1], rs3[:, j:j + 1],
                                ALU.subtract, ALU.mult).then_inc(xf_ready, 1)

            def xf_features(c, at, j):
                dve.wait_ge(b_t_done, t_num(at, f"xf{j}") + 1)
                V.tensor_copy(xfT[:, j].rearrange("p k t -> p (k t)"), tb(at, f"xf{j}")).then_inc(b_t_read, 1)

            def gate_bias(at):
                dve.wait_ge(mm_done, mm_num(at, "g") + 1)
                V.tensor_tensor(gs[:, :, :], mb(at, "g")[:, 0:TPC * NE].rearrange("p (j e) -> p j e", j=TPC),
                                gate_b[:, :].unsqueeze(1).to_broadcast([P, TPC, NE]), ALU.add).then_inc(mm_read, 1)

            class Steps:

                def __init__(self, c, n=0):
                    self.front, self.n = NROUTE * c, n

                def __call__(self, instruction):
                    self.n += 1
                    instruction.then_inc(route, 1)
                    dve.wait_ge(route, self.front + self.n)

            def choose(c, at):
                step = Steps(c)
                dve.wait_ge(mm_read, mm_num(at, "g") + 1)
                other = gs[:, :, :].unsqueeze(2).to_broadcast([P, TPC, NE, NE])
                own = gs[:, :, :].unsqueeze(3).to_broadcast([P, TPC, NE, NE])
                step(V.tensor_tensor(gcmp[:, 0], other, own, ALU.is_gt))
                step(V.tensor_tensor(gcmp[:, 1], other, own, ALU.is_equal))
                step(V.tensor_tensor(gcmp[:, 1], gcmp[:, 1], tie[:, :, :].unsqueeze(1).to_broadcast([P, TPC, NE, NE]),
                                     ALU.mult))
                step(V.tensor_tensor(gcmp[:, 0], gcmp[:, 0], gcmp[:, 1], ALU.add))
                step(V.tensor_reduce(rank[:, :, :], gcmp[:, 0], AX.X, ALU.add))
                step(V.tensor_scalar(sel[:, :, :], rank[:, :, :], 2.0, None, ALU.is_lt))
                assert step.n == ROUTE_CHOSEN

            def count(c):
                step = Steps(c, ROUTE_CHOSEN)
                for j in range(TPC):
                    step(V.tensor_tensor(counts[:, j + 1, :], counts[:, j, :], sel[:, j, :], ALU.add))
                assert step.n == ROUTE_COUNTED
                step(V.tensor_reduce(gmax[:, :], gs[:, :, :], AX.X, ALU.max))
                step(V.tensor_tensor(gexp[:, 0], gs[:, :, :], gmax[:, :].unsqueeze(2).to_broadcast([P, TPC, NE]),
                                     ALU.subtract))
                assert step.n == ROUTE_SHIFTED

            def read_positions(at, name="r", totals=False):
                dve.wait_ge(mm_done, mm_num(at, name) + 1)
                if totals:
                    V.tensor_copy(total[:, :], mb(at, name)[:, TPC * NE:(TPC + 1) * NE])
                V.tensor_tensor(pos[:, :, :], mb(at, name)[:, 0:TPC * NE].rearrange("p (j e) -> p j e", j=TPC),
                                region0[:, :].unsqueeze(1).to_broadcast([P, TPC, NE]), ALU.add).then_inc(mm_read, 1)

            def weigh(c):
                step = Steps(c, ROUTE_SHIFTED)
                for k in range(2):
                    step(V.tensor_scalar(is_k[:, k], rank[:, :, :], float(k), None, ALU.is_equal))
                dve.wait_ge(route_exp, c + 1)
                step(V.tensor_tensor(gexp[:, 1], gexp[:, 0], sel[:, :, :], ALU.mult))
                step(V.tensor_reduce(grec[:, 0, :], gexp[:, 1], AX.X, ALU.add))
                step(V.reciprocal(grec[:, 1, :], grec[:, 0, :]))
                step(V.tensor_tensor(gexp[:, 1], gexp[:, 1], grec[:, 1, :].unsqueeze(2).to_broadcast([P, TPC, NE]),
                                     ALU.mult))
                for k in range(2):
                    step(V.tensor_tensor(kth[:, k], is_k[:, k], gexp[:, 1], ALU.mult))
                step(V.tensor_reduce(kval[:, 0], kth[:, :, :, :], AX.X, ALU.add))
                assert step.n == ROUTE_WEIGHED

            def slots(c, at, name="r"):
                step = Steps(c, ROUTE_WEIGHED)
                dve.wait_ge(mm_read, mm_num(at, name) + 1)
                for k in range(2):
                    step(V.tensor_tensor(kth[:, k], is_k[:, k], pos[:, :, :], ALU.mult))
                step(V.tensor_reduce(kval[:, 1], kth[:, :, :, :], AX.X, ALU.add))
                need(dve, scattered, 16 * 2 * TPC * c)
                for k in range(2):
                    step(V.tensor_copy(payload[:, :, k, 0], tok[:, :]))
                    step(V.tensor_copy(payload[:, :, k, 1].bitcast(F32), kval[:, 0, k, :]))
                step(V.tensor_copy(slot_ix[:, :, :], kval[:, 1, :, :]))
                step(V.tensor_copy(counts[:, 0, :], counts[:, TPC, :]))
                step(V.tensor_scalar_add(tok[:, :], tok[:, :], float(CH)))
                assert step.n == NROUTE

            class Plan:
                n = 0

                def __call__(self, instruction):
                    self.n += 1
                    instruction.then_inc(plan, 1)
                    dve.wait_ge(plan, self.n)

            plan_step = Plan()

            def expert_tiles(add):
                plan_step(V.tensor_scalar(total_i[:, :], total[:, :], float(add), None, ALU.add))
                plan_step(V.tensor_scalar(total_i[:, :], total_i[:, :], P.bit_length() - 1, None, ALU.arith_shift_right))
                plan_step(V.tensor_copy(tiles[:, :], total_i[:, :]))

            def first_tiles():
                plan_step(V.memset(first[:, 0:1], 0.0))
                for e in range(1, NE):
                    plan_step(V.tensor_tensor(first[:, e:e + 1], first[:, e - 1:e], tiles[:, e - 1:e], ALU.add))

            def plan_tiles(at, count, skipped):
                number, experts, rows = tile_no[:, 0:count], tile_e[:, 0:count], tile_row[:, 0:count]
                first_tiles()
                plan_step(V.tensor_scalar(jump[:, :], tiles[:, :], -float(P), float(REG), ALU.mult, ALU.add))
                plan_step(V.tensor_scalar(rows, number, float(P), None, ALU.mult))
                if skipped is not None:
                    plan_step(V.scalar_tensor_tensor(jump[:, 0:NE - 1], skipped[:, 1:NE], float(P), jump[:, 0:NE - 1],
                                                     ALU.mult, ALU.add))
                    plan_step(V.scalar_tensor_tensor(jump[:, 0:NE - 1], skipped[:, 0:NE - 1], -float(P),
                                                     jump[:, 0:NE - 1], ALU.mult, ALU.add))
                    plan_step(V.tensor_scalar(total[:, 0:1], skipped[:, 0:1], float(P), None, ALU.mult))
                    plan_step(V.tensor_scalar(rows, rows, total[:, 0:1], None, ALU.add))
                for e in range(1, NE):
                    plan_step(V.tensor_scalar(tile_ge[:, e - 1, 0:count], number, first[:, e:e + 1], None, ALU.is_ge))
                    plan_step(V.scalar_tensor_tensor(rows, tile_ge[:, e - 1, 0:count], jump[:, e - 1:e], rows,
                                                     ALU.mult, ALU.add))
                plan_step(V.tensor_tensor(experts, tile_ge[:, 0, 0:count], tile_ge[:, 1, 0:count], ALU.add))
                plan_step(V.tensor_tensor(experts, experts, tile_ge[:, 2, 0:count], ALU.add))
                plan_step(V.tensor_copy(plan_e[:, at:at + count], experts))
                plan_step(V.tensor_copy(plan_row[:, at:at + count], rows))

            def plan_early():
                plan_step(V.tensor_copy(tile_no[:, :], tile_int[:, :]))
                expert_tiles(0)
                plan_tiles(0, EARLY, None)
                plan_step(V.tensor_scalar(taken[:, :], first[:, :], -1.0, float(EARLY), ALU.mult, ALU.add))
                plan_step(V.tensor_scalar(taken[:, :], taken[:, :], 0.0, None, ALU.max))
                plan_step(V.tensor_tensor(taken[:, :], taken[:, :], tiles[:, :], ALU.min))
                dve.sem_inc(plan_ready, 1)

            def plan_late():
                expert_tiles(P - 1)
                plan_step(V.tensor_tensor(tiles[:, :], tiles[:, :], taken[:, :], ALU.subtract))
                plan_tiles(EARLY, NSLOT - EARLY, taken)
                pairs = plan_pair[:, 1:(NSLOT - 5) // 2]
                behind = NSLOT - 7
                plan_step(V.tensor_copy(pairs, plan_e[:, 1:behind:2]))
                for k in range(1, 5):
                    plan_step(V.scalar_tensor_tensor(pairs, plan_e[:, 1 + k:behind + k:2], float(NE ** k), pairs,
                                                     ALU.mult, ALU.add))
                dve.sem_inc(plan_ready, 1)

            def b_turn(c, back=True, back2=True, ahead=True):
                max_scores(c, 1, 1)
                pT_lo_part(c, 0, (0, 1))
                if back2:
                    count(c - 2)
                if ahead:
                    x1_rows_n(c + 1)
                if back:
                    x2_rows(c - 1, c, 0)
                pT_lo_part(c, 0, (2,))
                if ahead:
                    x1_lo(c + 1, (0,))
                if back:
                    x2_rows(c - 1, c, 1)
                if ahead:
                    x1_lo(c + 1, (1, 2))
                if back:
                    ln3_pair(c - 1, 0)
                if back2:
                    read_positions(c, totals=not ahead)
                invert_sums(c, 1)
                if back:
                    x2_rows(c - 1, c, 2)
                if ahead:
                    x1_lo(c + 1, (3,))
                max_scores(c, 2, 0)
                if back:
                    ln3_apply(c - 1, c, 0)
                    ln3_apply(c - 1, c, 1)

                max_scores(c, 2, 1)
                pT_lo_part(c, 1, (0, 1))
                out_lo(c, 0)
                if back:
                    x2_rows(c - 1, c, 3)
                pT_lo_part(c, 1, (2,))
                if back:
                    xf_features(c - 1, c, 0)
                    ln3_pair(c - 1, 1)
                if ahead:
                    q_lo(c + 1, 0)
                invert_sums(c, 2)
                if back:
                    xf_features(c - 1, c, 1)
                max_scores(c, 3, 0)
                out_lo(c, 1)

                max_scores(c, 3, 1)
                pT_lo_part(c, 2, (0, 1))
                if back:
                    ln3_apply(c - 1, c, 2)
                    ln3_apply(c - 1, c, 3)
                if ahead:
                    q_lo(c + 1, 1)
                pT_lo_part(c, 2, (2,))
                if back:
                    xf_features(c - 1, c, 2)
                if not ahead:
                    plan_early()
                if back2:
                    weigh(c - 2)
                if ahead:
                    q_lo(c + 1, 2)
                invert_sums(c, 3)
                if back:
                    xf_features(c - 1, c, 3)
                if ahead:
                    max_scores(c + 1, 0, 0)
                out_lo(c, 2)

                if ahead:
                    max_scores(c + 1, 0, 1)
                pT_lo_part(c, 3, (0, 1))
                if back2:
                    slots(c - 2, c)
                if ahead:
                    q_lo(c + 1, 3)
                pT_lo_part(c, 3, (2,))
                if ahead:
                    invert_sums(c + 1, 0)
                if back:
                    gate_bias(c)
                    choose(c - 1, c)
                if ahead:
                    max_scores(c + 1, 1, 0)
                out_lo(c, 3)

            dve.wait_ge(g_done, KC * NCH)
            V.memset(mask_r[:, 1:CPB, :].rearrange("p s g -> p (s g)").bitcast(F32), 0.0).then_inc(kzero, 1)
            dve.wait_ge(tok_ready, 1)
            x1_rows_n(0)
            x1_lo(0, range(KC))
            for m in range(KC):
                q_lo(0, m)
            max_scores(0, 0, 0)
            max_scores(0, 0, 1)
            max_scores(0, 1, 0)
            invert_sums(0, 0)
            dve.wait_ge(gw_in, 32)
            b_turn(0, back=False, back2=False)
            b_turn(1, back2=False)
            b_turn(2)
            with dve.Fori(3, NCH - 1) as c:
                b_turn(c)
            b_turn(NCH - 1, ahead=False)
            last, tail = NCH - 1, NCH
            count(last - 1)
            for j in range(TPC):
                x2_rows(last, tail, j)
                if j % 2:
                    ln3_pair(last, j // 2)
                if j == 1:
                    read_positions(tail)
            weigh(last - 1)
            for j in range(TPC):
                ln3_apply(last, tail, j)
            slots(last - 1, tail)
            for j in range(TPC):
                xf_features(last, tail, j)
            gate_bias(tail)
            choose(last, tail)
            count(last)
            read_positions(tail, "t", totals=True)
            weigh(last)
            slots(last, tail, "t")
            plan_late()

            def row_of(rows, e):
                return rows[:, bass.ds(e, 1), :].rearrange("p e f -> p (e f)")

            def rows_lo(i):
                dve.wait_ge(cx_hi, i + 1)
                lo_part(xT[:, LO].rearrange("p k t -> p (k t)"), cx_bank, xT[:, HI].rearrange("p k t -> p (k t)")).then_inc(
                    cx_lo, 1)

            def statistics(i, which, src, ready, stat, aggr, eps):
                need_alone(dve, ready, i + 1, dve_passed)
                V.bn_stats(c_st[:, which, :], src).then_inc(stat, 1)
                need_alone(dve, stat, i + 1, dve_passed)
                V.bn_aggr(c_mv[:, which, :], c_st[:, which, :]).then_inc(aggr, 1)
                dve.wait_ge(aggr, i + 1)
                V.tensor_scalar_add(c_ve[:, which:which + 1], c_mv[:, which, 1:2], EPS).then_inc(eps, 1)

            def hidden_rows(i, e):
                need(dve, n1_ready, i)
                dve.wait_ge(m1_done, i + 1)
                V.tensor_tensor(u1, m1_bank, row_of(b1_rows, e), ALU.add).then_inc(u1_ready, 1)

            def hidden_norm(i):
                dve.wait_ge(c1_rstd, i + 1)
                need(dve, ch_done, i)
                V.tensor_scalar(n1, u1, c_mv[:, 0, 0:1], c_rs[:, 0:1], ALU.subtract, ALU.mult).then_inc(n1_ready, 1)

            def out_rows(n, u, e):
                dve.wait_ge(m2_done, 2 * n + u + 1)
                V.tensor_tensor(u2[u], m2_bank, row_of(b2_rows, e), ALU.add).then_inc(u2_ready, 1)

            def out_scale(n, u, e):
                need(dve, z2_ready, 2 * n + u)
                V.scalar_tensor_tensor(v2, u2[u], c_mv[:, 1, 0:1], row_of(g2_rows, e), ALU.subtract,
                                       ALU.mult).then_inc(v2_ready, 1)

            def out_norm(i, e):
                dve.wait_ge(c2_rstd, i + 1)
                dve.wait_ge(v2_ready, i + 1)
                need(dve, y2_ready, i)
                V.scalar_tensor_tensor(z2, v2, c_rs[:, 1:2], row_of(be2_rows, e), ALU.mult,
                                       ALU.add).then_inc(z2_ready, 1)

            def c_tile(n, u, experts, after):
                i = 2 * n + u
                last = (n if u else n - 1), 1 - u
                first = isinstance(i, int) and i == 0
                if not first:
                    out_rows(*last, experts[0])
                    statistics(i - 1, 1, u2[1 - u], u2_ready, c2_stat, c2_aggr, c2_eps)
                if after >= 1:
                    hidden_norm(i + 1)
                if not first:
                    out_scale(*last, experts[0])
                    out_norm(i - 1, experts[0])
                if after >= 2:
                    hidden_rows(i + 2, experts[3])
                    statistics(i + 2, 0, u1, u1_ready, c1_stat, c1_aggr, c1_eps)
                if after >= 3:
                    rows_lo(i + 3)

            dve.wait_ge(plan_ready, 2)
            dve.wait_ge(p1_in, 16 * 4)
            for j in range(TPC):
                dve.wait_ge(xf_out[j], 16 * NCH)
            dve.wait_ge(base_ready, NT)
            for i in range(2):
                rows_lo(i)
                hidden_rows(i, expert_at(dve, i))
                statistics(i, 0, u1, u1_ready, c1_stat, c1_aggr, c1_eps)
                if i == 0:
                    hidden_norm(i)
            rows_lo(2)
            tiles_of(dve, c_tile)
            i = NSLOT - 1
            e = expert_at(dve, i)
            out_rows(i // 2, i % 2, e)
            statistics(i, 1, u2[i % 2], u2_ready, c2_stat, c2_aggr, c2_eps)
            out_scale(i // 2, i % 2, e)
            out_norm(i, e)

        @block.gpsimd
        def _(pool):
            G = nc.gpsimd
            G.memset(half[:, :], -0.5)
            G.memset(causal[:, :], 0.0)
            G.memset(before[:, :], 1.0)
            G.memset(ones[:, :], 1.0)
            G.memset(tie[:, :, :], 0.0)
            for e in range(NE):
                G.memset(region0[:, e:e + 1], float(e * REG))
            G.iota(tok_i[:, :], pattern=[[P, TPC]], base=0, channel_multiplier=1)
            G.iota(tile_int[:, :], pattern=[[1, EARLY]], base=0, channel_multiplier=0)
            G.iota(tab0[:, :, 0], pattern=[[1, TABW]], base=0, channel_multiplier=TABW)
            G.memset(ident[:, :], 0.0).then_inc(pool_step, 1)
            pool.wait_ge(pool_step, 1)
            G.affine_select(out=ident[:, :], in_=ident[:, :], compare_op=ALU.not_equal, fill=1.0, base=0,
                            pattern=[[-1, P]], channel_multiplier=1).then_inc(const_ready, 1)
            for e in range(1, NE):
                G.memset(tie[:, e, 0:e], 1.0)
            G.affine_select(out=causal[:, :], in_=causal[:, :], compare_op=ALU.is_ge, fill=NEG, base=0,
                            pattern=[[-1, SK]], channel_multiplier=1)
            G.affine_select(out=before[:, :], in_=before[:, :], compare_op=ALU.is_gt, fill=0.0, base=0,
                            pattern=[[1, P]], channel_multiplier=-1).then_inc(consts_done, 1)

            def a_chunk(c, first=False, last=False):
                if not last:
                    pool.wait_ge(ln1_eps, c + 2)
                    pool.wait_ge(xn_ready, 4 * c + 4)
                    G.tensor_tensor(rs1[:, :], ve1[:, :], half[:, 0:TPC], ALU.pow).then_inc(ln1_rstd, 1)
                if not first:
                    t = bass.ds(4 * (c - 1), 4)
                    pool.wait_ge(ln2_eps, c)
                    G.tensor_tensor(rs2[:, t], ve2[:, t], half[:, 0:TPC], ALU.pow).then_inc(ln2_rstd, 1)

            pool.wait_ge(ln1_eps, 1)
            G.tensor_tensor(rs1[:, :], ve1[:, :], half[:, 0:TPC], ALU.pow).then_inc(ln1_rstd, 1)
            a_chunk(0, first=True)
            with pool.Fori(1, NCH - 1) as c:
                a_chunk(c)
            a_chunk(NCH - 1, last=True)
            pool.wait_ge(ln2_eps, NCH)
            t = bass.ds(4 * (NCH - 1), 4)
            G.tensor_tensor(rs2[:, t], ve2[:, t], half[:, 0:TPC], ALU.pow).then_inc(ln2_rstd, 1)

            def add_bo(c):
                for j in range(TPC):
                    need_alone(pool, x1n_ready, 4 * c + j + 1, pool_passed)
                    G.tensor_tensor(slot3(c)[:, j, :], slot3(c)[:, j, :], bo_rows, ALU.add).then_inc(x1b_ready, 1)

            def normalise(c, m):
                pool.wait_ge(p_rec, 4 * c + m + 1)
                p3 = pb[m % 2].rearrange("p j (h s) -> p (j h) s", h=HPG)
                G.tensor_tensor(p3, p3, srec[:, m % 2, :].unsqueeze(2).to_broadcast([P, TPC * HPG, SK]),
                                ALU.mult).then_inc(p_ready, 1)

            def ln3_pow(c, i):
                pool.wait_ge(ln3_eps, 2 * c + i + 1)
                need(pool, xf_ready, 4 * (c - 1) + 2 * i + 2)
                pair = slice(2 * i, 2 * i + 2)
                G.tensor_tensor(rs3[:, pair], ve3[:, pair], half[:, 0:2], ALU.pow).then_inc(ln3_rstd, 1)

            def base_row(c, j):
                t = 4 * c + j
                need(pool, base_out[j % 2], 16 * (2 * c + j // 2))
                need_alone(pool, xf_ready, t + 1, pool_passed)
                G.tensor_tensor(base[:, j % 2, :], slot3(c)[:, j, :], xf[:, j, :], ALU.add).then_inc(base_ready, 1)

            def scatter(c, j):
                need_alone(pool, route, NROUTE * (c + 1), pool_passed)
                for k in range(2):
                    G.indirect_dma_start(slots_d, bass.IndirectOffsetOnAxis(slot_ix[:, k, j:j + 1], 0),
                                         payload[:, j, k, :], None).then_inc(scattered, 16)

            def b_turn(c, back=True, back2=True, ahead=True):
                normalise(c, 0)
                if back:
                    ln3_pow(c - 1, 0)
                normalise(c, 1)
                if back:
                    ln3_pow(c - 1, 1)
                    base_row(c - 1, 0)
                    base_row(c - 1, 1)
                normalise(c, 2)
                if ahead:
                    add_bo(c + 1)
                if back:
                    base_row(c - 1, 2)
                    base_row(c - 1, 3)
                normalise(c, 3)
                if back2:
                    for j in range(TPC):
                        scatter(c - 2, j)

            pool.wait_ge(bo_in, 16)
            add_bo(0)
            pool.wait_ge(prefill_out, 16)
            b_turn(0, back=False, back2=False)
            b_turn(1, back2=False)
            with pool.Fori(2, NCH - 1) as c:
                b_turn(c)
            b_turn(NCH - 1, ahead=False)
            for i in range(2):
                ln3_pow(NCH - 1, i)
            for j in range(TPC):
                scatter(NCH - 2, j)
            for j in range(TPC):
                base_row(NCH - 1, j)
            for j in range(TPC):
                scatter(NCH - 1, j)

            def gather(n, u):
                i = 2 * n + u
                need(pool, cx_done, i - 1)
                need(pool, gathered[u], 16 * n)
                need_alone(pool, slots_in[u], 16 * (n + 1), pool_passed)
                G.tensor_copy(gix[u][:, :], tile_slots[:, bass.ds(i, 1), 0]).then_inc(gix_ready, 1)
                need_alone(pool, gix_ready, i + 1, pool_passed)
                G.indirect_dma_start(xg[u], None, xf_d, bass.IndirectOffsetOnAxis(gix[u][:, 0:1], 0)).then_inc(
                    gathered[u], 16)

            def add_out(n, u):
                i = 2 * n + u
                need(pool, added[u], 16 * n)
                need_alone(pool, slots_in[u], 16 * (n + 1), pool_passed)
                G.tensor_copy(six[u][:, :], tile_slots[:, bass.ds(i, 1), 0]).then_inc(six_ready, 1)
                need(pool, added[1 - u], 16 * (n + u))
                need(pool, y2_ready, i + 1)
                need_alone(pool, six_ready, i + 1, pool_passed)
                G.indirect_dma_start(out, bass.IndirectOffsetOnAxis(six[u][:, 0:1], 0), y2[u], None,
                                     compute_op=ALU.add).then_inc(added[u], 16)

            def rstd(i, which, eps, done):
                pool.wait_ge(eps, i + 1)
                G.tensor_tensor(c_rs[:, which:which + 1], c_ve[:, which:which + 1], half[:, 0:1],
                                ALU.pow).then_inc(done, 1)

            def hidden_lo(i):
                pool.wait_ge(hh_ready, i + 1)
                G.tensor_tensor(hTc[:, LO].rearrange("p k t -> p (k t)"), hf,
                                hTc[:, HI].rearrange("p k t -> p (k t)").bitcast(F32), ALU.subtract).then_inc(hl_ready, 1)

            def c_tile(n, u, experts, after):
                i = 2 * n + u
                first = isinstance(i, int) and i == 0
                if not first:
                    rstd(i - 1, 1, c2_eps, c2_rstd)
                hidden_lo(i)
                if after >= 4:
                    gather(n + 2, u)
                if not first:
                    add_out(n if u else n - 1, 1 - u)
                if after >= 2:
                    rstd(i + 2, 0, c1_eps, c1_rstd)

            pool.wait_ge(b_t_done, t_num(NCH - 1, f"p3{U - 1}") + 1)
            pool.wait_ge(x1b_ready, NT)
            for j in range(TPC):
                pool.wait_ge(xf_out[j], 16 * NCH)
            for i in range(2):
                pool.wait_ge(base_out[i], 16 * NT // 2)
            pool.wait_ge(zero_out, 160)
            gather(0, 0)
            gather(0, 1)
            gather(1, 0)
            rstd(0, 0, c1_eps, c1_rstd)
            gather(1, 1)
            rstd(1, 0, c1_eps, c1_rstd)
            pool.wait_ge(plan_ready, 2)
            pool.wait_ge(p1_in, 16 * 4)
            tiles_of(pool, c_tile)
            rstd(NSLOT - 1, 1, c2_eps, c2_rstd)
            add_out((NSLOT - 1) // 2, (NSLOT - 1) % 2)
            pool.wait_ge(added[0], 16 * ((NSLOT + 1) // 2))
            pool.wait_ge(added[1], 16 * (NSLOT // 2))



def kernel(**inputs):
    import concourse.bacc as bacc
    from concourse.bass_utils import run_bass_kernel_spmd

    nc = bacc.Bacc("TRN2", target_bir_lowering=False, num_devices=1)
    arrays = {f"in_{name}": np.ascontiguousarray(array) for name, array in inputs.items()}
    io = {name: nc.dram_tensor(f"in_{name}", arrays[f"in_{name}"].shape, mybir.dt.from_np(arrays[f"in_{name}"].dtype),
                               kind="ExternalInput").ap() for name in inputs}
    out = nc.dram_tensor("out", [T + P, D], F32, kind="ExternalOutput").ap()
    decoder_layer(nc, io, out)
    result = run_bass_kernel_spmd(nc, [arrays], core_ids=[0]).results[0]["out"]
    return result[:T].reshape(B, S, D)
```

```python
from contextlib import ExitStack

import numpy as np
import concourse.bass as bass
from concourse import mybir

F32, F32R, I32 = mybir.dt.float32, mybir.dt.float32r, mybir.dt.int32
ACT = mybir.ActivationFunctionType
ALU = mybir.AluOpType
AX = mybir.AxisListType

P = 128
B, S, D = 2, 2048, 512
T = B * S
KC = D // P
CH = 512
TPC = CH // P
NCH = T // CH
NT = T // P
CPB = S // CH
NH, DH = 16, 32
HPG = P // DH
SK = 77
GK = HPG * SK
U = 3
UK = -(-GK // U)
NE = 4
EPS = 1e-5
NEG = -(2.0 ** 99)
NSLOT = 2 * T // P + NE - 1
REG = (T // P + NE + 2) * P
EARLY_CH = NCH - 2
EARLY = 2 * EARLY_CH * TPC - (NE - 1)
HI, LO = 0, 1
ROUTE_CHOSEN, ROUTE_COUNTED, ROUTE_SHIFTED, ROUTE_WEIGHED, NROUTE = 6, 10, 12, 21, 31
TERMS = ((HI, HI), (HI, LO), (LO, HI))
ROW_BZ, ROW_BH, ROW_BG, ROW_BQ, ROW_BK, ROW_G1, ROW_BE1 = 0, 4, 8, 12, 16, 20, 36
NROWS = 52


TABW = NE * REG // P


def need(engine, semaphore, value):
    if isinstance(value, int) and value <= 0:
        return
    engine.wait_ge(semaphore, value)


def need_alone(engine, semaphore, value, passed):
    need(engine, semaphore, value)
    engine.sem_inc(passed, 1)


def decoder_layer(nc, io, out, scratch_kind="Internal"):
    ctx = ExitStack()
    with ctx:
        def sb(name, shape, dt):
            return ctx.enter_context(nc.sbuf_tensor(name, shape, dt))

        def sem(name):
            return ctx.enter_context(nc.semaphore(name))

        def sems(names):
            return [sem(n) for n in names.split()]

        def dram(name, shape, dt):
            return nc.dram_tensor(name, shape, dt, kind=scratch_kind).ap()

        x1_d = dram("x1_rows", [T, D], F32)
        xf_d = dram("xf_rows", [T + P, D], F32)
        slots_d = dram("slot_table", [NE * REG, 2], I32)
        vb_d = dram("v_blocks", [B, 2 * KC * U, UK, P], F32)
        ws_d = dram("expert_parts", [2 * NE, P, 2, KC, D], F32)
        x_v = io["x"].rearrange("b (c j p) f -> (b c) p j f", j=TPC, p=P)
        x1_v = x1_d.rearrange("(c j p) f -> c p j f", j=TPC, p=P)
        xf_v = xf_d[0:T, :].rearrange("(n p) f -> n p f", p=P)
        out_v = out[0:T, :].rearrange("(n p) f -> n p f", p=P)

        KB_ = 256
        R = sb("operands", [P, 136 * KB_], F32R)
        F = sb("rows", [P, 64 * KB_], F32)

        def r_at(kb, n):
            return R[:, int(kb * KB_):int(kb * KB_) + n]

        def f_at(kb, n):
            return F[:, int(kb * KB_):int(kb * KB_) + n]

        def w_at(kb):
            return r_at(kb, 2 * KC * D).rearrange("p (a k f) -> p a k f", a=2, k=KC)

        wz, wh, wg, wk, wv = (w_at(16 * i) for i in range(5))
        wq, wo = wk, wv
        kblk = r_at(80, 2 * B * KC * GK).rearrange("p (a b m g) -> p a b m g", a=2, b=B, m=KC)
        xnT = w_at(100)
        hTr = w_at(116)
        w_stage = r_at(132, 2 * D).rearrange("p (a f) -> p a f", a=2)
        zeros_r = r_at(132, 4 * KB_)
        ctxT = r_at(100, 2 * KC * B * SK).rearrange("p (a k n) -> p a k n", a=2, k=KC)
        v_r = r_at(116, B * 2 * D).rearrange("p (b a f) -> p b a f", b=B, a=2)
        ring = f_at(0, 3 * TPC * D).rearrange("p (r j f) -> p r j f", r=3, j=TPC)
        xn = f_at(24, TPC * D).rearrange("p (j f) -> p j f", j=TPC)
        za = f_at(32, 2 * CH).rearrange("p (i t) -> p i t", i=2)
        zb = f_at(36, 2 * CH).rearrange("p (i t) -> p i t", i=2)
        hT = f_at(40, KC * CH).rearrange("p (m t) -> p m t", m=KC)
        gate = f_at(48, 2 * CH).rearrange("p (i t) -> p i t", i=2)
        ghT = f_at(52, KC * CH).rearrange("p (m t) -> p m t", m=KC)
        w_raw = f_at(60, 2 * D).rearrange("p (i f) -> p i f", i=2)
        raw = [f_at(24 + 8 * i, KC * D).rearrange("p (k f) -> p k f", k=KC) for i in range(5)]
        ctx_rows = f_at(8, B * D).rearrange("p (b f) -> p b f", b=B)
        v_rows = f_at(12, B * D).rearrange("p (b f) -> p b f", b=B)
        bv_rows = f_at(16, D)

        prow = f_at(20, P)[0:NROWS]
        tab0 = f_at(18, TABW * 2).bitcast(I32).rearrange("p (n w) -> p n w", w=2)

        x1T, qT, outT = (w_at(16 * i) for i in range(3))
        pT = r_at(100, 2 * U * CH).rearrange("p (a u t) -> p a u t", a=2, u=U)
        vblk = r_at(112, 2 * KC * U * P).rearrange("p (a m u f) -> p a m u f", a=2, m=KC, u=U)
        mask_r = r_at(124, CPB * GK).rearrange("p (s g) -> p s g", s=CPB)
        ident_r = r_at(130, P)
        x1n = xn
        pb = [f_at(32 + 5 * i, TPC * GK).rearrange("p (j g) -> p j g", j=TPC) for i in range(2)]
        xf = f_at(50, TPC * D).rearrange("p (j f) -> p j f", j=TPC)
        base = f_at(58, 2 * D).rearrange("p (i f) -> p i f", i=2)
        xfT = f_at(42, TPC * KC * P).rearrange("p (j k t) -> p j k t", j=TPC, k=KC)
        bo_rows = f_at(62, D)

        weights = r_at(0, 4 * NE * KC * D).rearrange("p (e w a k f) -> p e w a k f", e=NE, w=2, a=2, k=KC)
        xT = r_at(128, 2 * KC * P).rearrange("p (a k t) -> p a k t", a=2, k=KC)
        hTc = r_at(132, 2 * KC * P).rearrange("p (a k t) -> p a k t", a=2, k=KC)
        b1_rows, b2_rows, g2_rows, be2_rows = (f_at(kb, NE * D).rearrange("p (e f) -> p e f", e=NE)
                                               for kb in (8, 16, 24, 0))
        tile_slots = f_at(32, 2 * NSLOT).bitcast(I32).rearrange("p (i w) -> p i w", w=2)
        xg = [f_at(kb, D) for kb in (62, 40)]
        u1, hf, v2, z2 = (f_at(kb, D) for kb in (42, 46, 50, 52))
        n1 = [f_at(kb, D) for kb in (34, 44)]
        u2 = [f_at(kb, D) for kb in (48, 58)]
        y2 = [f_at(kb, D) for kb in (54, 56)]

        ident = sb("ident", [P, P], F32)
        before = sb("before", [P, P], F32)
        ones = sb("ones", [P, P], F32)
        causal = sb("causal", [P, SK], F32)
        tie = sb("tie", [P, NE, NE], F32)
        region0 = sb("region0", [P, NE], F32)
        tok_i = sb("token_ints", [P, TPC], I32)
        tok = sb("tokens", [P, TPC], F32)
        half = sb("minus_half", [P, TPC], F32)
        gate_w = sb("gate_w", [P, KC, NE], F32)
        gate_b = sb("gate_b", [P, NE], F32)
        smax = sb("score_max", [P, TPC * HPG], F32)
        nmax = sb("score_shift", [P, 2, TPC * HPG], F32)
        ssum = sb("score_sum", [P, 2, TPC * HPG], F32)
        srec = sb("score_rec", [P, 2, TPC * HPG], F32)
        st3 = sb("ln3_stats", [P, TPC, 6], F32)
        mv3 = sb("ln3_mean_var", [P, TPC, 2], F32)
        ve3 = sb("ln3_var_eps", [P, TPC], F32)
        rs3 = sb("ln3_rstd", [P, TPC], F32)
        gs = sb("gate_scores", [P, TPC, NE], F32)
        gcmp = sb("gate_compare", [P, 2, TPC, NE, NE], F32)
        rank = sb("gate_rank", [P, TPC, NE], F32)
        sel = sb("gate_sel", [P, TPC, NE], F32)
        gmax = sb("gate_max", [P, TPC], F32)
        gexp = sb("gate_exp", [P, 2, TPC, NE], F32)
        grec = sb("gate_rec", [P, 2, TPC], F32)
        is_k = sb("is_kth", [P, 2, TPC, NE], F32)
        kth = sb("kth_of", [P, 2, TPC, NE], F32)
        counts = sb("counts", [P, TPC + 1, NE], F32)
        pos = sb("positions", [P, TPC, NE], F32)
        kval = sb("kth_value", [P, 2, 2, TPC], F32)
        slot_ix = sb("slot_rows", [P, 2, TPC], I32)
        payload = sb("slot_payload", [P, TPC, 2, 2], I32)
        plan_e = sb("plan_experts", [P, NSLOT + 3], I32)
        plan_row = sb("plan_rows", [P, NSLOT], I32)
        plan_around = sb("plan_arounds", [P, (NSLOT + 1) // 2], I32)
        tile_no = sb("tile_numbers", [P, EARLY], F32)
        tile_ge = sb("tile_behind", [P, NE - 1, EARLY], F32)
        tile_e = sb("tile_experts", [P, EARLY], F32)
        tile_row = sb("tile_rows", [P, EARLY], F32)
        tile_int = sb("tile_ints", [P, EARLY], I32)
        total = sb("expert_totals", [P, NE], F32)
        total_i = sb("expert_total_ints", [P, NE], I32)
        tiles = sb("expert_tiles", [P, NE], F32)
        taken = sb("expert_tiles_taken", [P, NE], F32)
        first = sb("expert_first_tile", [P, NE], F32)
        jump = sb("expert_row_jump", [P, NE], F32)
        gix = [sb(f"gather_rows{i}", [P, 1], I32) for i in range(2)]
        six = [sb(f"scatter_rows{i}", [P, 1], I32) for i in range(2)]
        c_st = sb("moe_stats", [P, 2, 6], F32)
        c_mv = sb("moe_mean_var", [P, 2, 2], F32)
        c_ve = sb("moe_var_eps", [P, 2], F32)
        c_rs = sb("moe_rstd", [P, 2], F32)
        pcol = sb("param_cols", [P, NROWS], F32)
        carry = sb("carry", [P, KC, NCH + B + 1], F32)
        st1 = sb("ln1_stats", [P, TPC, 6], F32)
        mv1 = sb("ln1_mean_var", [P, TPC, 2], F32)
        ve1 = sb("ln1_var_eps", [P, TPC], F32)
        rs1 = sb("ln1_rstd", [P, TPC], F32)
        st2 = sb("ln2_stats", [P, TPC, 6], F32)
        mv2 = sb("ln2_mean_var", [P, TPC, 2], F32)
        mean2 = sb("ln2_mean", [P, NT], F32)
        ve2 = sb("ln2_var_eps", [P, NT], F32)
        rs2 = sb("ln2_rstd", [P, NT], F32)

        ps = ctx.enter_context(nc.psum_tensor("banks", [P, 8, CH], F32))
        mm_bank = [ps[:, i, :] for i in (2, 3)]
        s_banks = ps[:, 4:8, 0:GK]
        t_bank = [ps[:, i, :] for i in (0, 1)]
        z_bank = [ps[:, i, :] for i in (2, 3)]
        h_bank = [ps[:, i, :] for i in (4, 5)]
        g_bank = [ps[:, i, :] for i in (6, 7)]

        cx_bank, m1_bank, m2_bank = ([ps[:, i, :] for i in pair] for pair in ((2, 4), (3, 6), (1, 7)))
        ch_bank = ps[:, 5, :]

        (const_ready, prow_in, ptr_done, pcol_ready, ctx_in, wk_in, wv_in, wz_in, wh_in, wg_in, bv_in,
         w_hi, w_lo, ctxT_done, ctxT_hi, ctxT_lo, k_done, k_hi, k_lo, v_done, v_ready, v_hi, v_lo,
         zero_out, vb_out, kzero, pool_step, dve_passed, pool_passed) = sems(
            "const_ready prow_in ptr_done pcol_ready ctx_in wk_in wv_in wz_in wh_in wg_in bv_in "
            "w_hi w_lo ctxT_done ctxT_hi ctxT_lo k_done k_hi k_lo v_done v_ready v_hi v_lo "
            "zero_out vb_out kzero pool_step dve_passed pool_passed")
        (x_in, ln1_stat, ln1_aggr, ln1_eps, ln1_rstd, xn_ready, a_t_done, xnT_hi, a_t_read, z_done,
         h_done, z_ready, b_ready, a_ready, h_ready, carry_ready, hT_hi, hT_lo, g_done, gate_ready, gh_ready,
         x1_out, ln2_stat, ln2_aggr, ln2_eps, ln2_rstd, split_hi, split_lo, split_out) = sems(
            "x_in ln1_stat ln1_aggr ln1_eps ln1_rstd xn_ready a_t_done xnT_hi a_t_read z_done "
            "h_done z_ready b_ready a_ready h_ready carry_ready hT_hi hT_lo g_done gate_ready gh_ready "
            "x1_out ln2_stat ln2_aggr ln2_eps ln2_rstd split_hi split_lo split_out")
        (consts_done, tok_ready, gw_in, bo_in, x1_in, vb_in, mask_ready, x1n_ready, x1b_ready, b_t_done, x1T_hi, b_t_read,
         mm_done, mm_read, qT_hi, s_done, s_read, smax_ready, shift_ready, p_rec, p_ready, pT_hi, outT_hi,
         ln3_stat, ln3_aggr, ln3_eps, ln3_rstd, xf_ready, base_ready, route, route_exp,
         scattered, prefill_ready, prefill_out) = sems(
            "consts_done tok_ready gw_in bo_in x1_in vb_in mask_ready x1n_ready x1b_ready b_t_done x1T_hi b_t_read "
            "mm_done mm_read qT_hi s_done s_read smax_ready shift_ready p_rec p_ready pT_hi outT_hi "
            "ln3_stat ln3_aggr ln3_eps ln3_rstd xf_ready base_ready route route_exp "
            "scattered prefill_ready prefill_out")
        (moe_rows_in, be2_in, plan, plan_ready, experts_ready, cx_done, cx_hi, cx_lo, m1_done, u1_ready, ch_done, relu_done,
         hh_ready, hl_ready, m2_done, u2_ready, c1_stat, c1_aggr, c1_eps, c1_rstd, n1_ready, c2_stat, c2_aggr, c2_eps,
         c2_rstd, v2_ready, z2_ready, y2_ready) = sems(
            "moe_rows_in be2_in plan plan_ready experts_ready cx_done cx_hi cx_lo m1_done u1_ready ch_done relu_done "
            "hh_ready hl_ready m2_done u2_ready c1_stat c1_aggr c1_eps c1_rstd n1_ready c2_stat c2_aggr c2_eps "
            "c2_rstd v2_ready z2_ready y2_ready")
        w_in = [sem(f"w_in{i}") for i in range(2 * NE)]
        slots_in = [sem(f"slots_in{i}") for i in range(2)]
        gix_ready, six_ready = sems("gix_ready six_ready")
        gathered = [sem(f"gathered{i}") for i in range(2)]
        added = [sem(f"added{i}") for i in range(2)]
        split_in = [sem(f"split_in{i}") for i in range(2)]
        xf_out = [sem(f"xf_out{i}") for i in range(TPC)]
        base_out = [sem(f"base_out{i}") for i in range(2)]

        def t_group(c):
            return 0 if isinstance(c, int) and c == 0 else 8 * c - 4

        def tg_group(c):
            return 8 * (NCH - 1) + 4 if isinstance(c, int) and c == NCH - 1 else 8 * c + 8

        A_T_GROUPS = 8 * NCH

        T_ORDER = "p00 p01 p02 x0 x1 x2 x3 p10 p11 p12 xf0 xf1 p20 p21 p22 xf2 xf3 p30 p31 p32".split()
        MM_ORDER = "o0 o1 r o2 v0 o3 q0 v1 q1 q2 v2 q3 g v3".split()

        LEAD = {id(T_ORDER): "x0 x1 x2 x3".split(), id(MM_ORDER): "q0 q1 q2 q3".split()}
        TAIL = {id(T_ORDER): "xf0 xf1 xf2 xf3".split(), id(MM_ORDER): "o0 o1 r o2 o3 g t".split()}

        def groups_of(order, c):
            if isinstance(c, int) and not 0 <= c < NCH:
                return [(g, i % 2) for i, g in enumerate((LEAD if c < 0 else TAIL)[id(order)])]
            n = c if isinstance(c, int) else 2
            return [(g, i % 2) for i, g in enumerate(order) if not (
                n == 0 and (g[0] in "go" or g[:2] == "xf") or n < 2 and g == "r"
                or n == NCH - 1 and (g[0] == "q" or g in ("x0", "x1", "x2", "x3")))]

        def in_front(order, c):
            if isinstance(c, int):
                return sum(len(groups_of(order, i)) for i in range(-1, c))
            return in_front(order, 2) + (c - 2) * len(order)

        def index_in(order, c, name):
            return [g for g, _ in groups_of(order, c)].index(name)

        def t_num(c, name):
            return in_front(T_ORDER, c) + index_in(T_ORDER, c, name)

        def mm_num(c, name):
            return in_front(MM_ORDER, c) + index_in(MM_ORDER, c, name)

        def bank_of(order, c, name):
            return dict(groups_of(order, c))[name]

        def last_in_bank(order, c, name):
            before_c = c - 1 if isinstance(c, int) else 1 if len(groups_of(order, 1)) == len(order) else 2
            own = groups_of(order, c)
            at = index_in(order, c, name)
            older = [] if isinstance(c, int) and c < 0 else groups_of(order, before_c)
            row = older + own[:at]
            same = [i for i, (_, bank) in enumerate(row) if bank == own[at][1]]
            return in_front(order, c) - len(older) + same[-1] + 1 if same else 0

        def tb(c, name):
            return t_bank[bank_of(T_ORDER, c, name)]

        def mb(c, name):
            return mm_bank[bank_of(MM_ORDER, c, name)]

        def slot3(c):
            return ring[:, (c + NCH) % 3] if isinstance(c, int) else ring[:, bass.ds((c + NCH) % 3, 1)].rearrange(
                "p r j f -> p (r j) f")

        def expert_at(engine, i):
            return engine.value_load(plan_e[0:1, bass.ds(i, 1)], min_val=0, max_val=NE - 1)

        def experts_around(engine, n):
            packed = engine.value_load(plan_around[0:1, bass.ds(n, 1)], min_val=0, max_val=NE ** 6 - 1)
            return [packed % NE] + [packed // NE ** k % NE for k in range(1, 5)] + [packed // NE ** 5]

        def tiles_of(engine, tile):
            for i in range(4):
                around = [expert_at(engine, t) if t >= 0 else None for t in range(i - 2, i + 3)]
                tile(i // 2, i % 2, around, NSLOT - 1 - i)
            engine.wait_ge(plan_ready, 2)
            with engine.Fori(2, (NSLOT - 5) // 2) as n:
                around = experts_around(engine, n)
                for u in range(2):
                    tile(n, u, around[u:u + 5], NSLOT)
            for i in range(NSLOT - 5, NSLOT):
                if i % 2 == 0:
                    around = experts_around(engine, i // 2)
                tile(i // 2, i % 2, around[i % 2:i % 2 + 5], NSLOT - 1 - i)

        block = ctx.enter_context(nc.Block())

        def split_source(n):
            return ("L0_ffn_W1", "L0_ffn_W2")[n // 2], n % 2

        @block.sync
        def _(sp):
            for name, row, n in (("L0_attn_bz", ROW_BZ, 4), ("L0_attn_bh", ROW_BH, 4)):
                sp.dma_start(prow[row:row + n, :], io[name]).then_inc(prow_in, 16)
            for name, row in (("L0_attn_bg", ROW_BG), ("L0_xattn_bq", ROW_BQ), ("L0_xattn_bk", ROW_BK)):
                sp.dma_start(prow[row:row + KC, :], io[name].rearrange("(k p) -> k p", p=P)).then_inc(prow_in, 16)
            for name, row in (("L0_ffn_g1", ROW_G1), ("L0_ffn_be1", ROW_BE1)):
                sp.dma_start(prow[row:row + NE * KC, :],
                             io[name].rearrange("e (k p) -> (e k) p", p=P)).then_inc(prow_in, 16)
            sp.dma_start(ctx_rows[0:SK], io["ctx_1024"].rearrange("b s f -> s b f")).then_inc(ctx_in, 16)
            sp.dma_start(raw[3], io["L0_xattn_Wk"].rearrange("(k p) f -> p k f", p=P)).then_inc(wk_in, 16)
            sp.dma_start(raw[4], io["L0_xattn_Wv"].rearrange("(k p) f -> p k f", p=P)).then_inc(wv_in, 16)
            sp.dma_start(bv_rows[0:SK], io["L0_xattn_bv"].partition_broadcast(SK)).then_inc(bv_in, 16)
            sp.dma_start(ring[:, 0], x_v[0]).then_inc(x_in, 16)
            for slot, name, loaded in ((0, "L0_attn_Wz", wz_in), (1, "L0_attn_Wh", wh_in)):
                for n in range(KC):
                    sp.dma_start(raw[slot][:, :, n * P:(n + 1) * P],
                                 io[name][n].rearrange("(k p) f -> p k f", p=P)).then_inc(loaded, 16)
            sp.dma_start(raw[2], io["L0_attn_Wg"].rearrange("(k p) f -> p k f", p=P)).then_inc(wg_in, 16)
            need(sp, kzero, 1)
            flat = vb_d.rearrange("b g r f -> (b g r f)").rearrange("(p n) -> p n", p=P)
            n_zero = flat.shape[1] // 8
            for i in range(8):
                sp.dma_start(flat[:, i * n_zero:(i + 1) * n_zero], zeros_r[:, 0:n_zero].bitcast(F32)).then_inc(zero_out, 16)
            sp.dma_start(xf_d[T:T + P, :], zeros_r[:, 0:D].bitcast(F32)).then_inc(zero_out, 16)
            sp.dma_start(out[T:T + P, :], zeros_r[:, 0:D].bitcast(F32)).then_inc(zero_out, 16)
            sp.wait_ge(zero_out, 16 * 10)
            sp.wait_ge(v_hi, B)
            sp.wait_ge(v_lo, B)
            for b in range(B):
                for part in (HI, LO):
                    rows = vb_d[b, part * KC * U:(part + 1) * KC * U].rearrange("(m u) r f -> m (u r) f", m=KC)
                    for hl in range(HPG):
                        sp.dma_start(
                            rows[:, hl * SK:(hl + 1) * SK, hl * DH:(hl + 1) * DH].rearrange("m s f -> s m f"),
                            v_r[0:SK, b, part, :].rearrange("p (m f) -> p m f", m=KC)[:, :, hl * DH:(hl + 1) * DH].bitcast(F32),
                        ).then_inc(vb_out, 16)
            sp.dma_start(gate_w[:, :, :], io["L0_ffn_gate_W"].rearrange("(k p) e -> p k e", p=P)).then_inc(gw_in, 16)
            sp.dma_start(gate_b[:, :], io["L0_ffn_gate_b"].partition_broadcast(P)).then_inc(gw_in, 16)
            sp.wait_ge(prefill_ready, 1)
            sp.dma_start(slots_d.rearrange("(p n) w -> p n w", p=P), tab0[:, :, :]).then_inc(prefill_out, 16)
            sp.wait_ge(w_lo, 2)
            sp.dma_start(raw[3], io["L0_xattn_Wq"].rearrange("(k p) f -> p k f", p=P)).then_inc(wk_in, 16)
            sp.dma_start(raw[4], io["L0_xattn_Wo"].rearrange("(k p) f -> p k f", p=P)).then_inc(wv_in, 16)
            sp.wait_ge(prefill_out, 16)
            sp.wait_ge(pcol_ready, 1)
            sp.wait_ge(ctxT_done, 2)
            sp.wait_ge(x_in, 16)
            sp.wait_ge(v_lo, B)
            sp.dma_start(ring[:, 1], x_v[1]).then_inc(x_in, 16)
            sp.wait_ge(x_in, 32)
            sp.dma_start(ring[:, 2], x_v[2]).then_inc(x_in, 16)

            def a_chunk(c, last=False):
                for n in range(4):
                    if n == 2 and not (isinstance(c, int) and c == 0):
                        a_store(c - 1, prefetch=not isinstance(c, int))
                    need(sp, split_lo, 4 * c + n - 1)
                    if n < 2 and isinstance(c, int) and c == 0:
                        sp.wait_ge(w_lo, 7)
                    name, k = split_source(n)
                    src = io[name].rearrange("e (k p) f -> e k p f", p=P)
                    e, kc = c // 2, (c % 2) * 2 + k
                    src = src[e, kc] if isinstance(c, int) else src[bass.ds(e, 1), bass.ds(kc, 1)].rearrange(
                        "a b p f -> p (a b f)")
                    sp.dma_start(w_raw[:, n % 2], src).then_inc(split_in[n % 2], 16)
                    if not (isinstance(c, int) and c == 0 and n == 0):
                        store_piece(c if n else c - 1, (n - 1) % 4, 4 * c + n)

            def store_piece(c, n, count):
                need(sp, split_lo, count)
                e2 = (c // 2) * 2 + n // 2
                kc = (c % 2) * 2 + n % 2
                dst = ws_d[e2, :, :, kc, :] if isinstance(c, int) else ws_d[
                    bass.ds(e2, 1), :, :, bass.ds(kc, 1), :].rearrange("m p a k f -> p (m a k) f")
                sp.dma_start(dst, w_stage[:, :, :].bitcast(F32)).then_inc(split_out, 16)

            def a_store(c, prefetch=True):
                need(sp, ln2_stat, 4 * (c + 1))
                x1 = ring[:, c % 3] if isinstance(c, int) else ring[:, bass.ds(c % 3, 1)].rearrange(
                    "p r j f -> p (r j) f")
                dst = x1_v[c] if isinstance(c, int) else x1_v[bass.ds(c, 1)].rearrange("c p j f -> p (c j) f")
                sp.dma_start(dst, x1).then_inc(x1_out, 16)
                sp.wait_ge(x1_out, 16 * (c + 1))
                if isinstance(c, int) and c >= NCH - 3:
                    sp.dma_start(x1, x1_v[c - (NCH - 3)]).then_inc(x1_in, 16)
                if prefetch:
                    sp.wait_ge(x_in, 16 * (c + 3))
                    src = x_v[c + 3] if isinstance(c, int) else x_v[bass.ds(c + 3, 1)].rearrange(
                        "c p j f -> p (c j) f")
                    sp.dma_start(x1, src).then_inc(x_in, 16)

            a_chunk(0)
            with sp.Fori(1, NCH - 2) as c:
                a_chunk(c)
            a_chunk(NCH - 2)
            a_chunk(NCH - 1)
            store_piece(NCH - 1, 3, 4 * NCH)
            a_store(NCH - 1, prefetch=False)

            def load_v(c):
                need(sp, mm_done, mm_num(c - 1, "v3") + 1 if not (isinstance(c, int) and c == 0) else 0)
                b = c // CPB
                src = vb_d[b] if isinstance(b, int) else vb_d[bass.ds(b, 1)].rearrange("b g r f -> (b g) r f")
                sp.dma_start(vblk[0:UK].rearrange("p a m u f -> p (a m u) f").bitcast(F32),
                             src.rearrange("g r f -> r g f")).then_inc(vb_in, 16)

            def store_xf(c, j):
                t = 4 * c + j
                need(sp, xf_ready, t + 1)
                sp.dma_start(xf_v[t] if isinstance(t, int) else xf_v[bass.ds(t, 1)].rearrange("n p f -> p (n f)"),
                             xf[:, j]).then_inc(xf_out[j], 16)

            def store_base(c, j):
                t = 4 * c + j
                need(sp, base_ready, t + 1)
                sp.dma_start(out_v[t] if isinstance(t, int) else out_v[bass.ds(t, 1)].rearrange("n p f -> p (n f)"),
                             base[:, j % 2]).then_inc(base_out[j % 2], 16)

            def store_rows(c):
                for j in range(TPC):
                    store_xf(c, j)
                    store_base(c, j)

            def b_chunk(c, first=False, load=True):
                load_v(c)
                if not first:
                    store_rows(c - 1)
                    if load:
                        sp.wait_ge(x1_in, 16 * (c + 2))
                        src = x1_v[c + 2] if isinstance(c, int) else x1_v[bass.ds(c + 2, 1)].rearrange(
                            "c p j f -> p (c j) f")
                        sp.dma_start(slot3(c + 2), src).then_inc(x1_in, 16)

            sp.wait_ge(w_lo, 7)
            sp.wait_ge(g_done, KC * NCH)
            sp.dma_start(bo_rows, io["L0_xattn_bo"].partition_broadcast(P)).then_inc(bo_in, 16)
            b_chunk(0, first=True)
            b_chunk(1)
            with sp.Fori(2, NCH - 2) as c:
                b_chunk(c)
            b_chunk(NCH - 2, load=False)
            load_v(NCH - 1)

            def load_expert(s):
                e, w = s // 2, s % 2
                sp.dma_start(weights[:, e, w].rearrange("p a k f -> p (a k f)").bitcast(F32),
                             ws_d[s].rearrange("p a k f -> p (a k f)")).then_inc(w_in[s], 16)

            def load_rows(dst, name, loaded=moe_rows_in):
                sp.dma_start(dst, io[name].rearrange("e f -> (e f)").partition_broadcast(P).rearrange(
                    "p (e f) -> p e f", e=NE)).then_inc(loaded, 16)

            sp.wait_ge(split_out, 16 * 4 * NCH)
            sp.wait_ge(mm_done, mm_num(NCH - 2, "q3") + 1)
            load_expert(0)
            load_expert(3)
            load_rows(b1_rows, "L0_ffn_b1")
            load_rows(g2_rows, "L0_ffn_g2")
            store_rows(NCH - 2)
            load_rows(b2_rows, "L0_ffn_b2")
            sp.wait_ge(s_done, 2 * KC * NCH)
            load_expert(1)
            load_expert(5)
            sp.wait_ge(b_t_done, t_num(NCH - 1, f"p3{U - 1}") + 1)
            sp.wait_ge(mm_done, mm_num(NCH - 1, "v3") + 1)
            load_expert(6)
            load_expert(7)
            sp.wait_ge(mm_done, mm_num(NCH, "o3") + 1)
            load_expert(2)
            load_expert(4)

            def load_slots(n, u):
                i = 2 * n + u
                row = sp.value_load(plan_row[0:1, bass.ds(i, 1)], min_val=0, max_val=NE * REG - P)
                need(sp, slots_in[u], 16 * n)
                sp.dma_start(tile_slots[:, bass.ds(i, 1), :].rearrange("p i w -> p (i w)"),
                             slots_d[bass.ds(row, P), :]).then_inc(slots_in[u], 16)

            sp.wait_ge(plan_ready, 1)
            sp.wait_ge(scattered, 16 * 2 * TPC * EARLY_CH)
            for u in range(2):
                load_slots(0, u)
            for j in range(TPC):
                store_xf(NCH - 1, j)
            for j in range(TPC):
                store_base(NCH - 1, j)
            load_rows(be2_rows, "L0_ffn_be2", be2_in)
            for e in range(NE):
                sp.wait_ge(w_in[2 * e], 16)
                sp.wait_ge(w_in[2 * e + 1], 16)
                sp.sem_inc(experts_ready, 1)

            with sp.Fori(1, EARLY // 2) as n:
                for u in range(2):
                    load_slots(n, u)
            sp.wait_ge(plan_ready, 2)
            sp.wait_ge(scattered, 16 * 2 * NT)
            with sp.Fori(EARLY // 2, NSLOT // 2) as n:
                for u in range(2):
                    load_slots(n, u)
            load_slots(NSLOT // 2, 0)

        @block.tensor
        def _(pe):
            def product(dst, terms, n_k, stationary, moving):
                last = None
                for t, (a, b) in enumerate(terms):
                    for k in range(n_k):
                        last = nc.tensor.matmul(dst, stationary(a, k), moving(b, k), start=(t == 0 and k == 0),
                                                stop=(t == len(terms) - 1 and k == n_k - 1))
                return last

            pe.wait_ge(const_ready, 1)
            pe.wait_ge(prow_in, 16 * 7)
            nc.tensor.transpose(g_bank[0][:, 0:NROWS], prow[:, :], ident[0:NROWS, 0:NROWS]).then_inc(ptr_done, 1)
            pe.wait_ge(ctx_in, 16)
            for half_k in range(2):
                for b in range(B):
                    for i in range(2):
                        k = 2 * half_k + i
                        last = nc.tensor.transpose(
                            t_bank[half_k][:, i * B * SK + b * SK:i * B * SK + (b + 1) * SK],
                            ctx_rows[0:SK, b, k * P:(k + 1) * P], ident[0:SK, 0:SK])
                last.then_inc(ctxT_done, 1)
            pe.wait_ge(w_lo, 1)
            pe.wait_ge(ctxT_lo, 2)
            for m in range(KC):
                if m >= 2:
                    pe.wait_ge(k_lo, HPG * (m - 1))
                product(z_bank[m % 2][:, 0:B * SK], TERMS, KC,
                        lambda a, k: wk[:, a, k, m * P:(m + 1) * P],
                        lambda a, k: ctxT[:, a, k, :]).then_inc(k_done, 1)
            pe.wait_ge(w_lo, 2)
            for b in range(B):
                product(h_bank[b][0:SK, :], TERMS, KC,
                        lambda a, k: ctxT[:, a, k, b * SK:(b + 1) * SK],
                        lambda a, k: wv[:, a, k, :]).then_inc(v_done, 1)

            def transpose_x(c, ks=range(KC)):
                for k in ks:
                    g = t_group(c) + k
                    need(pe, a_t_read, g - 1)
                    for j in range(TPC):
                        if k == 0:
                            pe.wait_ge(xn_ready, 4 * c + j + 1)
                        last = nc.tensor.transpose(t_bank[k % 2][:, j * P:(j + 1) * P],
                                                   xn[:, j, k * P:(k + 1) * P], ident[:, :])
                    last.then_inc(a_t_done, 1)

            def z_and_h(c, back=True):
                pe.wait_ge(a_t_read, t_group(c) + 4)
                for m in range(KC):
                    n = 4 * c + m
                    need(pe, z_ready, n - 1)
                    product(z_bank[m % 2], TERMS, KC, lambda a, k: wz[:, a, k, m * P:(m + 1) * P],
                            lambda a, k: xnT[:, a, k, :]).then_inc(z_done, 1)
                    need(pe, b_ready, n - 1)
                    product(h_bank[m % 2], TERMS, KC, lambda a, k: wh[:, a, k, m * P:(m + 1) * P],
                            lambda a, k: xnT[:, a, k, :]).then_inc(h_done, 1)
                    if back and m < 2:
                        gated_back(c - 1, 2 * m)
                        gated_back(c - 1, 2 * m + 1)

            def gate_terms(c, m, ks):
                for k in ks:
                    for t, (a, a2) in enumerate(TERMS):
                        last = nc.tensor.matmul(g_bank[m % 2], wg[:, a, k, m * P:(m + 1) * P], hTr[:, a2, k, :],
                                                start=(k == 0 and t == 0),
                                                stop=(k == KC - 1 and t == len(TERMS) - 1))
                return last

            def gates(c, ahead=True):
                if ahead:
                    transpose_x(c + 1, (0, 1))
                for m in range(2):
                    need(pe, gate_ready, 4 * c + m - 1)
                    if m == 0:
                        pe.wait_ge(hT_lo, 4 * c + KC - 1)
                    gate_terms(c, m, range(KC - 1))
                pe.wait_ge(hT_lo, 4 * c + KC)
                for m in range(2):
                    gate_terms(c, m, (KC - 1,)).then_inc(g_done, 1)
                if ahead:
                    transpose_x(c + 1, (2, 3))
                for m in range(2, KC):
                    pe.wait_ge(gate_ready, 4 * c + m - 1)
                    gate_terms(c, m, range(KC)).then_inc(g_done, 1)

            def gated_back(c, j):
                g = tg_group(c) + j
                pe.wait_ge(a_t_read, g - 1)
                for m in range(KC):
                    if j == 0:
                        pe.wait_ge(gh_ready, 4 * c + m + 1)
                    last = nc.tensor.transpose(t_bank[j % 2][:, m * P:(m + 1) * P],
                                               ghT[:, m, j * P:(j + 1) * P], ident[:, :])
                last.then_inc(a_t_done, 1)

            pe.wait_ge(ctxT_lo, 2)
            transpose_x(0)
            pe.wait_ge(k_lo, HPG * KC)
            pe.wait_ge(v_ready, B)
            pe.wait_ge(w_lo, 4)
            z_and_h(0, back=False)
            pe.wait_ge(pcol_ready, 1)
            pe.wait_ge(w_lo, 5)
            gates(0)
            with pe.Fori(1, NCH - 1) as c:
                z_and_h(c)
                gates(c)
            z_and_h(NCH - 1)
            gates(NCH - 1, ahead=False)
            for j in range(TPC):
                gated_back(NCH - 1, j)

            def t_free(c, name):
                need(pe, b_t_read, last_in_bank(T_ORDER, c, name))

            def mm_free(c, name):
                need(pe, mm_read, last_in_bank(MM_ORDER, c, name))

            def x1_to_features(c, at, ks):
                for k in ks:
                    t_free(at, f"x{k}")
                    for j in range(TPC):
                        if k == 0:
                            pe.wait_ge(x1n_ready, 4 * c + j + 1)
                        last = nc.tensor.transpose(tb(at, f"x{k}")[:, j * P:(j + 1) * P],
                                                   x1n[:, j, k * P:(k + 1) * P], ident[:, :])
                    last.then_inc(b_t_done, 1)

            def queries(c, at, m):
                mm_free(at, f"q{m}")
                pe.wait_ge(b_t_read, t_num(c - 1, "x3") + 1)
                product(mb(at, f"q{m}"), TERMS, KC, lambda a, k: wq[:, a, k, m * P:(m + 1) * P],
                        lambda a, k: x1T[:, a, k, :]).then_inc(mm_done, 1)

            def scores(c, m, tiles):
                need(pe, s_read, TPC * HPG * (4 * c + m - 1) + HPG * (tiles[-1] + 1))
                if tiles[0] == 0:
                    need(pe, mm_read, mm_num(c - 1, f"q{m}") + 1)
                b = c // CPB
                for j in tiles:
                    for t, (a, a2) in enumerate(TERMS):
                        keys = kblk[:, a2, b, m, :] if isinstance(b, int) else kblk[:, a2, bass.ds(b, 1), m, :].rearrange(
                            "p b g -> p (b g)")
                        last = nc.tensor.matmul(s_banks[:, j, :], qT[:, a, m, j * P:(j + 1) * P], keys,
                                                start=(t == 0), stop=(t == len(TERMS) - 1 and j > 0))
                    if j == 0:
                        s = c % CPB
                        last = nc.tensor.matmul(
                            s_banks[:, j, :], ident_r, mask_r[:, s, :] if isinstance(s, int) else
                            mask_r[:, bass.ds(s, 1), :].rearrange("p s g -> p (s g)"), start=False, stop=True)
                last.then_inc(s_done, 1)

            def probs_to_keys(c, m, parts):
                for u in parts:
                    if u == 0:
                        pe.wait_ge(p_ready, 4 * c + m + 1)
                    n = min(UK, GK - u * UK)
                    t_free(c, f"p{m}{u}")
                    for j in range(TPC):
                        last = nc.tensor.transpose(tb(c, f"p{m}{u}")[0:n, j * P:(j + 1) * P],
                                                   pb[m % 2][:, j, u * UK:u * UK + n], ident[:, :])
                    last.then_inc(b_t_done, 1)

            def attend(c, m):
                mm_free(c, f"v{m}")
                pe.wait_ge(vb_in, 16 * (c + 1))
                pe.wait_ge(pT_hi, 12 * c + U * (m + 1))
                for t, (a, a2) in enumerate(((HI, HI), (LO, HI), (HI, LO))):
                    if a2 == LO:
                        pe.wait_ge(b_t_read, t_num(c, f"p{m}{U - 1}") + 1)
                    for u in range(U):
                        n = min(UK, GK - u * UK)
                        last = nc.tensor.matmul(mb(c, f"v{m}"), vblk[0:n, a, m, u, :], pT[0:n, a2, u, :],
                                                start=(t == 0 and u == 0), stop=(t == len(TERMS) - 1 and u == U - 1))
                last.then_inc(mm_done, 1)

            def project(c, at, j):
                mm_free(at, f"o{j}")
                for m in range(KC):
                    pe.wait_ge(mm_read, mm_num(c, f"v{m}") + 1)
                    for t, (a, a2) in enumerate(TERMS):
                        last = nc.tensor.matmul(mb(at, f"o{j}"), outT[:, a, m, j * P:(j + 1) * P], wo[:, a2, m, :],
                                                start=(m == 0 and t == 0), stop=(m == KC - 1 and t == len(TERMS) - 1))
                last.then_inc(mm_done, 1)

            def xf_to_features(c, at, j):
                t_free(at, f"xf{j}")
                pe.wait_ge(xf_ready, 4 * c + j + 1)
                for k in range(KC):
                    last = nc.tensor.transpose(tb(at, f"xf{j}")[:, k * P:(k + 1) * P], xf[:, j, k * P:(k + 1) * P],
                                               ident[:, :])
                last.then_inc(b_t_done, 1)

            def gate_scores(at, tiles=range(TPC)):
                if tiles[0] == 0:
                    mm_free(at, "g")
                for j in tiles:
                    pe.wait_ge(b_t_read, t_num(at, f"xf{j}") + 1)
                    for k in range(KC):
                        last = nc.tensor.matmul(mb(at, "g")[:, j * NE:(j + 1) * NE], xfT[:, j, k, :], gate_w[:, k, :],
                                                start=(k == 0), stop=(k == KC - 1))
                if tiles[-1] == TPC - 1:
                    last.then_inc(mm_done, 1)

            def positions(c, at, name, totals=False):
                mm_free(at, name)
                pe.wait_ge(route, NROUTE * c + ROUTE_COUNTED)
                dst = mb(at, name)[:, 0:TPC * NE]
                nc.tensor.matmul(dst, before[:, :], sel[:, :, :].rearrange("p j e -> p (j e)"), start=True, stop=False)
                last = nc.tensor.matmul(dst, ones[:, :], counts[:, 0:TPC, :].rearrange("p j e -> p (j e)"),
                                        start=False, stop=True)
                if totals:
                    last = nc.tensor.matmul(mb(at, name)[:, TPC * NE:(TPC + 1) * NE], ones[:, :], counts[:, TPC, :],
                                            start=True, stop=True)
                last.then_inc(mm_done, 1)

            def b_turn(c, back=True, back2=True, ahead=True):
                scores(c, 1, (2, 3))
                probs_to_keys(c, 0, (0, 1))
                if back:
                    project(c - 1, c, 0)
                probs_to_keys(c, 0, (2,))
                if ahead:
                    x1_to_features(c + 1, c, (0,))
                if back:
                    project(c - 1, c, 1)
                if ahead:
                    x1_to_features(c + 1, c, (1, 2))
                if back2:
                    positions(c - 2, c, "r", totals=not ahead)
                if back:
                    project(c - 1, c, 2)
                if ahead:
                    x1_to_features(c + 1, c, (3,))
                scores(c, 2, (0, 1))
                attend(c, 0)
                scores(c, 2, (2, 3))
                probs_to_keys(c, 1, (0, 1))
                if back:
                    project(c - 1, c, 3)
                probs_to_keys(c, 1, (2,))
                if back:
                    xf_to_features(c - 1, c, 0)
                if ahead:
                    queries(c + 1, c, 0)
                if back:
                    xf_to_features(c - 1, c, 1)
                scores(c, 3, (0, 1))
                attend(c, 1)
                scores(c, 3, (2, 3))
                probs_to_keys(c, 2, (0, 1))
                if ahead:
                    queries(c + 1, c, 1)
                probs_to_keys(c, 2, (2,))
                if back:
                    xf_to_features(c - 1, c, 2)
                if ahead:
                    queries(c + 1, c, 2)
                if back:
                    xf_to_features(c - 1, c, 3)
                if ahead:
                    scores(c + 1, 0, (0, 1))
                attend(c, 2)
                if ahead:
                    scores(c + 1, 0, (2, 3))
                probs_to_keys(c, 3, (0, 1))
                if ahead:
                    queries(c + 1, c, 3)
                if back:
                    gate_scores(c, (0, 1))
                probs_to_keys(c, 3, (2,))
                if back:
                    gate_scores(c, (2,))
                if ahead:
                    scores(c + 1, 1, (0, 1))
                if back:
                    gate_scores(c, (3,))
                attend(c, 3)

            pe.wait_ge(consts_done, 1)
            pe.wait_ge(gw_in, 32)
            pe.wait_ge(w_lo, 7)
            pe.wait_ge(a_t_read, A_T_GROUPS)
            pe.wait_ge(z_ready, KC * NCH)
            x1_to_features(0, -1, range(KC))
            for m in range(KC):
                queries(0, -1, m)
            pe.wait_ge(b_ready, KC * NCH)
            pe.wait_ge(gate_ready, KC * NCH)
            pe.wait_ge(mask_ready, 2)
            scores(0, 0, (0, 1))
            scores(0, 0, (2, 3))
            scores(0, 1, (0, 1))
            b_turn(0, back=False, back2=False)
            b_turn(1, back2=False)
            with pe.Fori(2, NCH - 1) as c:
                b_turn(c)
            b_turn(NCH - 1, ahead=False)
            for j in range(TPC):
                project(NCH - 1, NCH, j)
                if j == 1:
                    positions(NCH - 2, NCH, "r")
            for j in range(TPC):
                xf_to_features(NCH - 1, NCH, j)
            gate_scores(NCH)
            positions(NCH - 1, NCH, "t", totals=True)

            def expert_product(dst, e, w, stationary, ready=None):
                for t, (a, a2) in enumerate(TERMS):
                    if a == LO and ready is not None:
                        pe.wait_ge(*ready)
                    for k in range(KC):
                        last = nc.tensor.matmul(
                            dst, stationary[:, a, k, :],
                            weights[:, bass.ds(e, 1), w, a2, k, :].rearrange("p e f -> p (e f)"),
                            start=(t == 0 and k == 0), stop=(t == len(TERMS) - 1 and k == KC - 1))
                return last

            def rows_in(n, u):
                i = 2 * n + u
                pe.wait_ge(gathered[u], 16 * (n + 1))
                need(pe, cx_lo, i - 1)
                for k in range(KC):
                    last = nc.tensor.transpose(cx_bank[u][:, k * P:(k + 1) * P], xg[u][:, k * P:(k + 1) * P], ident[:, :])
                last.then_inc(cx_done, 1)

            def first_product(i, u, e):
                pe.wait_ge(experts_ready, e + 1)
                pe.wait_ge(cx_lo, i + 1)
                need(pe, u1_ready, i - 1)
                expert_product(m1_bank[u], e, 0, xT).then_inc(m1_done, 1)

            def hidden_in(i, u):
                pe.wait_ge(n1_ready, i + 1)
                need(pe, relu_done, KC * i)
                for k in range(KC):
                    last = nc.tensor.transpose(ch_bank[:, k * P:(k + 1) * P], n1[u][:, k * P:(k + 1) * P], ident[:, :])
                last.then_inc(ch_done, 1)

            def second_product(i, u, e):
                pe.wait_ge(hh_ready, i + 1)
                need(pe, u2_ready, i - 1)
                expert_product(m2_bank[u], e, 1, hTc, ready=(hl_ready, i + 1)).then_inc(m2_done, 1)

            def c_tile(n, u, experts, after):
                i = 2 * n + u
                hidden_in(i, u)
                if after >= 3:
                    rows_in(n + 1 + u, 1 - u)
                if after >= 2:
                    first_product(i + 2, u, experts[4])
                second_product(i, u, experts[2])

            pe.wait_ge(plan_ready, 1)
            pe.wait_ge(s_read, TPC * HPG * KC * NCH)
            pe.wait_ge(mm_read, mm_num(NCH, "t") + 1)
            pe.wait_ge(b_t_read, t_num(NCH, "xf3") + 1)
            rows_in(0, 0)
            first_product(0, 0, expert_at(pe, 0))
            rows_in(0, 1)
            first_product(1, 1, expert_at(pe, 1))
            rows_in(1, 0)
            tiles_of(pe, c_tile)

        @block.scalar
        def _(act):
            def hi_part(dst, src):
                return nc.scalar.activation(dst, src, ACT.Copy)

            for half_k in range(2):
                act.wait_ge(ctxT_done, half_k + 1)
                hi_part(ctxT[:, HI, 2 * half_k:2 * half_k + 2, :],
                        t_bank[half_k][:, 0:2 * B * SK].rearrange("p (k n) -> p k n", k=2)).then_inc(ctxT_hi, 1)
            for dst, src, loaded, count in ((wk, raw[3], wk_in, 16), (wv, raw[4], wv_in, 16)):
                act.wait_ge(loaded, count)
                hi_part(dst[:, HI], src).then_inc(w_hi, 1)
            act.wait_ge(pcol_ready, 1)
            act.wait_ge(kzero, 1)
            for m in range(KC):
                act.wait_ge(k_done, m + 1)
                for hl in range(HPG):
                    rows = slice(hl * DH, (hl + 1) * DH)
                    nc.scalar.activation(kblk[rows, HI, :, m, hl * SK:(hl + 1) * SK],
                                         z_bank[m % 2][rows, 0:B * SK].rearrange("p (b s) -> p b s", b=B),
                                         ACT.Identity, bias=pcol[rows, ROW_BK + m:ROW_BK + m + 1]).then_inc(k_hi, 1)
            act.wait_ge(wz_in, 64)
            hi_part(wz[:, HI], raw[0]).then_inc(w_hi, 1)
            for b in range(B):
                act.wait_ge(v_ready, b + 1)
                hi_part(v_r[0:SK, b, HI, :], v_rows[0:SK, b, :]).then_inc(v_hi, 1)
            for dst, src, loaded, count in ((wh, raw[1], wh_in, 64), (wg, raw[2], wg_in, 16)):
                act.wait_ge(loaded, count)
                hi_part(dst[:, HI], src).then_inc(w_hi, 1)

            def x_hi(c, ks=range(KC)):
                for k in ks:
                    act.wait_ge(a_t_done, t_group(c) + k + 1)
                    hi_part(xnT[:, HI, k, :], t_bank[k % 2]).then_inc(xnT_hi, 1)

            def h_hi(c, m):
                act.wait_ge(h_ready, 4 * c + m + 1)
                hi_part(hTr[:, HI, m, :], hT[:, m, :]).then_inc(hT_hi, 1)

            def split_piece_hi(c, n):
                act.wait_ge(split_in[n % 2], 16 * (2 * c + n // 2 + 1))
                need(act, split_out, 16 * (4 * c + n))
                hi_part(w_stage[:, HI], w_raw[:, n % 2]).then_inc(split_hi, 1)

            def a_chunk(c, last=False):
                for m in range(KC):
                    n = 4 * c + m
                    if m:
                        h_hi(c, m - 1)
                    act.wait_ge(z_done, n + 1)
                    need(act, h_ready, n - 1)
                    nc.scalar.activation(za[:, m % 2, :], z_bank[m % 2], ACT.Sigmoid,
                                         bias=pcol[:, ROW_BZ + m:ROW_BZ + m + 1]).then_inc(z_ready, 1)
                    if m % 2:
                        split_piece_hi(c, m // 2)
                h_hi(c, KC - 1)
                for m in range(KC):
                    if not last and m % 2 == 0:
                        x_hi(c + 1, (m, m + 1))
                    n = 4 * c + m
                    act.wait_ge(g_done, n + 1)
                    need(act, gh_ready, n - 1)
                    nc.scalar.activation(gate[:, m % 2, :], g_bank[m % 2], ACT.Sigmoid,
                                         bias=pcol[:, ROW_BG + m:ROW_BG + m + 1]).then_inc(gate_ready, 1)
                    if m >= 2:
                        split_piece_hi(c, m)

            x_hi(0)
            for dst, src, loaded, used, count in ((wq, raw[3], wk_in, k_done, KC), (wo, raw[4], wv_in, v_done, B)):
                act.wait_ge(loaded, 32)
                act.wait_ge(used, count)
                hi_part(dst[:, HI], src).then_inc(w_hi, 1)
            act.wait_ge(zero_out, 160)
            a_chunk(0)
            with act.Fori(1, NCH - 1) as c:
                a_chunk(c)
            a_chunk(NCH - 1, last=True)

            def x1_hi(c, ks):
                for k in ks:
                    act.wait_ge(b_t_done, t_num(c - 1, f"x{k}") + 1)
                    hi_part(x1T[:, HI, k, :], tb(c - 1, f"x{k}")).then_inc(x1T_hi, 1)

            def q_hi(c, m):
                act.wait_ge(mm_done, mm_num(c - 1, f"q{m}") + 1)
                nc.scalar.activation(qT[:, HI, m, :], mb(c - 1, f"q{m}"), ACT.Identity,
                                     bias=pcol[:, ROW_BQ + m:ROW_BQ + m + 1]).then_inc(qT_hi, 1)

            def exp_scores(c, m, tiles):
                for half_j in sorted({j // 2 for j in tiles if j % 2 == 0}):
                    act.wait_ge(shift_ready, 2 * (4 * c + m) + half_j + 1)
                if tiles[0] == 0:
                    need(act, p_rec, 4 * c + m - 1)
                    if m >= 2:
                        act.wait_ge(b_t_done, t_num(c, f"p{m - 2}{U - 1}") + 1)
                    elif not (isinstance(c, int) and c == 0):
                        act.wait_ge(b_t_done, t_num(c - 1, f"p{m + 2}{U - 1}") + 1)
                for j in tiles:
                    for hl in range(HPG):
                        keys, at = slice(hl * SK, (hl + 1) * SK), slice(HPG * j + hl, HPG * j + hl + 1)
                        nc.scalar.activation(pb[m % 2][:, j, keys], s_banks[:, j, keys], ACT.Exp,
                                             bias=nmax[:, m % 2, at], scale=float(DH) ** -0.5,
                                             accum_out=ssum[:, m % 2, at]).then_inc(s_read, 1)

            def pT_hi_part(c, m, parts):
                for u in parts:
                    n = min(UK, GK - u * UK)
                    act.wait_ge(b_t_done, t_num(c, f"p{m}{u}") + 1)
                    hi_part(pT[0:n, HI, u, :], tb(c, f"p{m}{u}")[0:n]).then_inc(pT_hi, 1)

            def out_hi(c, m, back=False):
                act.wait_ge(mm_done, mm_num(c, f"v{m}") + 1)
                if m == 0 and back:
                    act.wait_ge(mm_done, mm_num(c, "o3") + 1)
                hi_part(outT[:, HI, m, :], mb(c, f"v{m}")).then_inc(outT_hi, 1)

            def route_weights(c):
                act.wait_ge(route, NROUTE * c + ROUTE_SHIFTED)
                nc.scalar.activation(gexp[:, 0].rearrange("p j e -> p (j e)"), gexp[:, 0].rearrange("p j e -> p (j e)"),
                                     ACT.Exp).then_inc(route_exp, 1)

            def b_turn(c, back=True, back2=True, ahead=True):
                exp_scores(c, 1, (0,))
                pT_hi_part(c, 0, (0, 1))
                exp_scores(c, 1, (1,))
                exp_scores(c, 1, (2,))
                pT_hi_part(c, 0, (2,))
                if ahead:
                    x1_hi(c + 1, (0,))
                exp_scores(c, 1, (3,))
                if ahead:
                    x1_hi(c + 1, (1, 2))
                if back2:
                    route_weights(c - 2)
                if ahead:
                    x1_hi(c + 1, (3,))
                exp_scores(c, 2, (0,))
                pT_hi_part(c, 1, (0, 1))
                exp_scores(c, 2, (1,))
                exp_scores(c, 2, (2,))
                out_hi(c, 0, back)
                pT_hi_part(c, 1, (2,))
                exp_scores(c, 2, (3,))
                if ahead:
                    q_hi(c + 1, 0)
                out_hi(c, 1)
                exp_scores(c, 3, (0,))
                pT_hi_part(c, 2, (0, 1))
                exp_scores(c, 3, (1,))
                exp_scores(c, 3, (2,))
                if ahead:
                    q_hi(c + 1, 1)
                pT_hi_part(c, 2, (2,))
                exp_scores(c, 3, (3,))
                if ahead:
                    q_hi(c + 1, 2)
                out_hi(c, 2)
                if ahead:
                    exp_scores(c + 1, 0, (0,))
                pT_hi_part(c, 3, (0, 1))
                if ahead:
                    exp_scores(c + 1, 0, (1,))
                    exp_scores(c + 1, 0, (2,))
                    q_hi(c + 1, 3)
                pT_hi_part(c, 3, (2,))
                if ahead:
                    exp_scores(c + 1, 0, (3,))
                out_hi(c, 3)

            act.wait_ge(g_done, KC * NCH)
            hi_part(ident_r, ident[:, :]).then_inc(mask_ready, 1)
            act.wait_ge(kzero, 2)
            hi_part(mask_r[:, 0, :].rearrange("p (h s) -> p h s", h=HPG),
                    causal[:, :].unsqueeze(1).to_broadcast([P, HPG, SK])).then_inc(mask_ready, 1)
            x1_hi(0, range(KC))
            for m in range(KC):
                q_hi(0, m)
            for j in range(TPC):
                exp_scores(0, 0, (j,))
            b_turn(0, back=False, back2=False)
            b_turn(1, back2=False)
            with act.Fori(2, NCH - 1) as c:
                b_turn(c)
            b_turn(NCH - 1, ahead=False)
            route_weights(NCH - 2)
            route_weights(NCH - 1)

            def rows_hi(i, u):
                act.wait_ge(cx_done, i + 1)
                need(act, m1_done, i)
                hi_part(xT[:, HI].rearrange("p k t -> p (k t)"), cx_bank[u]).then_inc(cx_hi, 1)

            def hidden(i, e):
                act.wait_ge(ch_done, i + 1)
                need(act, hl_ready, i)
                for k in range(KC):
                    at = slice(k * P, (k + 1) * P)
                    nc.scalar.activation(hf[:, at], ch_bank[:, at], ACT.Relu,
                                         scale=pcol[:, bass.ds(e * KC + (ROW_G1 + k), 1)],
                                         bias=pcol[:, bass.ds(e * KC + (ROW_BE1 + k), 1)]).then_inc(relu_done, 1)
                need(act, m2_done, i)
                act.wait_ge(relu_done, KC * (i + 1))
                hi_part(hTc[:, HI].rearrange("p k t -> p (k t)"), hf).then_inc(hh_ready, 1)

            def weigh_rows(n, u):
                act.wait_ge(slots_in[u], 16 * (n + 1))
                need(act, added[u], 16 * n)
                act.wait_ge(z2_ready, 2 * n + u + 1)
                nc.scalar.activation(y2[u], z2, ACT.Copy,
                                     scale=tile_slots[:, bass.ds(2 * n + u, 1), 1].bitcast(F32)).then_inc(y2_ready, 1)

            def c_tile(n, u, experts, after):
                i = 2 * n + u
                hidden(i, experts[2])
                if not (isinstance(i, int) and i < 2):
                    weigh_rows(n - 1, u)
                if after >= 3:
                    rows_hi(i + 3, 1 - u)

            act.wait_ge(plan_ready, 1)
            for i in range(3):
                rows_hi(i, i % 2)
            tiles_of(act, c_tile)
            for i in (NSLOT - 2, NSLOT - 1):
                weigh_rows(i // 2, i % 2)

        @block.vector
        def _(dve):
            V = nc.vector

            def lo_part(dst, src, hi):
                return V.tensor_tensor(dst, src, hi.bitcast(F32), ALU.subtract)

            V.memset(zeros_r[:, :].bitcast(F32), 0.0)
            V.memset(carry[:, :, :], 0.0)
            V.memset(kblk[:, :, :, :, :].rearrange("p a b m g -> p (a b m g)").bitcast(F32), 0.0).then_inc(kzero, 1)
            dve.wait_ge(ptr_done, 1)
            V.tensor_copy(pcol[:, :], g_bank[0][:, 0:NROWS]).then_inc(pcol_ready, 1)
            for half_k in range(2):
                dve.wait_ge(ctxT_hi, half_k + 1)
                lo_part(ctxT[:, LO, 2 * half_k:2 * half_k + 2, :],
                        t_bank[half_k][:, 0:2 * B * SK].rearrange("p (k n) -> p k n", k=2),
                        ctxT[:, HI, 2 * half_k:2 * half_k + 2, :]).then_inc(ctxT_lo, 1)
            for i, (dst, src) in enumerate(((wk, raw[3]), (wv, raw[4]))):
                dve.wait_ge(w_hi, i + 1)
                lo_part(dst[:, LO], src, dst[:, HI]).then_inc(w_lo, 1)
            dve.wait_ge(pcol_ready, 1)
            for m in range(KC):
                for hl in range(HPG):
                    dve.wait_ge(k_hi, HPG * m + hl + 1)
                    rows = slice(hl * DH, (hl + 1) * DH)
                    keys = slice(hl * SK, (hl + 1) * SK)
                    V.scalar_tensor_tensor(kblk[rows, LO, :, m, keys],
                                           z_bank[m % 2][rows, 0:B * SK].rearrange("p (b s) -> p b s", b=B),
                                           pcol[rows, ROW_BK + m:ROW_BK + m + 1],
                                           kblk[rows, HI, :, m, keys].bitcast(F32),
                                           ALU.add, ALU.subtract).then_inc(k_lo, 1)
            def xr(c, j):
                return ring[:, c % 3, j] if isinstance(c, int) else ring[:, bass.ds(c % 3, 1), j].rearrange(
                    "p r f -> p (r f)")

            def ln1_stats(c):
                need(dve, xn_ready, 4 * c)
                need_alone(dve, x_in, 16 * (c + 1), dve_passed)
                for j in range(TPC):
                    V.bn_stats(st1[:, j, :], xr(c, j)).then_inc(ln1_stat, 1)
                need_alone(dve, ln1_stat, 4 * (c + 1), dve_passed)
                for j in range(TPC):
                    V.bn_aggr(mv1[:, j, :], st1[:, j, :]).then_inc(ln1_aggr, 1)
                dve.wait_ge(ln1_aggr, 4 * (c + 1))
                need(dve, ln1_rstd, c)
                V.tensor_scalar_add(ve1[:, :], mv1[:, :, 1], EPS).then_inc(ln1_eps, 1)

            def ln1_apply(c):
                dve.wait_ge(ln1_rstd, c + 1)
                need(dve, a_t_done, t_group(c - 1) + 4 if not (isinstance(c, int) and c == 0) else 0)
                for j in range(TPC):
                    V.tensor_scalar(xn[:, j, :], xr(c, j), mv1[:, j, 0:1], rs1[:, j:j + 1],
                                    ALU.subtract, ALU.mult).then_inc(xn_ready, 1)

            def x_lo(c, ks=range(KC)):
                for k in ks:
                    dve.wait_ge(xnT_hi, 4 * c + k + 1)
                    lo_part(xnT[:, LO, k, :], t_bank[k % 2], xnT[:, HI, k, :]).then_inc(a_t_read, 1)

            def h_lo(c, m):
                dve.wait_ge(hT_hi, 4 * c + m + 1)
                lo_part(hTr[:, LO, m, :], hT[:, m, :], hTr[:, HI, m, :]).then_inc(hT_lo, 1)

            def carry_at(c, m, n):
                at = c + c // CPB + n
                return carry[:, m, at:at + 1] if isinstance(at, int) else carry[:, m, bass.ds(at, 1)]

            def recurrence(c, m):
                n = 4 * c + m
                dve.wait_ge(z_ready, n + 1)
                dve.wait_ge(h_done, n + 1)
                need(dve, h_ready, n - 1)
                V.scalar_tensor_tensor(zb[:, m % 2, :], h_bank[m % 2], pcol[:, ROW_BH + m:ROW_BH + m + 1],
                                       za[:, m % 2, :], ALU.add, ALU.mult).then_inc(b_ready, 1)
                dve.wait_ge(b_ready, n + 1)
                V.tensor_scalar(za[:, m % 2, :], za[:, m % 2, :], -1.0, 1.0, ALU.mult, ALU.add).then_inc(a_ready, 1)
                dve.wait_ge(a_ready, n + 1)
                need(dve, carry_ready, n - 3)
                V.tensor_tensor_scan(hT[:, m, :], za[:, m % 2, :], zb[:, m % 2, :], carry_at(c, m, 0),
                                     ALU.mult, ALU.add).then_inc(h_ready, 1)
                dve.wait_ge(h_ready, n + 1)
                V.tensor_copy(carry_at(c, m, 1), hT[:, m, CH - 1:CH]).then_inc(carry_ready, 1)

            def split_piece_lo(c, m):
                dve.wait_ge(split_hi, 4 * c + m + 1)
                lo_part(w_stage[:, LO], w_raw[:, m % 2], w_stage[:, HI]).then_inc(split_lo, 1)

            def x1_rows(c, j):
                g = tg_group(c) + j
                dve.wait_ge(a_t_done, g + 1)
                V.tensor_tensor(xr(c, j), t_bank[j % 2], xr(c, j), ALU.add).then_inc(a_t_read, 1)
                need_alone(dve, a_t_read, g + 1, dve_passed)
                V.bn_stats(st2[:, j, :], xr(c, j)).then_inc(ln2_stat, 1)

            def ln2_means(c):
                need_alone(dve, ln2_stat, 4 * (c + 1), dve_passed)
                for j in range(TPC):
                    V.bn_aggr(mv2[:, j, :], st2[:, j, :]).then_inc(ln2_aggr, 1)
                dve.wait_ge(ln2_aggr, 4 * (c + 1))
                t = bass.ds(4 * c, 4)
                V.tensor_copy(mean2[:, t], mv2[:, :, 0])
                V.tensor_scalar_add(ve2[:, t], mv2[:, :, 1], EPS).then_inc(ln2_eps, 1)

            def gated(c, m):
                dve.wait_ge(gate_ready, 4 * c + m + 1)
                V.tensor_tensor(ghT[:, m, :], gate[:, m % 2, :], hT[:, m, :], ALU.mult).then_inc(gh_ready, 1)

            def a_chunk(c, first=False, ahead=2):
                for m in range(KC):
                    if m:
                        h_lo(c, m - 1)
                    recurrence(c, m)
                    if m == 1:
                        split_piece_lo(c, 0)
                    if m < 2 and not first:
                        x1_rows(c - 1, 2 * m)
                        x1_rows(c - 1, 2 * m + 1)
                    if m == 2 and not first:
                        ln2_means(c - 1)
                h_lo(c, KC - 1)
                split_piece_lo(c, 1)
                if ahead >= 1:
                    x_lo(c + 1, (0, 1))
                gated(c, 0)
                gated(c, 1)
                if ahead >= 1:
                    x_lo(c + 1, (2, 3))
                for m in (2, 3):
                    gated(c, m)
                    if m == 2 or ahead:
                        split_piece_lo(c, m)
                    if ahead >= 2 and m == 2:
                        ln1_stats(c + 2)
                if ahead >= 2:
                    ln1_apply(c + 2)

            dve.wait_ge(consts_done, 1)
            V.memset(tab0[:, :, 1], 0)
            V.tensor_copy(tok[:, :], tok_i[:, :]).then_inc(tok_ready, 1)
            V.memset(counts[:, 0, :], 0.0)
            V.tensor_scalar(tab0[:, :, 0], tab0[:, :, 0], P - 1, T, ALU.bitwise_and,
                            ALU.bitwise_or).then_inc(prefill_ready, 1)
            ln1_stats(0)
            dve.wait_ge(bv_in, 16)
            for b in range(B):
                dve.wait_ge(v_done, b + 1)
                V.tensor_tensor(v_rows[0:SK, b, :], h_bank[b][0:SK, :], bv_rows[0:SK], ALU.add).then_inc(v_ready, 1)
            for b in range(B):
                dve.wait_ge(v_hi, b + 1)
                lo_part(v_r[0:SK, b, LO, :], v_rows[0:SK, b, :], v_r[0:SK, b, HI, :]).then_inc(v_lo, 1)

            def w_low(n, dst, src):
                dve.wait_ge(w_hi, n)
                lo_part(dst[:, LO], src, dst[:, HI]).then_inc(w_lo, 1)

            w_low(3, wz, raw[0])
            dve.wait_ge(w_lo, 3)
            ln1_apply(0)
            w_low(4, wh, raw[1])
            x_lo(0)
            w_low(5, wg, raw[2])
            dve.wait_ge(w_lo, 5)
            dve.wait_ge(vb_out, 16 * 2 * B * HPG)
            for i, (dst, src) in enumerate(((wq, raw[3]), (wo, raw[4]))):
                dve.wait_ge(w_hi, i + 6)
                lo_part(dst[:, LO], src, dst[:, HI]).then_inc(w_lo, 1)
            ln1_stats(1)
            ln1_apply(1)
            a_chunk(0, first=True)
            with dve.Fori(1, NCH - 2) as c:
                a_chunk(c)
            a_chunk(NCH - 2, ahead=1)
            a_chunk(NCH - 1, ahead=0)

            def x1_rows_n(c):
                dve.wait_ge(x1_in, 16 * (c + 1))
                dve.wait_ge(ln2_rstd, c + 1)
                if not (isinstance(c, int) and c == 0):
                    dve.wait_ge(b_t_done, t_num(c - 2, "x3") + 1)
                for j in range(TPC):
                    t = 4 * c + j
                    V.tensor_scalar(x1n[:, j, :], slot3(c)[:, j, :], mean2[:, bass.ds(t, 1)], rs2[:, bass.ds(t, 1)],
                                    ALU.subtract, ALU.mult).then_inc(x1n_ready, 1)

            def x1_lo(c, ks):
                for k in ks:
                    dve.wait_ge(x1T_hi, 4 * c + k + 1)
                    lo_part(x1T[:, LO, k, :], tb(c - 1, f"x{k}"), x1T[:, HI, k, :]).then_inc(b_t_read, 1)

            def q_lo(c, m):
                dve.wait_ge(qT_hi, 4 * c + m + 1)
                V.scalar_tensor_tensor(qT[:, LO, m, :], mb(c - 1, f"q{m}"), pcol[:, ROW_BQ + m:ROW_BQ + m + 1],
                                       qT[:, HI, m, :].bitcast(F32), ALU.add, ALU.subtract).then_inc(mm_read, 1)

            def max_scores(c, m, i):
                n = 4 * c + m
                pair, heads = slice(2 * i, 2 * i + 2), slice(2 * HPG * i, 2 * HPG * (i + 1))
                dve.wait_ge(s_done, 2 * n + i + 1)
                V.tensor_reduce(smax[:, heads].rearrange("p (j h) -> p j h", j=2),
                                s_banks[:, pair, :].rearrange("p j (h s) -> p j h s", h=HPG), AX.X,
                                ALU.max).then_inc(smax_ready, 1)
                dve.wait_ge(smax_ready, 2 * n + i + 1)
                need(dve, s_read, TPC * HPG * (n - 1))
                V.tensor_scalar(nmax[:, m % 2, heads], smax[:, heads], -float(DH) ** -0.5, None,
                                ALU.mult).then_inc(shift_ready, 1)

            def invert_sums(c, m):
                n = 4 * c + m
                dve.wait_ge(s_read, TPC * HPG * (n + 1))
                need(dve, p_ready, n - 1)
                V.reciprocal(srec[:, m % 2, :], ssum[:, m % 2, :]).then_inc(p_rec, 1)

            def pT_lo_part(c, m, parts):
                for u in parts:
                    n = min(UK, GK - u * UK)
                    dve.wait_ge(pT_hi, 12 * c + U * m + u + 1)
                    lo_part(pT[0:n, LO, u, :], tb(c, f"p{m}{u}")[0:n], pT[0:n, HI, u, :]).then_inc(b_t_read, 1)

            def out_lo(c, m):
                dve.wait_ge(outT_hi, 4 * c + m + 1)
                lo_part(outT[:, LO, m, :], mb(c, f"v{m}"), outT[:, HI, m, :]).then_inc(mm_read, 1)

            def x2_rows(c, at, j):
                t = 4 * c + j
                dve.wait_ge(mm_done, mm_num(at, f"o{j}") + 1)
                dve.wait_ge(x1b_ready, t + 1)
                V.tensor_tensor(slot3(c)[:, j, :], mb(at, f"o{j}"), slot3(c)[:, j, :], ALU.add).then_inc(mm_read, 1)
                need_alone(dve, mm_read, mm_num(at, f"o{j}") + 1, dve_passed)
                V.bn_stats(st3[:, j, :], slot3(c)[:, j, :]).then_inc(ln3_stat, 1)

            def ln3_pair(c, i):
                need_alone(dve, ln3_stat, 4 * c + 2 * i + 2, dve_passed)
                need_alone(dve, xf_ready, 4 * (c - 1) + 2 * i + 2, dve_passed)
                for j in (2 * i, 2 * i + 1):
                    V.bn_aggr(mv3[:, j, :], st3[:, j, :]).then_inc(ln3_aggr, 1)
                dve.wait_ge(ln3_aggr, 4 * c + 2 * i + 2)
                V.tensor_scalar_add(ve3[:, 2 * i:2 * i + 2], mv3[:, 2 * i:2 * i + 2, 1], EPS).then_inc(ln3_eps, 1)

            def ln3_apply(c, at, j):
                dve.wait_ge(ln3_rstd, 2 * c + j // 2 + 1)
                need(dve, xf_out[j], 16 * c)
                need(dve, base_ready, 4 * (c - 1) + j + 1)
                if not (isinstance(at, int) and at == 1):
                    dve.wait_ge(b_t_done, t_num(at - 1, f"xf{j}") + 1)
                V.tensor_scalar(xf[:, j, :], slot3(c)[:, j, :], mv3[:, j, 0:1], rs3[:, j:j + 1],
                                ALU.subtract, ALU.mult).then_inc(xf_ready, 1)

            def xf_features(c, at, j):
                dve.wait_ge(b_t_done, t_num(at, f"xf{j}") + 1)
                V.tensor_copy(xfT[:, j].rearrange("p k t -> p (k t)"), tb(at, f"xf{j}")).then_inc(b_t_read, 1)

            def gate_bias(at):
                dve.wait_ge(mm_done, mm_num(at, "g") + 1)
                V.tensor_tensor(gs[:, :, :], mb(at, "g")[:, 0:TPC * NE].rearrange("p (j e) -> p j e", j=TPC),
                                gate_b[:, :].unsqueeze(1).to_broadcast([P, TPC, NE]), ALU.add).then_inc(mm_read, 1)

            class Steps:

                def __init__(self, c, n=0):
                    self.front, self.n = NROUTE * c, n

                def __call__(self, instruction):
                    self.n += 1
                    instruction.then_inc(route, 1)
                    dve.wait_ge(route, self.front + self.n)

            def choose(c, at):
                step = Steps(c)
                dve.wait_ge(mm_read, mm_num(at, "g") + 1)
                other = gs[:, :, :].unsqueeze(2).to_broadcast([P, TPC, NE, NE])
                own = gs[:, :, :].unsqueeze(3).to_broadcast([P, TPC, NE, NE])
                step(V.tensor_tensor(gcmp[:, 0], other, own, ALU.is_gt))
                step(V.tensor_tensor(gcmp[:, 1], other, own, ALU.is_equal))
                step(V.tensor_tensor(gcmp[:, 1], gcmp[:, 1], tie[:, :, :].unsqueeze(1).to_broadcast([P, TPC, NE, NE]),
                                     ALU.mult))
                step(V.tensor_tensor(gcmp[:, 0], gcmp[:, 0], gcmp[:, 1], ALU.add))
                step(V.tensor_reduce(rank[:, :, :], gcmp[:, 0], AX.X, ALU.add))
                step(V.tensor_scalar(sel[:, :, :], rank[:, :, :], 2.0, None, ALU.is_lt))
                assert step.n == ROUTE_CHOSEN

            def count(c):
                step = Steps(c, ROUTE_CHOSEN)
                for j in range(TPC):
                    step(V.tensor_tensor(counts[:, j + 1, :], counts[:, j, :], sel[:, j, :], ALU.add))
                assert step.n == ROUTE_COUNTED
                step(V.tensor_reduce(gmax[:, :], gs[:, :, :], AX.X, ALU.max))
                step(V.tensor_tensor(gexp[:, 0], gs[:, :, :], gmax[:, :].unsqueeze(2).to_broadcast([P, TPC, NE]),
                                     ALU.subtract))
                assert step.n == ROUTE_SHIFTED

            def read_positions(at, name="r", totals=False):
                dve.wait_ge(mm_done, mm_num(at, name) + 1)
                if totals:
                    V.tensor_copy(total[:, :], mb(at, name)[:, TPC * NE:(TPC + 1) * NE])
                V.tensor_tensor(pos[:, :, :], mb(at, name)[:, 0:TPC * NE].rearrange("p (j e) -> p j e", j=TPC),
                                region0[:, :].unsqueeze(1).to_broadcast([P, TPC, NE]), ALU.add).then_inc(mm_read, 1)

            def weigh(c):
                step = Steps(c, ROUTE_SHIFTED)
                for k in range(2):
                    step(V.tensor_scalar(is_k[:, k], rank[:, :, :], float(k), None, ALU.is_equal))
                dve.wait_ge(route_exp, c + 1)
                step(V.tensor_tensor(gexp[:, 1], gexp[:, 0], sel[:, :, :], ALU.mult))
                step(V.tensor_reduce(grec[:, 0, :], gexp[:, 1], AX.X, ALU.add))
                step(V.reciprocal(grec[:, 1, :], grec[:, 0, :]))
                step(V.tensor_tensor(gexp[:, 1], gexp[:, 1], grec[:, 1, :].unsqueeze(2).to_broadcast([P, TPC, NE]),
                                     ALU.mult))
                for k in range(2):
                    step(V.tensor_tensor(kth[:, k], is_k[:, k], gexp[:, 1], ALU.mult))
                step(V.tensor_reduce(kval[:, 0], kth[:, :, :, :], AX.X, ALU.add))
                assert step.n == ROUTE_WEIGHED

            def slots(c, at, name="r"):
                step = Steps(c, ROUTE_WEIGHED)
                dve.wait_ge(mm_read, mm_num(at, name) + 1)
                for k in range(2):
                    step(V.tensor_tensor(kth[:, k], is_k[:, k], pos[:, :, :], ALU.mult))
                step(V.tensor_reduce(kval[:, 1], kth[:, :, :, :], AX.X, ALU.add))
                need(dve, scattered, 16 * 2 * TPC * c)
                for k in range(2):
                    step(V.tensor_copy(payload[:, :, k, 0], tok[:, :]))
                    step(V.tensor_copy(payload[:, :, k, 1].bitcast(F32), kval[:, 0, k, :]))
                step(V.tensor_copy(slot_ix[:, :, :], kval[:, 1, :, :]))
                step(V.tensor_copy(counts[:, 0, :], counts[:, TPC, :]))
                step(V.tensor_scalar_add(tok[:, :], tok[:, :], float(CH)))
                assert step.n == NROUTE

            class Plan:
                n = 0

                def __call__(self, instruction):
                    self.n += 1
                    instruction.then_inc(plan, 1)
                    dve.wait_ge(plan, self.n)

            plan_step = Plan()

            def expert_tiles(add):
                plan_step(V.tensor_scalar(total_i[:, :], total[:, :], float(add), None, ALU.add))
                plan_step(V.tensor_scalar(total_i[:, :], total_i[:, :], P.bit_length() - 1, None, ALU.arith_shift_right))
                plan_step(V.tensor_copy(tiles[:, :], total_i[:, :]))

            def first_tiles():
                plan_step(V.memset(first[:, 0:1], 0.0))
                for e in range(1, NE):
                    plan_step(V.tensor_tensor(first[:, e:e + 1], first[:, e - 1:e], tiles[:, e - 1:e], ALU.add))

            def plan_tiles(at, count, skipped):
                number, experts, rows = tile_no[:, 0:count], tile_e[:, 0:count], tile_row[:, 0:count]
                first_tiles()
                plan_step(V.tensor_scalar(jump[:, :], tiles[:, :], -float(P), float(REG), ALU.mult, ALU.add))
                plan_step(V.tensor_scalar(rows, number, float(P), None, ALU.mult))
                if skipped is not None:
                    plan_step(V.scalar_tensor_tensor(jump[:, 0:NE - 1], skipped[:, 1:NE], float(P), jump[:, 0:NE - 1],
                                                     ALU.mult, ALU.add))
                    plan_step(V.scalar_tensor_tensor(jump[:, 0:NE - 1], skipped[:, 0:NE - 1], -float(P),
                                                     jump[:, 0:NE - 1], ALU.mult, ALU.add))
                    plan_step(V.tensor_scalar(total[:, 0:1], skipped[:, 0:1], float(P), None, ALU.mult))
                    plan_step(V.tensor_scalar(rows, rows, total[:, 0:1], None, ALU.add))
                for e in range(1, NE):
                    plan_step(V.tensor_scalar(tile_ge[:, e - 1, 0:count], number, first[:, e:e + 1], None, ALU.is_ge))
                    plan_step(V.scalar_tensor_tensor(rows, tile_ge[:, e - 1, 0:count], jump[:, e - 1:e], rows,
                                                     ALU.mult, ALU.add))
                plan_step(V.tensor_tensor(experts, tile_ge[:, 0, 0:count], tile_ge[:, 1, 0:count], ALU.add))
                plan_step(V.tensor_tensor(experts, experts, tile_ge[:, 2, 0:count], ALU.add))
                plan_step(V.tensor_copy(plan_e[:, at:at + count], experts))
                plan_step(V.tensor_copy(plan_row[:, at:at + count], rows))

            def plan_early():
                plan_step(V.tensor_copy(tile_no[:, :], tile_int[:, :]))
                expert_tiles(0)
                plan_tiles(0, EARLY, None)
                plan_step(V.tensor_scalar(taken[:, :], first[:, :], -1.0, float(EARLY), ALU.mult, ALU.add))
                plan_step(V.tensor_scalar(taken[:, :], taken[:, :], 0.0, None, ALU.max))
                plan_step(V.tensor_tensor(taken[:, :], taken[:, :], tiles[:, :], ALU.min))
                dve.sem_inc(plan_ready, 1)

            def plan_late():
                expert_tiles(P - 1)
                plan_step(V.tensor_tensor(tiles[:, :], tiles[:, :], taken[:, :], ALU.subtract))
                plan_tiles(EARLY, NSLOT - EARLY, taken)

            def pack_plan():
                plan_step(V.memset(plan_e[:, NSLOT:], 0))
                pairs = plan_around[:, 1:(NSLOT + 1) // 2]
                behind = NSLOT - 2
                plan_step(V.tensor_copy(pairs, plan_e[:, 0:behind:2]))
                for k in range(1, 6):
                    plan_step(V.scalar_tensor_tensor(pairs, plan_e[:, k:behind + k:2], float(NE ** k), pairs,
                                                     ALU.mult, ALU.add))
                dve.sem_inc(plan_ready, 1)

            def b_turn(c, back=True, back2=True, ahead=True):
                max_scores(c, 1, 1)
                if ahead:
                    x1_rows_n(c + 1)
                pT_lo_part(c, 0, (0, 1))
                if back2:
                    count(c - 2)
                if back:
                    x2_rows(c - 1, c, 0)
                pT_lo_part(c, 0, (2,))
                if ahead:
                    x1_lo(c + 1, (0,))
                if back:
                    x2_rows(c - 1, c, 1)
                if ahead:
                    x1_lo(c + 1, (1, 2))
                if back:
                    ln3_pair(c - 1, 0)
                if back2:
                    read_positions(c, totals=not ahead)
                invert_sums(c, 1)
                if back:
                    x2_rows(c - 1, c, 2)
                if ahead:
                    x1_lo(c + 1, (3,))
                max_scores(c, 2, 0)
                if back:
                    ln3_apply(c - 1, c, 0)
                    ln3_apply(c - 1, c, 1)

                max_scores(c, 2, 1)
                pT_lo_part(c, 1, (0, 1))
                out_lo(c, 0)
                if back:
                    x2_rows(c - 1, c, 3)
                pT_lo_part(c, 1, (2,))
                if back:
                    xf_features(c - 1, c, 0)
                    ln3_pair(c - 1, 1)
                if ahead:
                    q_lo(c + 1, 0)
                invert_sums(c, 2)
                if back:
                    xf_features(c - 1, c, 1)
                max_scores(c, 3, 0)
                out_lo(c, 1)

                max_scores(c, 3, 1)
                pT_lo_part(c, 2, (0, 1))
                if back:
                    ln3_apply(c - 1, c, 2)
                    ln3_apply(c - 1, c, 3)
                if ahead:
                    q_lo(c + 1, 1)
                pT_lo_part(c, 2, (2,))
                if back:
                    xf_features(c - 1, c, 2)
                if not ahead:
                    plan_early()
                if back2:
                    weigh(c - 2)
                if ahead:
                    q_lo(c + 1, 2)
                invert_sums(c, 3)
                if back:
                    xf_features(c - 1, c, 3)
                if ahead:
                    max_scores(c + 1, 0, 0)
                out_lo(c, 2)

                if ahead:
                    max_scores(c + 1, 0, 1)
                pT_lo_part(c, 3, (0, 1))
                if back2:
                    slots(c - 2, c)
                if ahead:
                    q_lo(c + 1, 3)
                pT_lo_part(c, 3, (2,))
                if ahead:
                    invert_sums(c + 1, 0)
                if back:
                    gate_bias(c)
                    choose(c - 1, c)
                if ahead:
                    max_scores(c + 1, 1, 0)
                out_lo(c, 3)

            x1_rows_n(0)
            for j in range(TPC):
                x1_rows(NCH - 1, j)
            ln2_means(NCH - 1)
            split_piece_lo(NCH - 1, 3)
            dve.wait_ge(g_done, KC * NCH)
            V.memset(mask_r[:, 1:CPB, :].rearrange("p s g -> p (s g)").bitcast(F32), 0.0).then_inc(kzero, 1)
            dve.wait_ge(tok_ready, 1)
            x1_lo(0, range(KC))
            for m in range(KC):
                q_lo(0, m)
            max_scores(0, 0, 0)
            max_scores(0, 0, 1)
            max_scores(0, 1, 0)
            invert_sums(0, 0)
            dve.wait_ge(gw_in, 32)
            b_turn(0, back=False, back2=False)
            b_turn(1, back2=False)
            b_turn(2)
            with dve.Fori(3, NCH - 1) as c:
                b_turn(c)
            b_turn(NCH - 1, ahead=False)
            last, tail = NCH - 1, NCH
            count(last - 1)
            for j in range(TPC):
                x2_rows(last, tail, j)
                if j % 2:
                    ln3_pair(last, j // 2)
                if j == 1:
                    read_positions(tail)
            weigh(last - 1)
            for j in range(TPC):
                ln3_apply(last, tail, j)
            slots(last - 1, tail)
            for j in range(TPC):
                xf_features(last, tail, j)
            gate_bias(tail)
            choose(last, tail)
            count(last)
            read_positions(tail, "t", totals=True)
            weigh(last)
            slots(last, tail, "t")

            def row_of(rows, e):
                return rows[:, bass.ds(e, 1), :].rearrange("p e f -> p (e f)")

            def rows_lo(i, u):
                dve.wait_ge(cx_hi, i + 1)
                lo_part(xT[:, LO].rearrange("p k t -> p (k t)"), cx_bank[u],
                        xT[:, HI].rearrange("p k t -> p (k t)")).then_inc(cx_lo, 1)

            def statistics(i, which, src, ready, stat):
                need_alone(dve, ready, i + 1, dve_passed)
                V.bn_stats(c_st[:, which, :], src).then_inc(stat, 1)

            def moments(i, which, stat, aggr):
                need_alone(dve, stat, i + 1, dve_passed)
                V.bn_aggr(c_mv[:, which, :], c_st[:, which, :]).then_inc(aggr, 1)

            def add_eps(i, which, aggr, eps):
                dve.wait_ge(aggr, i + 1)
                V.tensor_scalar_add(c_ve[:, which:which + 1], c_mv[:, which, 1:2], EPS).then_inc(eps, 1)

            def hidden_rows(i, u, e):
                need(dve, n1_ready, i)
                dve.wait_ge(m1_done, i + 1)
                V.tensor_tensor(u1, m1_bank[u], row_of(b1_rows, e), ALU.add).then_inc(u1_ready, 1)

            def hidden_norm(i, u):
                dve.wait_ge(c1_rstd, i + 1)
                need(dve, ch_done, i - 1)
                V.tensor_scalar(n1[u], u1, c_mv[:, 0, 0:1], c_rs[:, 0:1], ALU.subtract, ALU.mult).then_inc(n1_ready, 1)

            def out_rows(n, u, e):
                dve.wait_ge(m2_done, 2 * n + u + 1)
                V.tensor_tensor(u2[u], m2_bank[u], row_of(b2_rows, e), ALU.add).then_inc(u2_ready, 1)

            def out_scale(n, u, e):
                need(dve, z2_ready, 2 * n + u)
                V.scalar_tensor_tensor(v2, u2[u], c_mv[:, 1, 0:1], row_of(g2_rows, e), ALU.subtract,
                                       ALU.mult).then_inc(v2_ready, 1)

            def out_norm(i, e):
                dve.wait_ge(c2_rstd, i + 1)
                dve.wait_ge(v2_ready, i + 1)
                need(dve, y2_ready, i)
                V.scalar_tensor_tensor(z2, v2, c_rs[:, 1:2], row_of(be2_rows, e), ALU.mult,
                                       ALU.add).then_inc(z2_ready, 1)

            def c_tile(n, u, experts, after):
                i = 2 * n + u
                last = (n if u else n - 1), 1 - u
                early = i if isinstance(i, int) else 2
                if after >= 1:
                    statistics(i + 1, 0, u1, u1_ready, c1_stat)
                    moments(i + 1, 0, c1_stat, c1_aggr)
                if early >= 1:
                    out_rows(*last, experts[1])
                if after >= 1:
                    add_eps(i + 1, 0, c1_aggr, c1_eps)
                if early >= 2:
                    out_norm(i - 2, experts[0])
                if early >= 1:
                    statistics(i - 1, 1, u2[1 - u], u2_ready, c2_stat)
                if after >= 1:
                    hidden_norm(i + 1, 1 - u)
                if early >= 1:
                    moments(i - 1, 1, c2_stat, c2_aggr)
                if after >= 2:
                    hidden_rows(i + 2, u, experts[4])
                if early >= 1:
                    add_eps(i - 1, 1, c2_aggr, c2_eps)
                if after >= 3:
                    rows_lo(i + 3, 1 - u)
                if early >= 1:
                    out_scale(*last, experts[1])

            dve.wait_ge(moe_rows_in, 16 * 3)
            for j in range(TPC):
                dve.wait_ge(xf_out[j], 16 * NCH)
            dve.wait_ge(base_ready, NT)
            rows_lo(0, 0)
            plan_late()
            hidden_rows(0, 0, expert_at(dve, 0))
            rows_lo(1, 1)
            statistics(0, 0, u1, u1_ready, c1_stat)
            moments(0, 0, c1_stat, c1_aggr)
            add_eps(0, 0, c1_aggr, c1_eps)
            hidden_norm(0, 0)
            pack_plan()
            hidden_rows(1, 1, expert_at(dve, 1))
            rows_lo(2, 0)
            dve.wait_ge(be2_in, 16)
            tiles_of(dve, c_tile)
            i = NSLOT - 1
            e = expert_at(dve, i)
            out_rows(i // 2, i % 2, e)
            out_norm(i - 1, expert_at(dve, i - 1))
            statistics(i, 1, u2[i % 2], u2_ready, c2_stat)
            moments(i, 1, c2_stat, c2_aggr)
            add_eps(i, 1, c2_aggr, c2_eps)
            out_scale(i // 2, i % 2, e)
            out_norm(i, e)

        @block.gpsimd
        def _(pool):
            G = nc.gpsimd
            G.memset(half[:, :], -0.5)
            G.memset(causal[:, :], 0.0)
            G.memset(before[:, :], 1.0)
            G.memset(ones[:, :], 1.0)
            G.memset(tie[:, :, :], 0.0)
            for e in range(NE):
                G.memset(region0[:, e:e + 1], float(e * REG))
            G.iota(tok_i[:, :], pattern=[[P, TPC]], base=0, channel_multiplier=1)
            G.iota(tile_int[:, :], pattern=[[1, EARLY]], base=0, channel_multiplier=0)
            G.iota(tab0[:, :, 0], pattern=[[1, TABW]], base=0, channel_multiplier=TABW)
            G.memset(ident[:, :], 0.0).then_inc(pool_step, 1)
            pool.wait_ge(pool_step, 1)
            G.affine_select(out=ident[:, :], in_=ident[:, :], compare_op=ALU.not_equal, fill=1.0, base=0,
                            pattern=[[-1, P]], channel_multiplier=1).then_inc(const_ready, 1)
            for e in range(1, NE):
                G.memset(tie[:, e, 0:e], 1.0)
            G.affine_select(out=causal[:, :], in_=causal[:, :], compare_op=ALU.is_ge, fill=NEG, base=0,
                            pattern=[[-1, SK]], channel_multiplier=1)
            G.affine_select(out=before[:, :], in_=before[:, :], compare_op=ALU.is_gt, fill=0.0, base=0,
                            pattern=[[1, P]], channel_multiplier=-1).then_inc(consts_done, 1)

            def ln1_pow(c):
                pool.wait_ge(ln1_eps, c + 1)
                need(pool, xn_ready, 4 * c)
                G.tensor_tensor(rs1[:, :], ve1[:, :], half[:, 0:TPC], ALU.pow).then_inc(ln1_rstd, 1)

            def ln2_pow(c):
                t = bass.ds(4 * c, 4)
                pool.wait_ge(ln2_eps, c + 1)
                G.tensor_tensor(rs2[:, t], ve2[:, t], half[:, 0:TPC], ALU.pow).then_inc(ln2_rstd, 1)

            for c in range(3):
                ln1_pow(c)
            with pool.Fori(1, NCH - 2) as c:
                ln2_pow(c - 1)
                ln1_pow(c + 2)
            ln2_pow(NCH - 3)
            ln2_pow(NCH - 2)
            ln2_pow(NCH - 1)

            def add_bo(c):
                for j in range(TPC):
                    need_alone(pool, x1n_ready, 4 * c + j + 1, pool_passed)
                    G.tensor_tensor(slot3(c)[:, j, :], slot3(c)[:, j, :], bo_rows, ALU.add).then_inc(x1b_ready, 1)

            def normalise(c, m):
                pool.wait_ge(p_rec, 4 * c + m + 1)
                p3 = pb[m % 2].rearrange("p j (h s) -> p (j h) s", h=HPG)
                G.tensor_tensor(p3, p3, srec[:, m % 2, :].unsqueeze(2).to_broadcast([P, TPC * HPG, SK]),
                                ALU.mult).then_inc(p_ready, 1)

            def ln3_pow(c, i):
                pool.wait_ge(ln3_eps, 2 * c + i + 1)
                need(pool, xf_ready, 4 * (c - 1) + 2 * i + 2)
                pair = slice(2 * i, 2 * i + 2)
                G.tensor_tensor(rs3[:, pair], ve3[:, pair], half[:, 0:2], ALU.pow).then_inc(ln3_rstd, 1)

            def base_row(c, j):
                t = 4 * c + j
                need(pool, base_out[j % 2], 16 * (2 * c + j // 2))
                need_alone(pool, xf_ready, t + 1, pool_passed)
                G.tensor_tensor(base[:, j % 2, :], slot3(c)[:, j, :], xf[:, j, :], ALU.add).then_inc(base_ready, 1)

            def scatter(c, j):
                need_alone(pool, route, NROUTE * (c + 1), pool_passed)
                for k in range(2):
                    G.indirect_dma_start(slots_d, bass.IndirectOffsetOnAxis(slot_ix[:, k, j:j + 1], 0),
                                         payload[:, j, k, :], None).then_inc(scattered, 16)

            def b_turn(c, back=True, back3=True, ahead=True):
                normalise(c, 0)
                if back3:
                    scatter(c - 3, 0)
                    scatter(c - 3, 1)
                if back:
                    ln3_pow(c - 1, 0)
                normalise(c, 1)
                if back3:
                    scatter(c - 3, 2)
                    scatter(c - 3, 3)
                if back:
                    ln3_pow(c - 1, 1)
                    base_row(c - 1, 0)
                    base_row(c - 1, 1)
                normalise(c, 2)
                if ahead:
                    add_bo(c + 1)
                if back:
                    base_row(c - 1, 2)
                    base_row(c - 1, 3)
                normalise(c, 3)

            pool.wait_ge(bo_in, 16)
            add_bo(0)
            pool.wait_ge(prefill_out, 16)
            b_turn(0, back=False, back3=False)
            b_turn(1, back3=False)
            b_turn(2, back3=False)
            with pool.Fori(3, NCH - 1) as c:
                b_turn(c)
            b_turn(NCH - 1, ahead=False)
            for j in range(TPC):
                scatter(NCH - 3, j)
            for i in range(2):
                ln3_pow(NCH - 1, i)

            def gather(n, u):
                i = 2 * n + u
                need(pool, cx_done, i - 1)
                need(pool, gathered[u], 16 * n)
                need_alone(pool, slots_in[u], 16 * (n + 1), pool_passed)
                G.tensor_copy(gix[u][:, :], tile_slots[:, bass.ds(i, 1), 0]).then_inc(gix_ready, 1)
                need_alone(pool, gix_ready, i + 1, pool_passed)
                G.indirect_dma_start(xg[u], None, xf_d, bass.IndirectOffsetOnAxis(gix[u][:, 0:1], 0)).then_inc(
                    gathered[u], 16)

            pool.wait_ge(b_t_done, t_num(NCH - 1, f"p3{U - 1}") + 1)
            pool.wait_ge(x1b_ready, NT)
            for j in range(TPC):
                scatter(NCH - 2, j)
            for j in range(TPC):
                pool.wait_ge(xf_out[j], 16 * NCH)
            gather(0, 0)
            gather(0, 1)
            for j in range(TPC):
                base_row(NCH - 1, j)

            def add_out(n, u):
                i = 2 * n + u
                need(pool, added[u], 16 * n)
                need_alone(pool, slots_in[u], 16 * (n + 1), pool_passed)
                G.tensor_copy(six[u][:, :], tile_slots[:, bass.ds(i, 1), 0]).then_inc(six_ready, 1)
                need(pool, added[1 - u], 16 * (n + u))
                need(pool, y2_ready, i + 1)
                need_alone(pool, six_ready, i + 1, pool_passed)
                G.indirect_dma_start(out, bass.IndirectOffsetOnAxis(six[u][:, 0:1], 0), y2[u], None,
                                     compute_op=ALU.add).then_inc(added[u], 16)

            def rstd(i, which, eps, done):
                pool.wait_ge(eps, i + 1)
                G.tensor_tensor(c_rs[:, which:which + 1], c_ve[:, which:which + 1], half[:, 0:1],
                                ALU.pow).then_inc(done, 1)

            def hidden_lo(i):
                pool.wait_ge(hh_ready, i + 1)
                G.tensor_tensor(hTc[:, LO].rearrange("p k t -> p (k t)"), hf,
                                hTc[:, HI].rearrange("p k t -> p (k t)").bitcast(F32), ALU.subtract).then_inc(hl_ready, 1)

            def c_tile(n, u, experts, after):
                i = 2 * n + u
                early = i if isinstance(i, int) else 2
                if early == 0:
                    hidden_lo(i)
                if after >= 1:
                    rstd(i + 1, 0, c1_eps, c1_rstd)
                if early:
                    hidden_lo(i)
                if early >= 2:
                    add_out(n - 1, u)
                if after >= 5:
                    gather(n + 2 + u, 1 - u)
                if early >= 1:
                    rstd(i - 1, 1, c2_eps, c2_rstd)

            scatter(NCH - 1, 0)
            rstd(0, 0, c1_eps, c1_rstd)
            gather(1, 0)
            scatter(NCH - 1, 1)
            gather(1, 1)
            scatter(NCH - 1, 2)
            gather(2, 0)
            scatter(NCH - 1, 3)
            for i in range(2):
                pool.wait_ge(base_out[i], 16 * NT // 2)
            pool.wait_ge(zero_out, 160)
            tiles_of(pool, c_tile)
            add_out((NSLOT - 2) // 2, (NSLOT - 2) % 2)
            rstd(NSLOT - 1, 1, c2_eps, c2_rstd)
            add_out((NSLOT - 1) // 2, (NSLOT - 1) % 2)
            pool.wait_ge(added[0], 16 * ((NSLOT + 1) // 2))
            pool.wait_ge(added[1], 16 * (NSLOT // 2))



def kernel(**inputs):
    import concourse.bacc as bacc
    from concourse.bass_utils import run_bass_kernel_spmd

    nc = bacc.Bacc("TRN2", target_bir_lowering=False, num_devices=1)
    arrays = {f"in_{name}": np.ascontiguousarray(array) for name, array in inputs.items()}
    io = {name: nc.dram_tensor(f"in_{name}", arrays[f"in_{name}"].shape, mybir.dt.from_np(arrays[f"in_{name}"].dtype),
                               kind="ExternalInput").ap() for name in inputs}
    out = nc.dram_tensor("out", [T + P, D], F32, kind="ExternalOutput").ap()
    decoder_layer(nc, io, out)
    result = run_bass_kernel_spmd(nc, [arrays], core_ids=[0]).results[0]["out"]
    return result[:T].reshape(B, S, D)
```
